# Optimizing a Trainium2 kernel written in Bass

```python
import numpy as np
import jax
import jax.numpy as jnp

def _softmax(x, axis=-1):
    return jax.nn.softmax(x, axis=axis)

def _gelu(x):
    return jax.nn.gelu(x, approximate=True)

def _silu(x):
    return jax.nn.silu(x)

def _sigmoid(x):
    return jax.nn.sigmoid(x)

def _layernorm(x, axis=-1, eps=1e-05):
    m = jnp.mean(x, axis=axis, keepdims=True)
    v = jnp.var(x, axis=axis, keepdims=True)
    return (x - m) / jnp.sqrt(v + eps)

def _scatter_add(tgt, idx, src, axis=0):
    return tgt.at[idx].add(src)

def _segment_sum(src, seg, n):
    return jax.ops.segment_sum(src, seg, n)
kernel_name = 'mk_seq_preln_d1_jaxref_r8_5ffabd'

def setup_inputs(seed: int=0):
    np.random.seed(seed)
    _w = jnp.asarray

    def _L0_attn_setup():
        import jax, jax.numpy as jnp
        import numpy as np
        from functools import partial
        B, S, D, H, DK, DV, DFF = (4, 256, 128, 8, 128, 128, 512)
        EPS = 1e-06

        def rms_norm(x):
            return x * jax.lax.rsqrt(jnp.mean(x * x, axis=-1, keepdims=True) + EPS)

        def l2norm(x):
            return x * jax.lax.rsqrt(jnp.sum(x * x, axis=-1, keepdims=True) + EPS)

        def gated_delta_net(h, Wq, Wk, Wv, Wb, Wa, A_log, dt_bias, Wg, o_norm_w, Wo):
            b, s, _ = h.shape
            q = l2norm(jax.nn.silu(h @ Wq).reshape(b, s, H, DK))
            k = l2norm(jax.nn.silu(h @ Wk).reshape(b, s, H, DK))
            v = jax.nn.silu(h @ Wv).reshape(b, s, H, DV)
            beta = jax.nn.sigmoid(h @ Wb)
            g = -jnp.exp(A_log) * jax.nn.softplus(h @ Wa + dt_bias)
            alpha = jnp.exp(g)
            scale = DK ** (-0.5)
            tm = lambda a: jnp.moveaxis(a, 1, 0)
            qs, ks_, vs, als, bts = (tm(q), tm(k), tm(v), tm(alpha), tm(beta))

            def step(Sst, inp):
                q_t, k_t, v_t, a_t, b_t = inp
                Sst = Sst * a_t[..., None, None]
                kv = jnp.einsum('bhd,bhde->bhe', k_t, Sst)
                delta = (v_t - kv) * b_t[..., None]
                Sst = Sst + jnp.einsum('bhd,bhe->bhde', k_t, delta)
                o_t = jnp.einsum('bhd,bhde->bhe', q_t, Sst) * scale
                return (Sst, o_t)
            S0 = jnp.zeros((b, H, DK, DV), dtype=h.dtype)
            _, o = jax.lax.scan(step, S0, (qs, ks_, vs, als, bts))
            o = jnp.moveaxis(o, 0, 1)
            gate = (h @ Wg).reshape(b, s, H, DV)
            o = rms_norm(o) * o_norm_w * jax.nn.silu(gate)
            return o.reshape(b, s, H * DV) @ Wo
        key = jax.random.key(seed)
        ks = jax.random.split(key, 16)
        w = lambda k, shp: jax.random.normal(k, shp, dtype=jnp.float32) * 0.02
        return {'x': jax.random.normal(ks[0], (B, S, D), dtype=jnp.float32), 'Wq': w(ks[1], (D, H * DK)), 'Wk': w(ks[2], (D, H * DK)), 'Wv': w(ks[3], (D, H * DV)), 'Wb': w(ks[4], (D, H)), 'Wa': w(ks[5], (D, H)), 'A_log': jnp.log(jnp.linspace(1.0, 8.0, H).astype(jnp.float32)), 'dt_bias': jax.random.normal(ks[6], (H,), dtype=jnp.float32) * 0.1, 'Wg': w(ks[7], (D, H * DV)), 'o_norm_w': jnp.ones((DV,), dtype=jnp.float32), 'Wo': w(ks[8], (H * DV, D)), 'W_fc': w(ks[9], (D, DFF)), 'W_proj': w(ks[10], (DFF, D))}
    _L0_attn_in = _L0_attn_setup()

    def _L0_ffn_setup():
        import jax, jax.numpy as jnp
        import numpy as np
        HIDDEN = 128
        NUM_EXPERTS = 8
        BATCH, SEQ = (4, 512)
        key = jax.random.key(seed)
        ks = jax.random.split(key, 6)
        s = 1.0 / np.sqrt(HIDDEN)
        tokens = jax.random.normal(ks[0], (BATCH, SEQ, HIDDEN), dtype=jnp.float32)
        gate_w = jax.random.uniform(ks[1], (NUM_EXPERTS, HIDDEN), jnp.float32, -s, s)
        expert_w = jax.random.uniform(ks[2], (NUM_EXPERTS, HIDDEN, HIDDEN), jnp.float32, -s, s)
        expert_b = jax.random.uniform(ks[3], (NUM_EXPERTS, HIDDEN), jnp.float32, -s, s)
        combine_w = jax.random.uniform(ks[4], (HIDDEN, HIDDEN), jnp.float32, -s, s)
        return {'tokens': tokens, 'gate_w': gate_w, 'expert_w': expert_w, 'expert_b': expert_b, 'combine_w': combine_w}
    _L0_ffn_in = _L0_ffn_setup()
    _d = {'L0_attn_x': _L0_attn_in['x'], 'L0_attn_Wq': _L0_attn_in['Wq'], 'L0_attn_Wk': _L0_attn_in['Wk'], 'L0_attn_Wv': _L0_attn_in['Wv'], 'L0_attn_Wb': _L0_attn_in['Wb'], 'L0_attn_Wa': _L0_attn_in['Wa'], 'L0_attn_A_log': _L0_attn_in['A_log'], 'L0_attn_dt_bias': _L0_attn_in['dt_bias'], 'L0_attn_Wg': _L0_attn_in['Wg'], 'L0_attn_o_norm_w': _L0_attn_in['o_norm_w'], 'L0_attn_Wo': _L0_attn_in['Wo'], 'L0_attn_W_fc': _L0_attn_in['W_fc'], 'L0_attn_W_proj': _L0_attn_in['W_proj'], 'L0_ffn_gate_w': _L0_ffn_in['gate_w'], 'L0_ffn_expert_w': _L0_ffn_in['expert_w'], 'L0_ffn_expert_b': _L0_ffn_in['expert_b'], 'L0_ffn_combine_w': _L0_ffn_in['combine_w']}
    _x0 = _d['L0_attn_x']
    _d['L0_attn_x'] = jax.random.normal(jax.random.fold_in(jax.random.key(seed), 1), (8, 1024, 128), dtype=_x0.dtype)
    del _x0
    return _d

def reference(L0_attn_x, L0_attn_Wq, L0_attn_Wk, L0_attn_Wv, L0_attn_Wb, L0_attn_Wa, L0_attn_A_log, L0_attn_dt_bias, L0_attn_Wg, L0_attn_o_norm_w, L0_attn_Wo, L0_attn_W_fc, L0_attn_W_proj, L0_ffn_gate_w, L0_ffn_expert_w, L0_ffn_expert_b, L0_ffn_combine_w):

    def _L0_attn_ref(x, Wq, Wk, Wv, Wb, Wa, A_log, dt_bias, Wg, o_norm_w, Wo, W_fc, W_proj):
        import jax, jax.numpy as jnp
        import numpy as np
        from functools import partial
        B, S, D, H, DK, DV, DFF = (4, 256, 128, 8, 128, 128, 512)
        EPS = 1e-06

        def rms_norm(x):
            return x * jax.lax.rsqrt(jnp.mean(x * x, axis=-1, keepdims=True) + EPS)

        def l2norm(x):
            return x * jax.lax.rsqrt(jnp.sum(x * x, axis=-1, keepdims=True) + EPS)

        def gated_delta_net(h, Wq, Wk, Wv, Wb, Wa, A_log, dt_bias, Wg, o_norm_w, Wo):
            b, s, _ = h.shape
            q = l2norm(jax.nn.silu(h @ Wq).reshape(b, s, H, DK))
            k = l2norm(jax.nn.silu(h @ Wk).reshape(b, s, H, DK))
            v = jax.nn.silu(h @ Wv).reshape(b, s, H, DV)
            beta = jax.nn.sigmoid(h @ Wb)
            g = -jnp.exp(A_log) * jax.nn.softplus(h @ Wa + dt_bias)
            alpha = jnp.exp(g)
            scale = DK ** (-0.5)
            tm = lambda a: jnp.moveaxis(a, 1, 0)
            qs, ks_, vs, als, bts = (tm(q), tm(k), tm(v), tm(alpha), tm(beta))

            def step(Sst, inp):
                q_t, k_t, v_t, a_t, b_t = inp
                Sst = Sst * a_t[..., None, None]
                kv = jnp.einsum('bhd,bhde->bhe', k_t, Sst)
                delta = (v_t - kv) * b_t[..., None]
                Sst = Sst + jnp.einsum('bhd,bhe->bhde', k_t, delta)
                o_t = jnp.einsum('bhd,bhde->bhe', q_t, Sst) * scale
                return (Sst, o_t)
            S0 = jnp.zeros((b, H, DK, DV), dtype=h.dtype)
            _, o = jax.lax.scan(step, S0, (qs, ks_, vs, als, bts))
            o = jnp.moveaxis(o, 0, 1)
            gate = (h @ Wg).reshape(b, s, H, DV)
            o = rms_norm(o) * o_norm_w * jax.nn.silu(gate)
            return o.reshape(b, s, H * DV) @ Wo
        ln_scale = 1.0
        h = gated_delta_net(ln_scale * rms_norm(x), Wq, Wk, Wv, Wb, Wa, A_log, dt_bias, Wg, o_norm_w, Wo)
        x = x + h
        m = ln_scale * rms_norm(x)
        y = jnp.square(jax.nn.relu(m @ W_fc)) @ W_proj
        return x + y

    def _L0_ffn_ref(tokens, gate_w, expert_w, expert_b, combine_w):
        import jax, jax.numpy as jnp
        import numpy as np
        HIDDEN = 128
        NUM_EXPERTS = 8
        BATCH, SEQ = (4, 512)
        B, S, H = tokens.shape
        logits = jnp.einsum('bsh,eh->bse', tokens, gate_w)
        probs = jax.nn.softmax(logits, axis=-1)
        top2_w, top2_idx = jax.lax.top_k(probs, 2)
        flat = tokens.reshape(B * S, H)
        flat_idx = top2_idx.reshape(B * S, 2)
        flat_w = top2_w.reshape(B * S, 2)
        expert_out = jax.nn.silu(jnp.einsum('nh,edh->ned', flat, expert_w) + expert_b[None, :, :])
        gathered = jnp.take_along_axis(expert_out, flat_idx[:, :, None], axis=1)
        mixed = jnp.sum(gathered * flat_w[:, :, None], axis=1)
        out = jnp.einsum('bsh,dh->bsd', mixed.reshape(B, S, H), combine_w)
        return out
    x = L0_attn_x
    x = x + _L0_attn_ref(_layernorm(x, axis=-1), L0_attn_Wq, L0_attn_Wk, L0_attn_Wv, L0_attn_Wb, L0_attn_Wa, L0_attn_A_log, L0_attn_dt_bias, L0_attn_Wg, L0_attn_o_norm_w, L0_attn_Wo, L0_attn_W_fc, L0_attn_W_proj)
    x = x + _L0_ffn_ref(_layernorm(x, axis=-1), L0_ffn_gate_w, L0_ffn_expert_w, L0_ffn_expert_b, L0_ffn_combine_w)
    return x

_drawn_inputs = setup_inputs


def setup_inputs(seed=0):
    import zlib

    import numpy as np

    out = dict(_drawn_inputs(seed))
    spreads = {'L0_attn_o_norm_w': (1.0, 0.6)}
    factors = {'L0_attn_Wq': 3.973,
     'L0_attn_Wk': 3.956,
     'L0_attn_Wv': 3.945,
     'L0_attn_Wb': 8.0,
     'L0_attn_Wa': 8.0,
     'L0_attn_A_log': 8.0,
     'L0_attn_dt_bias': 8.0,
     'L0_attn_Wg': 3.957,
     'L0_attn_Wo': 3.923,
     'L0_attn_W_fc': 4.303,
     'L0_attn_W_proj': 3.991,
     'L0_ffn_expert_b': 36.903,
     'L0_ffn_gate_w': 2.963,
     'L0_ffn_expert_w': 3.113}
    for name, (base, spread) in spreads.items():
        noise = np.random.default_rng([zlib.crc32(name.encode()), seed]).standard_normal(out[name].shape)
        drawn = base * np.exp(spread * noise) if base else spread * noise
        out[name] = jnp.asarray(drawn.astype(out[name].dtype))
    for name, factor in factors.items():
        out[name] = (out[name] * factor).astype(out[name].dtype)
    return out
```

```python
from contextlib import ExitStack

import concourse.bass as bass
from concourse import mybir

ALU = mybir.AluOpType
ACT = mybir.ActivationFunctionType
AX = mybir.AxisListType
F32 = mybir.dt.float32
F16 = mybir.dt.float16

P = 128
H = 8
HD = H * P
BANK = 512
HH = H // 2
GRP = 4
BLK = 16
ESC = 1024.0
LN_EPS, RMS_EPS = 1e-5, 1e-6

PAIR_USES = [("G", "b"), ("QK", "b"), ("KS", "c"), ("K", "a"), ("D", "c"), ("PD", "c"), ("QS", "c"),
             ("SU", "c"), ("Q", "a"), ("QT", "a"), ("KT", "a"), ("UB", "b"), ("X0", "b"), ("GT", "c"),
             ("T0", "b"), ("U0", "b"), ("X1", "b"), ("V", "a"), ("T1", "b"), ("U1", "b"), ("X2", "b"),
             ("OT", "c"), ("T2", "b"), ("U2", "b"), ("E", "b"), ("C", "b")]
STAGE = dict(PAIR_USES)
PAIR = {name: k % 3 for k, (name, _) in enumerate(PAIR_USES)}


def upto(t, half):
    return 2 * t + half + 1


def wait(eng, sem, value):
    if not isinstance(value, int) or value > 0:
        eng.wait_ge(sem, value)


def delta_moe(nc, x, Wq, Wk, Wv, Wb, Wa, A_log, dt_bias, Wg, o_norm_w, Wo, W_fc, W_proj,
              gate_w, expert_w, expert_b, combine_w, out, dram):
    B, S_LEN, D = x.shape
    T = B * S_LEN // P
    CH = S_LEN // P
    NG = T // GRP
    DFF = W_fc.shape[1]
    NF = DFF // P
    NE = gate_w.shape[0]
    TH = T * H
    NR = TH // P
    x_t = x.rearrange("b s d -> (b s) d")
    out_t = out.rearrange("b s d -> (b s) d")
    y_d, hT_d, xp_d, al_d, ce_d, x1_d, tT_d = (dram[k] for k in ("y", "hT", "xp", "al", "ce", "x1", "tT"))

    with ExitStack() as ctx:
        def sb(name, shape, dt=F32):
            return ctx.enter_context(nc.sbuf_tensor(name, shape, dt))

        sems = {}

        def sem(name):
            if name not in sems:
                sems[name] = nc.alloc_semaphore(name=name)
            return sems[name]

        def end_program():
            nc.clear_and_free_semaphores(list(sems.values()))
            sems.clear()
            nc.all_engine_barrier()

        bank = [ctx.enter_context(nc.psum_tensor(f"bank{i}", [P, BANK], F32)) for i in range(8)]

        ident = sb("ident", [P, P])
        ident16 = sb("ident16", [P, P], F16)
        negid16 = sb("negid16", [P, P], F16)
        ones = sb("ones", [P, 8])
        mhalf = sb("mhalf", [P, 64])
        keps, krt, kinv = (sb(n, [P, H]) for n in ("keps", "krt", "kinv"))
        mask = [sb(f"mask{i}", [P, P], F16) for i in range(3)]
        maskbd = sb("maskbd", [P, P], F16)
        identp = sb("identp", [P, BLK], F16)
        identp8 = sb("identp8", [P, H, BLK], F16)
        wq, wk, wv, wg, wo = (sb(n, [P, HD]) for n in ("wq", "wk", "wv", "wg", "wo"))
        onw = sb("onw", [P, 1])
        tab = sb("tab", [P, T, 4 * H])
        W_ARENA = 28 * HD
        arena = sb("arena", [P, W_ARENA])

        with ExitStack() as c1:
            bA = c1.enter_context(nc.Block())
            xs = arena[:, 0:T * P].rearrange("p (t d) -> p t d", t=T)
            off = [T * P]

            def cut(n):
                off[0] += n
                assert off[0] <= W_ARENA
                return arena[:, off[0] - n:off[0]]
            hst = cut(2 * BANK).rearrange("p (s k d) -> p s k d", s=2, k=GRP)
            hTs = cut(2 * BANK).rearrange("p (s k d) -> p s k d", s=2, k=GRP)
            st = cut(T * 6).rearrange("p (t s) -> p t s", s=6)
            mean, var, r1, r2, tmp1, tmp2 = (cut(T) for _ in range(6))
            wab = cut(2 * H)
            alog, dtb = cut(H), cut(H)
            z = cut(T * 2 * H).rearrange("p (t k) -> p t k", k=2 * H)
            za, nz, ez, den, sser, s2, pol, al = (cut(TH) for _ in range(8))
            eb = cut(TH)
            arow = cut(TH).rearrange("p (r i) -> p r i", i=P)
            crow = cut(TH).rearrange("p (r i) -> p r i", i=P)
            zrow = cut(P)
            rmask = cut(1)
            v3 = lambda a: a.rearrange("p (t h) -> p t h", h=H)

            @bA.sync
            def _(sp):
                for dst, src in ((wq, Wq), (wk, Wk), (wv, Wv), (wg, Wg)):
                    sp.dma_start(dst[:], src).then_inc(sem("w_in"), 16)
                sp.dma_start(wo[:].rearrange("p (h n) -> p h n", h=H),
                             Wo.rearrange("(h p) n -> p h n", p=P)).then_inc(sem("w_in"), 16)
                sp.wait_ge(sem("y_ready"), 1)
                sp.dma_start(y_d.rearrange("t p d -> p t d"), xs).then_inc(sem("y_out"), 16)
                for g in range(2):
                    sp.wait_ge(sem("hT_ready"), g + 1)
                    sp.dma_start(hT_d[g * GRP:g * GRP + GRP].rearrange("t p i -> p t i"),
                                 hTs[:, g % 2]).then_inc(sem(f"hT_out{g % 2}"), 16)
                with sp.Fori(2, NG - 1, 2) as g0:
                    for k in range(2):
                        sp.wait_ge(sem("hT_ready"), g0 + k + 1)
                        sp.dma_start(hT_d[bass.ds(g0 * GRP + k * GRP, GRP)].rearrange("t p i -> p t i"),
                                     hTs[:, k]).then_inc(sem(f"hT_out{k}"), 16)
                sp.wait_ge(sem("arow_ready"), 1)
                sp.dma_start(al_d.rearrange("(r p) i -> p r i", p=P), arow).then_inc(sem("al_out"), 16)
                sp.wait_ge(sem("crow_ready"), 1)
                with nc.allow_non_contiguous_dma("512 numbers, once"):
                    sp.dma_start(ce_d.rearrange("(r p) -> p r", p=P), crow[:, :, P - 1]).then_inc(sem("ce_out"), 16)
                sp.wait_ge(sem("ce_out"), 16)
                sp.dma_start(al, ce_d.rearrange("(a n) -> a n", a=1).broadcast_to([P, TH])).then_inc(sem("ce_in"), 16)
                for s, v in (("y_out", 16), ("hT_out0", 8 * NG), ("hT_out1", 8 * NG), ("al_out", 16),
                             ("w_in", 80), ("ce_in", 16)):
                    sp.wait_ge(sem(s), v)

            @bA.gpsimd
            def _(pool):
                pool.dma_start(xs, x_t.rearrange("(t p) d -> p t d", p=P)).then_inc(sem("x_in"), 16)
                pool.dma_start(wab[:, 0:H], Wa).then_inc(sem("small_in"), 16)
                pool.dma_start(wab[:, H:2 * H], Wb).then_inc(sem("small_in"), 16)
                pool.dma_start(alog, A_log.rearrange("(a n) -> a n", a=1).broadcast_to([P, H])).then_inc(sem("small_in"), 16)
                pool.dma_start(dtb, dt_bias.rearrange("(a n) -> a n", a=1).broadcast_to([P, H])).then_inc(sem("small_in"), 16)
                pool.dma_start(onw[:], o_norm_w.rearrange("(p a) -> p a", a=1)).then_inc(sem("small_in"), 16)
                n = 0
                g = nc.gpsimd

                def step(ins):
                    nonlocal n
                    n += 1
                    ins.then_inc(sem("const"), 1)
                    pool.wait_ge(sem("const"), n)
                step(g.memset(ident[:], 0.0))
                step(g.memset(ident16[:], 0.0))
                step(g.memset(negid16[:], 0.0))
                step(g.memset(ones[:], 1.0))
                step(g.memset(mhalf[:], -0.5))
                step(g.memset(keps[:], RMS_EPS))
                step(g.memset(krt[:], float(P) ** -0.5))
                step(g.memset(kinv[:], 1.0 / P))
                step(g.memset(maskbd[:], 1.0))
                for m in mask:
                    step(g.memset(m[:], 0.0))
                step(g.memset(zrow, 0.0))
                step(g.memset(rmask, 1.0))
                for m, v in ((ident, 1.0), (ident16, 1.0), (negid16, -1.0)):
                    step(g.affine_select(out=m[:], in_=m[:], compare_op=ALU.not_equal, fill=v, base=0,
                                         pattern=[[-1, P]], channel_multiplier=1))
                for r in range(0, P // H, CH):
                    step(g.memset(rmask[r * H:r * H + H, :], 0.0))
                mb = maskbd[:].rearrange("p (g c) -> p g c", c=BLK)
                step(g.affine_select(out=mb, in_=mb, compare_op=ALU.is_ge, fill=0.0, base=0,
                                     pattern=[[-BLK, P // BLK], [0, BLK]], channel_multiplier=1))
                step(g.affine_select(out=mb, in_=mb, compare_op=ALU.is_ge, fill=0.0, base=BLK - 1,
                                     pattern=[[BLK, P // BLK], [0, BLK]], channel_multiplier=-1))
                for i, m in enumerate(mask):
                    s = BLK << i
                    half = m[:].rearrange("p (g c) -> p g c", c=2 * s)[:, :, 0:s]
                    step(g.memset(half, 1.0))
                for i, m in enumerate(mask):
                    s = BLK << i
                    half = m[:].rearrange("p (g c) -> p g c", c=2 * s)[:, :, 0:s]
                    step(g.affine_select(out=half, in_=half, compare_op=ALU.is_ge, fill=0.0, base=-s,
                                         pattern=[[-2 * s, P // (2 * s)], [0, s]], channel_multiplier=1))
                for i, m in enumerate(mask):
                    s = BLK << i
                    half = m[:].rearrange("p (g c) -> p g c", c=2 * s)[:, :, 0:s]
                    step(g.affine_select(out=half, in_=half, compare_op=ALU.is_ge, fill=0.0, base=2 * s - 1,
                                         pattern=[[2 * s, P // (2 * s)], [0, s]], channel_multiplier=-1))
                g.memset(zrow[0:1, 0:1], 0.0).then_inc(sem("const_all"), 1)
                pool.wait_ge(sem("var_ready"), 1)
                g.tensor_tensor(r1, tmp1, mhalf[:, 0:T], ALU.pow).then_inc(sem("r1_ready"), 1)
                pool.wait_ge(sem("w_ready"), 1)
                g.tensor_tensor(r2, tmp2, mhalf[:, 0:T], ALU.pow).then_inc(sem("r2_ready"), 1)
                pool.wait_ge(sem("small_in"), 80)

            @bA.vector
            def _(dve):
                v = nc.vector
                cnt = [0]

                def link(ins):
                    cnt[0] += 1
                    ins.then_inc(sem("v1"), 1)
                    dve.wait_ge(sem("v1"), cnt[0])
                dve.wait_ge(sem("const_all"), 1)
                with nc.allow_low_precision("zeros and ones"):
                    link(v.tensor_reduce(identp[:], ident16[:].rearrange("p (g c) -> p c g", c=BLK), AX.X, ALU.add))
                link(v.tensor_copy(identp8[:], identp[:].rearrange("p (a c) -> p a c", a=1).broadcast_to([P, H, BLK])))
                dve.wait_ge(sem("x_in"), 16)
                with dve.Fori(0, T) as t:
                    v.bn_stats(st[:, bass.ds(t, 1), :].rearrange("p a s -> p (a s)"),
                               xs[:, bass.ds(t, 1), :].rearrange("p a d -> p (a d)")).then_inc(sem("st"), 1)
                dve.wait_ge(sem("st"), T)
                v.tensor_tensor(mean, st[:, :, 1], st[:, :, 4], ALU.add)
                link(v.tensor_tensor(tmp1, st[:, :, 1], st[:, :, 4], ALU.subtract))
                link(v.tensor_scalar(mean, mean, 0.5, None, ALU.mult))
                link(v.scalar_tensor_tensor(tmp1, tmp1, 0.25, tmp1, ALU.mult, ALU.mult))
                link(v.tensor_tensor(tmp2, st[:, :, 2], st[:, :, 5], ALU.add))
                link(v.scalar_tensor_tensor(var, tmp2, 1.0 / D, tmp1, ALU.mult, ALU.add))
                v.tensor_scalar(tmp1, var, LN_EPS, None, ALU.add).then_inc(sem("var_ready"), 1)
                bc = lambda a: a.rearrange("p (t a) -> p t a", a=1).broadcast_to([P, T, P])
                link(v.tensor_tensor(xs, xs, bc(mean), ALU.subtract))
                dve.wait_ge(sem("r1_ready"), 1)
                link(v.tensor_tensor(tmp2, r1, r1, ALU.mult))
                link(v.tensor_tensor(tmp2, tmp2, var, ALU.mult))
                v.tensor_scalar(tmp2, tmp2, RMS_EPS, None, ALU.add).then_inc(sem("w_ready"), 1)
                v.tensor_tensor(xs, xs, bc(r1), ALU.mult).then_inc(sem("y_ready"), 1)
                dve.wait_ge(sem("w_in"), 80)
                dve.wait_ge(sem("small_in"), 80)
                v.tensor_scalar(wo[:], wo[:], onw[:, 0:1], None, ALU.mult).then_inc(sem("wo_scaled"), 1)
                dve.wait_ge(sem("r2_ready"), 1)
                dve.wait_ge(sem("y_ready"), 1)

                def h_group(g, k):
                    if isinstance(g, int) and g < 2:
                        pass
                    else:
                        dve.wait_ge(sem("hTp"), g - 1)
                    for j in range(GRP):
                        t = g * GRP + j
                        ins = v.tensor_scalar(hst[:, k, j, :], xs[:, bass.ds(t, 1), :].rearrange("p a d -> p (a d)"),
                                              r2[:, bass.ds(t, 1)], None, ALU.mult)
                    ins.then_inc(sem("h_ready"), 1)
                h_group(0, 0)
                h_group(1, 1)
                with dve.Fori(2, NG - 1, 2) as g0:
                    for k in range(2):
                        h_group(g0 + k, k)
                dve.wait_ge(sem("z_ready"), NG)
                v.tensor_scalar(v3(eb), z[:, :, H:2 * H], -1.0, None, ALU.mult).then_inc(sem("eb_in"), 1)
                link(v.tensor_tensor(v3(za), z[:, :, 0:H], dtb.rearrange("p (a h) -> p a h", a=1).broadcast_to([P, T, H]), ALU.add))
                link(v.tensor_scalar(nz, za, -1.0, None, ALU.mult))
                v.tensor_tensor(nz, nz, za, ALU.min).then_inc(sem("nz_ready"), 1)
                dve.wait_ge(sem("ez_ready"), 1)
                dve.wait_ge(sem("alog"), 1)
                link(v.tensor_scalar(den, ez, 2.0, None, ALU.add))
                link(v.reciprocal(den, den))
                link(v.tensor_tensor(sser, ez, den, ALU.mult))
                link(v.tensor_tensor(s2, sser, sser, ALU.mult))
                link(v.tensor_scalar(pol, s2, 1.0 / 15, None, ALU.mult))
                for k in (13, 11, 9, 7, 5, 3):
                    link(v.scalar_tensor_tensor(pol, pol, 1.0 / k, s2, ALU.add, ALU.mult))
                link(v.scalar_tensor_tensor(pol, pol, 1.0, sser, ALU.add, ALU.mult))
                link(v.tensor_scalar(za, za, 0.0, None, ALU.max))
                link(v.scalar_tensor_tensor(za, pol, 2.0, za, ALU.mult, ALU.add))
                v.scalar_tensor_tensor(v3(nz), v3(za), -1.0, alog.rearrange("p (a h) -> p a h", a=1).broadcast_to([P, T, H]),
                                       ALU.mult, ALU.mult).then_inc(sem("g_ready"), 1)
                dve.wait_ge(sem("ez_ready"), 2)
                link(v.tensor_scalar(eb, eb, 1.0, None, ALU.add))
                v.reciprocal(tab[:, :, 0:H], v3(eb)).then_inc(sem("beta"), 1)
                dve.wait_ge(sem("arow_made"), 1)
                link(v.tensor_copy(arow, bank[0][:, 0:TH].rearrange("p (r i) -> p r i", i=P)))
                for r in range(NR):
                    ins = v.tensor_tensor_scan(crow[:, r, :], arow[:, r, :], zrow, 1.0, ALU.mult, ALU.add)
                link(ins)
                v.tensor_scalar(crow, crow, rmask, None, ALU.mult).then_inc(sem("crow_ready"), 1)
                v.memset(arow[:, :, 0:1], 0.0).then_inc(sem("arow_ready"), 1)
                dve.wait_ge(sem("ctab_made"), 1)
                v.tensor_copy(tab[:, :, H:2 * H], v3(bank[1][:, 0:TH]))
                v.tensor_scalar(tab[:, :, 2 * H:3 * H], v3(bank[1][:, 0:TH]), -1.0, None, ALU.mult)
                dve.wait_ge(sem("ce_in"), 16)
                v.tensor_copy(tab[:, :, 3 * H:4 * H], v3(al)).then_inc(sem("tab_done"), 1)

            @bA.scalar
            def _(act):
                a = nc.scalar
                act.wait_ge(sem("small_in"), 80)
                a.activation(alog, alog, ACT.Exp).then_inc(sem("alog"), 1)

                def z_group(g, k):
                    act.wait_ge(sem("hTp"), g + 1)
                    if not (isinstance(g, int) and g < 2):
                        act.wait_ge(sem(f"hT_out{k}"), 8 * (g - k))
                        act.wait_ge(sem("zp"), g - 1)
                    a.copy(hTs[:, k].rearrange("p k i -> p (k i)"), bank[2 + k][:, :]).then_inc(sem("hT_ready"), 1)
                    act.wait_ge(sem("zp"), g + 1)
                    a.copy(z[:, bass.ds(g * GRP, GRP), :].rearrange("p t k -> p (t k)"),
                           bank[4 + k][:, 0:GRP * 2 * H]).then_inc(sem("z_ready"), 1)
                z_group(0, 0)
                z_group(1, 1)
                with act.Fori(2, NG - 1, 2) as g0:
                    for k in range(2):
                        z_group(g0 + k, k)
                act.wait_ge(sem("nz_ready"), 1)
                a.activation(ez, nz, ACT.Exp).then_inc(sem("ez_ready"), 1)
                act.wait_ge(sem("eb_in"), 1)
                act.wait_ge(sem("alog"), 1)
                a.activation(eb, eb, ACT.Exp).then_inc(sem("ez_ready"), 1)
                act.wait_ge(sem("g_ready"), 1)
                a.activation(al, nz, ACT.Exp).then_inc(sem("alpha"), 1)

            @bA.tensor
            def _(pe):
                pe.wait_ge(sem("const_all"), 1)
                pe.wait_ge(sem("small_in"), 80)

                def h_group(g, k):
                    pe.wait_ge(sem("h_ready"), g + 1)
                    if not (isinstance(g, int) and g < 2):
                        pe.wait_ge(sem("z_ready"), g - 1)
                    for j in range(GRP):
                        ins = nc.tensor.transpose(bank[2 + k][:, j * P:j * P + P], hst[:, k, j, :], ident[:])
                    ins.then_inc(sem("hTp"), 1)
                    pe.wait_ge(sem("hT_ready"), g + 1)
                    for j in range(GRP):
                        ins = nc.tensor.matmul(bank[4 + k][:, j * 2 * H:(j + 1) * 2 * H], hTs[:, k, j, :], wab,
                                               start=(j == 0), stop=(j == GRP - 1), skip_group_check=True)
                    ins.then_inc(sem("zp"), 1)
                h_group(0, 0)
                h_group(1, 1)
                with pe.Fori(2, NG - 1, 2) as g0:
                    for k in range(2):
                        h_group(g0 + k, k)
                pe.wait_ge(sem("alpha"), 1)
                for r in range(NR):
                    ins = nc.tensor.transpose(bank[0][:, r * P:r * P + P], al[:, r * P:r * P + P], ident[:])
                ins.then_inc(sem("arow_made"), 1)
                pe.wait_ge(sem("crow_ready"), 1)
                for r in range(NR):
                    ins = nc.tensor.transpose(bank[1][:, r * P:r * P + P], crow[:, r, :], ident[:])
                ins.then_inc(sem("ctab_made"), 1)

        end_program()

        with ExitStack() as c2:
            off2 = [0]

            def cutd(dt=F32, n=HD):
                w = n if dt == F32 else n // 2
                off2[0] += w
                assert off2[0] <= W_ARENA, off2[0]
                r = arena[:, off2[0] - w:off2[0]]
                return r if dt == F32 else r.bitcast(dt)

            kbuf = cutd()
            sq = cutd()
            khT = [cutd() for _ in range(2)]
            qT = [cutd() for _ in range(2)]
            vbuf = [cutd() for _ in range(2)]
            gbuf = cutd()
            qbuf = cutd()
            Eb = cutd()
            N32 = cutd()
            UF = cutd()
            Pm = [cutd() for _ in range(2)]
            kw = [cutd() for _ in range(2)]
            St = cutd()
            Rb = cutd()
            Db = cutd()
            Ob = cutd()
            osq = cutd()
            onT = cutd()
            Nhi, Nlo, Nbd, Tm, Um, Xm, Em = (cutd(F16) for _ in range(7))
            alb = c2.enter_context(nc.sbuf_tensor("alb", [P, HD], F32))
            bI = c2.enter_context(nc.sbuf_tensor("bI", [P, HD], F32))
            hT = c2.enter_context(nc.sbuf_tensor("hT", [P, 2, P], F32))
            hTc = c2.enter_context(nc.sbuf_tensor("hTc", [P, P], F32))
            ident4 = c2.enter_context(nc.sbuf_tensor("ident4", [P, HH, P], F16))
            yt = c2.enter_context(nc.sbuf_tensor("yt", [P, P], F32))
            xpt = c2.enter_context(nc.sbuf_tensor("xpt", [P, P], F32))
            Tp = c2.enter_context(nc.sbuf_tensor("Tp", [P, H, BLK], F16))
            cur = c2.enter_context(nc.sbuf_tensor("cur", [P, 4 * H], F32))
            qsum = c2.enter_context(nc.sbuf_tensor("qsum", [P, H], F32))
            ksum = c2.enter_context(nc.sbuf_tensor("ksum", [P, H], F32))
            rk = c2.enter_context(nc.sbuf_tensor("rk", [P, H], F32))
            osum = c2.enter_context(nc.sbuf_tensor("osum", [P, H], F32))
            small = c2.enter_context(nc.sbuf_tensor("small", [P, 5, H], F32))
            ssq = c2.enter_context(nc.sbuf_tensor("ssq", [P, T, H], F32))
            bB = c2.enter_context(nc.Block())

            hv = lambda a: a.rearrange("p (h c) -> p h c", h=H)
            hh = lambda a, f: a[:, f * BANK:(f + 1) * BANK]
            h4 = lambda a: a.rearrange("p (h c) -> p h c", h=HH)
            ps = lambda name, f: bank[2 * PAIR[name] + f][:, :]
            SUB, AUX = bank[7], bank[6]
            kind = lambda name: name.rstrip("012")
            made = lambda name: sem("made_" + kind(name))
            read = lambda name: sem("read_" + kind(name))

            def at(name, t, f):
                return upto(t, f) if name[-1] not in "012" else 6 * t + 2 * int(name[-1]) + f + 1
            bcm = lambda m: m[:].rearrange("p (a c) -> p a c", a=1).broadcast_to([P, HH, P])

            def tile_of(stage, tau):
                return {"a": tau + 1, "b": tau, "c": tau - 1}[stage]

            def live(stage, tau):
                return not isinstance(tau, int) or 0 <= tile_of(stage, tau) < T

            def claim(pe, name, tau, f):
                k = [n for n, _ in PAIR_USES].index(name)
                for back in range(1, 2 * len(PAIR_USES) + 1):
                    n, s = PAIR_USES[(k - back) % len(PAIR_USES)]
                    when = tau - (0 if k - back >= 0 else 1 if k - back >= -len(PAIR_USES) else 2)
                    if PAIR[n] == PAIR[name] and live(s, when):
                        wait(pe, read(n), at(n, tile_of(s, when), f))
                        return

            def each(body):
                return body

            def run(eng, body):
                for tau in (-1, 0, 1, 2):
                    body(tau, tau % 2)
                with eng.Fori(3, T - 2, 2) as i:
                    body(i, 1)
                    body(i + 1, 0)
                for tau in (T - 1, T):
                    body(tau, tau % 2)

            @bB.sync
            def _(sp):
                def load_h(t, p):
                    wait(sp, made("V"), at("V", t - 2, 1))
                    sp.dma_start(hT[:, p, :], hT_d[bass.ds(t, 1)].rearrange("a p i -> p (a i)")
                                 ).then_inc(sem(f"hT_in{p}"), 16)

                def body(tau, p):
                    a, c = tau + 1, tau - 1
                    if isinstance(tau, int) and tau == -1:
                        load_h(0, 0)
                    if live("a", tau):
                        wait(sp, sem("scan"), a)
                        sp.dma_start(alb[:], al_d[bass.ds(a * H, H)].rearrange("(o h) i -> o (h i)", o=1)
                                     .broadcast_to([P, HD])).then_inc(sem("al_in"), 16)
                        if not isinstance(tau, int) or a + 1 < T:
                            load_h(a + 1, p)
                    if live("c", tau):
                        wait(sp, sem("xp_ready"), c)
                        wait(sp, made("GT"), at("GT", c - 1, 1))
                        sp.dma_start(hTc[:], hT_d[bass.ds(c, 1)].rearrange("a p i -> p (a i)")).then_inc(sem("hTc_in"), 16)
                        sp.dma_start(yt[:], y_d[bass.ds(c, 1)].rearrange("a p i -> p (a i)")).then_inc(sem("y_in"), 16)
                        sp.wait_ge(sem("xp_ready"), c + 1)
                        sp.dma_start(xp_d[bass.ds(c, 1)].rearrange("a p i -> p (a i)"), xpt[:]).then_inc(sem("xp_out"), 16)
                for tau in (-1, 0, 1, 2):
                    body(tau, tau % 2)
                with sp.Fori(3, T - 4, 2) as i:
                    body(i, 1)
                    body(i + 1, 0)
                for tau in (T - 3, T - 2, T - 1, T):
                    body(tau, tau % 2)
                sp.wait_ge(sem("xp_out"), 16 * T)

            @bB.tensor
            def _(pe):
                mm = nc.tensor.matmul

                def heads(name, tau, f, t, lhs, rhs):
                    claim(pe, name, tau, f)
                    for j in range(HH):
                        h = f * HH + j
                        ins = mm(ps(name, f)[:, j * P:j * P + P], lhs(h), rhs(h), start=(j == 0), stop=(j == HH - 1),
                                 skip_group_check=True)
                    ins.then_inc(made(name), 1)

                def col(buf):
                    return lambda h: buf[:, h * P:h * P + P]

                def project(name, tau, f, w, lhs):
                    claim(pe, name, tau, f)
                    mm(ps(name, f), lhs, hh(w, f), start=True, stop=True).then_inc(made(name), 1)

                def merged(name, tau, f, base, lhs, rhs):
                    claim(pe, name, tau, f)
                    mm(ps(name, f), ident16[:], hh(base, f), start=True, stop=False, skip_group_check=True)
                    for j in range(HH):
                        h = f * HH + j
                        ins = mm(ps(name, f)[:, j * P:j * P + P], col(lhs)(h), col(rhs)(h), start=False,
                                 stop=(j == HH - 1), skip_group_check=True)
                    ins.then_inc(made(name), 1)

                def transposes(name, tau, f, src):
                    claim(pe, name, tau, f)
                    for j in range(HH):
                        h = f * HH + j
                        ins = nc.tensor.transpose(ps(name, f)[:, j * P:j * P + P], col(src)(h), ident[:])
                    ins.then_inc(made(name), 1)

                def body(tau, p):
                    A, Bs, C = (live(s, tau) for s in "abc")
                    a, b, c = tau + 1, tau, tau - 1
                    q = 1 - p
                    if Bs:
                        for f in range(2):
                            pe.wait_ge(read("KT"), at("KT", b, f))
                            heads("G", tau, f, b, col(khT[p]), col(khT[p]))
                        for f in range(2):
                            pe.wait_ge(read("Q"), at("Q", b, f))
                            heads("QK", tau, f, b, col(khT[p]), col(qT[p]))
                    if C:
                        for f in range(2):
                            wait(pe, read("SU"), at("SU", c - 1, f))
                            if isinstance(c, int) and c == 0:
                                pe.wait_ge(sem("state0"), 2)
                            heads("KS", tau, f, c, col(khT[q]), col(St))
                    if A:
                        pe.wait_ge(sem(f"hT_in{q}"), 8 * (a - q) + 16)
                        for f in range(2):
                            project("K", tau, f, wk, hT[:, q, :])
                    for n in range(BLK - 1):
                        if Bs:
                            if n == 0:
                                pe.wait_ge(sem("Nbd"), b + 1)
                                wait(pe, sem("Tbd"), b)
                            else:
                                pe.wait_ge(sem("sub"), (BLK - 1) * b + n)
                            mm(SUB[:, 0:P], ident16[:], identp8[:].rearrange("p h c -> p (h c)"), start=True, stop=False,
                               skip_group_check=True)
                            for h in range(H):
                                rhs = identp[:] if n == 0 else Tp[:, h, :]
                                ins = mm(SUB[:, h * BLK:(h + 1) * BLK], col(Nbd)(h), rhs, start=False, stop=(h == H - 1),
                                         skip_group_check=True)
                            ins.then_inc(sem("sub_made"), 1)
                        f = n % 2
                        if C and n < 2:
                            pe.wait_ge(read("KS"), at("KS", c, f))
                            pe.wait_ge(read("C"), at("C", c, f))
                            heads("D", tau, f, c, col(UF), col(Rb))
                        elif C and n < 4:
                            pe.wait_ge(read("D"), at("D", c, f))
                            pe.wait_ge(read("QK"), at("QK", c, f))
                            heads("PD", tau, f, c, col(Pm[q]), col(Db))
                        elif C and n < 6:
                            heads("QS", tau, f, c, col(qT[q]), col(St))
                        elif C and n < 8:
                            if f == 0:
                                pe.wait_ge(sem("kw"), c + 1)
                            heads("SU", tau, f, c, col(kw[q]), col(Db))
                        elif A and 8 <= n < 10:
                            project("Q", tau, f, wq, hT[:, q, :])
                        elif A and 10 <= n < 12:
                            pe.wait_ge(read("Q"), at("Q", a, f))
                            transposes("QT", tau, f, qbuf)
                        elif A and 12 <= n < 14:
                            pe.wait_ge(sem("kh"), a + 1)
                            transposes("KT", tau, f, kbuf)
                    if Bs:
                        pe.wait_ge(sem("Tbd"), b + 1)
                        for f in range(2):
                            heads("UB", tau, f, b, col(Tm), lambda h: ident16[:])
                    for lv in range(3):
                        if Bs:
                            for f in range(2):
                                if lv == 0:
                                    pe.wait_ge(sem("Nhi"), upto(b, f))
                                else:
                                    pe.wait_ge(read(f"T{lv - 1}"), at(f"T{lv - 1}", b, f))
                                heads(f"X{lv}", tau, f, b, col(Nhi), col(Tm))
                        if C and lv == 0:
                            pe.wait_ge(sem("hTc_in"), 16 * c + 16)
                            for f in range(2):
                                project("GT", tau, f, wg, hTc[:])
                        if A and lv == 1:
                            for f in range(2):
                                project("V", tau, f, wv, hT[:, q, :])
                        if C and lv == 2:
                            pe.wait_ge(sem("on"), c + 1)
                            for f in range(2):
                                transposes("OT", tau, f, Ob)
                        if Bs:
                            for f in range(2):
                                pe.wait_ge(read(f"X{lv}"), at(f"X{lv}", b, f))
                                U = "UB" if lv == 0 else f"U{lv - 1}"
                                pe.wait_ge(read(U), at(U, b, f))
                                merged(f"T{lv}", tau, f, Tm, Um, Xm)
                                merged(f"U{lv}", tau, f, Um, Xm, Um)
                    if Bs:
                        pe.wait_ge(sem("Nlo"), b + 1)
                        for f in range(2):
                            pe.wait_ge(read("T2"), at("T2", b, f))
                            claim(pe, "E", tau, f)
                            o = ps("E", f)
                            mm(o, negid16[:], hh(Tm, f), start=True, stop=False, skip_group_check=True)
                            mm(o, ident16[:], ident4[:].rearrange("p h c -> p (h c)"), start=False, stop=False,
                               skip_group_check=True)
                            for j in range(HH):
                                h = f * HH + j
                                oj = o[:, j * P:j * P + P]
                                mm(oj, col(Nhi)(h), col(Tm)(h), start=False, stop=False, skip_group_check=True)
                                ins = mm(oj, col(Nlo)(h), col(Tm)(h), start=False, stop=(j == HH - 1), skip_group_check=True)
                            ins.then_inc(made("E"), 1)
                    if C:
                        for f in range(2):
                            pe.wait_ge(read("OT"), at("OT", c, f))
                        wait(pe, sem("xp_ready"), c)
                        for h in range(H):
                            ins = mm(AUX[:, 0:P], col(onT)(h), col(wo)(h), start=(h == 0), stop=(h == H - 1))
                        ins.then_inc(sem("att_made"), 1)
                    if Bs:
                        for f in range(2):
                            pe.wait_ge(read("E"), at("E", b, f))
                            pe.wait_ge(read("U2"), at("U2", b, f))
                            heads("C", tau, f, b, col(Em), col(Um))
                run(pe, body)

            @bB.scalar
            def _(act):
                a_ = nc.scalar

                def body(tau, p):
                    A, Bs, C = (live(s, tau) for s in "abc")
                    a, b, c = tau + 1, tau, tau - 1
                    q = 1 - p

                    def take(name, t, f, dst, func=ACT.Copy, scale=1.0):
                        act.wait_ge(made(name), at(name, t, f))
                        a_.activation(hh(dst, f), ps(name, f), func, scale=scale).then_inc(read(name), 1)
                    if Bs:
                        for f in range(2):
                            act.wait_ge(read("G"), at("G", b, f))
                            wait(act, made("E"), at("E", b - 1, 1))
                            wait(act, sem("Nlo"), b)
                            a_.copy(hh(Nhi, f), hh(N32, f)).then_inc(sem("Nhi"), 1)
                    if A:
                        for f in range(2):
                            wait(act, made("KT"), at("KT", a - 1, 1))
                            wait(act, sem("kw"), a)
                            take("K", a, f, kbuf, ACT.Silu)
                    for n in range(BLK - 1):
                        if Bs:
                            act.wait_ge(sem("sub_made"), (BLK - 1) * b + n + 1)
                            a_.copy(Tp[:].rearrange("p h c -> p (h c)"), SUB[:, 0:P]).then_inc(sem("sub"), 1)
                        f = n % 2
                        if C and n < 2:
                            wait(act, made("SU"), at("SU", c - 1, f))
                            take("D", c, f, Db)
                        elif C and n < 4:
                            wait(act, made("OT"), at("OT", c - 1, f))
                            take("PD", c, f, Ob)
                        elif A and 8 <= n < 10:
                            wait(act, made("QT"), at("QT", a - 1, 1))
                            wait(act, sem("qsq"), a)
                            take("Q", a, f, qbuf, ACT.Silu)
                        elif A and 10 <= n < 12:
                            wait(act, made("QS"), at("QS", a - 2, f))
                            take("QT", a, f, qT[q])
                        elif A and 12 <= n < 14:
                            wait(act, made("KS"), at("KS", a - 2, f))
                            take("KT", a, f, khT[q])
                    if Bs:
                        for f in range(2):
                            wait(act, made("C"), at("C", b - 1, f))
                            take("UB", b, f, Um)
                    for lv in range(3):
                        if C and lv == 0:
                            for f in range(2):
                                wait(act, sem("sgr"), c)
                                take("GT", c, f, gbuf, ACT.Silu)
                        if A and lv == 1:
                            for f in range(2):
                                wait(act, read("KS"), at("KS", a - 2, f))
                                take("V", a, f, vbuf[q], ACT.Silu)
                        if C and lv == 2:
                            for f in range(2):
                                wait(act, sem("att_made"), c)
                                take("OT", c, f, onT)
                        if Bs:
                            for f in range(2):
                                take(f"T{lv}", b, f, Tm)
                                take(f"U{lv}", b, f, Um)
                    if Bs:
                        for f in range(2):
                            wait(act, made("C"), at("C", b - 1, f))
                            take("E", b, f, Em, scale=ESC)
                run(act, body)

            @bB.vector
            def _(dve):
                v = nc.vector

                def body(tau, p):
                    A, Bs, C = (live(s, tau) for s in "abc")
                    a, b, c = tau + 1, tau, tau - 1
                    q = 1 - p
                    if isinstance(tau, int) and tau == -1:
                        v.memset(St, 0.0).then_inc(sem("state0"), 1)
                        v.tensor_copy(ident4[:], bcm(ident16)).then_inc(sem("state0"), 1)
                    if Bs:
                        for f in range(2):
                            dve.wait_ge(made("G"), at("G", b, f))
                            dve.wait_ge(sem("Ebn"), b + 1)
                            v.tensor_tensor(hh(N32, f), ps("G", f), hh(N32, f), ALU.mult).then_inc(read("G"), 1)
                        for f in range(2):
                            dve.wait_ge(made("QK"), at("QK", b, f))
                            wait(dve, made("PD"), at("PD", b - 2, f))
                            v.tensor_tensor(hh(Pm[p], f), ps("QK", f), hh(Eb, f), ALU.mult).then_inc(read("QK"), 1)
                    if C:
                        wait(dve, read("SU"), at("SU", c - 1, 1))
                        v.tensor_copy(cur[:], tab[:, bass.ds(c, 1), :].rearrange("p a k -> p (a k)")).then_inc(sem("cur"), 1)
                        dve.wait_ge(sem("cur"), c + 1)
                        for f in range(2):
                            dve.wait_ge(made("KS"), at("KS", c, f))
                            wait(dve, made("D"), at("D", c - 1, f))
                            dve.wait_ge(read("V"), at("V", c, f))
                            for j in range(HH):
                                h = f * HH + j
                                ins = v.scalar_tensor_tensor(hv(Rb)[:, h, :], ps("KS", f)[:, j * P:j * P + P],
                                                             cur[:, 2 * H + h:2 * H + h + 1], hv(vbuf[q])[:, h, :],
                                                             ALU.mult, ALU.add)
                            ins.then_inc(read("KS"), 1)
                    for n in range(BLK - 1):
                        f = n % 2
                        if A and n == 2:
                            dve.wait_ge(sem("ksq"), a + 1)
                            wait(dve, sem("rk"), a)
                            v.tensor_reduce(ksum[:], hv(sq), AX.X, ALU.add).then_inc(sem("ksum"), 1)
                        elif C and 4 <= n < 6:
                            dve.wait_ge(made("QS"), at("QS", c, f))
                            dve.wait_ge(read("PD"), at("PD", c, f))
                            for j in range(HH):
                                h = f * HH + j
                                ins = v.scalar_tensor_tensor(hv(Ob)[:, h, :], ps("QS", f)[:, j * P:j * P + P],
                                                             cur[:, H + h:H + h + 1], hv(Ob)[:, h, :], ALU.mult, ALU.add)
                            ins.then_inc(read("QS"), 1)
                        elif C and 6 <= n < 8:
                            dve.wait_ge(made("SU"), at("SU", c, f))
                            for j in range(HH):
                                h = f * HH + j
                                ins = v.scalar_tensor_tensor(hv(St)[:, h, :], hv(St)[:, h, :],
                                                             cur[:, 3 * H + h:3 * H + h + 1],
                                                             ps("SU", f)[:, j * P:j * P + P], ALU.mult, ALU.add)
                            ins.then_inc(read("SU"), 1)
                        elif A and n == 10:
                            dve.wait_ge(sem("bI"), a + 1)
                            dve.wait_ge(sem("al_in"), 16 * a + 16)
                            if Bs:
                                dve.wait_ge(read("QK"), at("QK", b, 1))
                            wait(dve, sem("kw"), a)
                            v.tensor_tensor_scan(Eb, alb[:], bI[:], 0.0, ALU.mult, ALU.add).then_inc(sem("scan"), 1)
                        elif C and n == 12:
                            dve.wait_ge(sem("osq"), c + 1)
                            v.tensor_reduce(osum[:], hv(osq), AX.X, ALU.add).then_inc(sem("osum"), 1)
                        elif A and n == 13:
                            dve.wait_ge(sem("qsq"), a + 1)
                            v.tensor_reduce(qsum[:], hv(sq), AX.X, ALU.add).then_inc(sem("qsum"), 1)
                            dve.wait_ge(sem("qsum"), a + 1)
                            v.tensor_scalar(ssq[:, bass.ds(a, 1), :].rearrange("p a h -> p (a h)"), qsum[:], RMS_EPS, None,
                                            ALU.add).then_inc(sem("ssq_ready"), 1)
                    if Bs:
                        dve.wait_ge(sem("sub"), (BLK - 1) * (b + 1))
                        wait(dve, made("E"), at("E", b - 1, 1))
                        v.tensor_tensor(Tm.rearrange("p (h g c) -> p h g c", h=H, c=BLK),
                                        Tp[:].rearrange("p h (a c) -> p h a c", a=1).broadcast_to([P, H, P // BLK, BLK]),
                                        maskbd[:].rearrange("p (a g c) -> p a g c", a=1, c=BLK).broadcast_to([P, H, P // BLK, BLK]),
                                        ALU.mult).then_inc(sem("Tbd"), 1)
                    for lv in range(3):
                        if Bs:
                            for f in range(2):
                                dve.wait_ge(made(f"X{lv}"), at(f"X{lv}", b, f))
                                if lv == 0:
                                    wait(dve, made("U2"), at("U2", b - 1, f))
                                else:
                                    dve.wait_ge(made(f"U{lv - 1}"), at(f"U{lv - 1}", b, f))
                                v.tensor_tensor(h4(hh(Xm, f)), h4(ps(f"X{lv}", f)), bcm(mask[lv]), ALU.mult
                                                ).then_inc(read(f"X{lv}"), 1)
                        if C and lv == 1:
                            dve.wait_ge(sem("sgr"), c + 1)
                            dve.wait_ge(read("QS"), at("QS", c, 1))
                            v.tensor_tensor(Ob, Ob, osq, ALU.mult).then_inc(sem("on"), 1)
                    if C:
                        dve.wait_ge(sem("att_made"), c + 1)
                        dve.wait_ge(sem("y_in"), 16 * c + 16)
                        wait(dve, sem("xp_out"), 16 * c)
                        v.tensor_tensor(xpt[:], AUX[:, 0:P], yt[:], ALU.add).then_inc(sem("xp_ready"), 1)
                    if Bs:
                        for f in range(2):
                            dve.wait_ge(made("C"), at("C", b, f))
                            wait(dve, made("D"), at("D", b - 1, f))
                            v.scalar_tensor_tensor(hh(UF, f), ps("C", f), 1.0 / ESC, hh(Um, f), ALU.mult, ALU.add
                                                   ).then_inc(read("C"), 1)
                run(dve, body)

            @bB.gpsimd
            def _(pool):
                g = nc.gpsimd
                bch = lambda cols: cols.rearrange("p (h a) -> p h a", a=1).broadcast_to([P, H, P])

                def body(tau, p):
                    A, Bs, C = (live(s, tau) for s in "abc")
                    a, b, c = tau + 1, tau, tau - 1
                    q = 1 - p
                    if Bs:
                        pool.wait_ge(sem("Nhi"), upto(b, 1))
                        wait(pool, sem("sub_made"), (BLK - 1) * b)
                        g.tensor_tensor(hv(Nbd), hv(Nhi), maskbd[:].rearrange("p (a c) -> p a c", a=1).broadcast_to([P, H, P]),
                                        ALU.mult).then_inc(sem("Nbd"), 1)
                        g.tensor_tensor(Nlo, N32, Nhi, ALU.subtract).then_inc(sem("Nlo"), 1)
                    if A:
                        pool.wait_ge(read("K"), at("K", a, 1))
                        wait(pool, sem("qsum"), a)
                        g.tensor_tensor(sq, kbuf, kbuf, ALU.mult).then_inc(sem("ksq"), 1)
                        wait(pool, sem("scan"), a)
                        wait(pool, sem("Ebn"), a)
                        g.tensor_tensor(hv(bI[:]), ident[:].rearrange("p (a c) -> p a c", a=1).broadcast_to([P, H, P]),
                                        bch(tab[:, bass.ds(a, 1), 0:H].rearrange("p a h -> p (a h)")), ALU.mult
                                        ).then_inc(sem("bI"), 1)
                        pool.wait_ge(sem("ksum"), a + 1)
                        g.tensor_tensor(ksum[:], ksum[:], keps[:], ALU.add).then_inc(sem("kpe"), 1)
                        pool.wait_ge(sem("kpe"), a + 1)
                        g.tensor_tensor(rk[:], ksum[:], mhalf[:, 0:H], ALU.pow).then_inc(sem("rk"), 1)
                        pool.wait_ge(sem("rk"), a + 1)
                        g.tensor_tensor(hv(kbuf), hv(kbuf), bch(rk[:]), ALU.mult).then_inc(sem("kh"), 1)
                    if C:
                        for f in range(2):
                            pool.wait_ge(read("QS"), at("QS", c, f))
                        wait(pool, sem("on"), c)
                        g.tensor_tensor(osq, Ob, Ob, ALU.mult).then_inc(sem("osq"), 1)
                    if A:
                        pool.wait_ge(read("Q"), at("Q", a, 1))
                        pool.wait_ge(sem("ksum"), a + 1)
                        g.tensor_tensor(sq, qbuf, qbuf, ALU.mult).then_inc(sem("qsq"), 1)
                        pool.wait_ge(sem("scan"), a + 1)
                        g.tensor_tensor(N32, bI[:], Eb, ALU.subtract).then_inc(sem("Ebn"), 1)
                        wait(pool, made("SU"), at("SU", a - 2, 1))
                        pool.wait_ge(sem("kh"), a + 1)
                        g.tensor_tensor(hv(kw[q]), hv(kbuf), hv(Eb)[:, :, P - 1:P].broadcast_to([P, H, P]), ALU.mult
                                        ).then_inc(sem("kw"), 1)
                    if C:
                        o = small[:]

                        def step(ins, k):
                            ins.then_inc(sem("r_chain"), 1)
                            pool.wait_ge(sem("r_chain"), 6 * c + k)
                        pool.wait_ge(sem("ssq_ready"), c + 1)
                        step(g.tensor_tensor(o[:, 0, :], ssq[:, bass.ds(c, 1), :].rearrange("p a h -> p (a h)"),
                                             mhalf[:, 0:H], ALU.pow), 1)
                        g.tensor_tensor(o[:, 1, :], o[:, 0, :], krt[:], ALU.mult)
                        step(g.tensor_tensor(o[:, 2, :], o[:, 0, :], kinv[:], ALU.mult), 2)
                        step(g.tensor_tensor(o[:, 2, :], o[:, 2, :], o[:, 2, :], ALU.mult), 3)
                        pool.wait_ge(sem("osum"), c + 1)
                        step(g.tensor_tensor(o[:, 3, :], o[:, 2, :], osum[:], ALU.mult), 4)
                        step(g.tensor_tensor(o[:, 3, :], o[:, 3, :], keps[:], ALU.add), 5)
                        step(g.tensor_tensor(o[:, 4, :], o[:, 3, :], mhalf[:, 0:H], ALU.pow), 6)
                        g.tensor_tensor(o[:, 4, :], o[:, 4, :], o[:, 1, :], ALU.mult).then_inc(sem("r"), 1)
                        pool.wait_ge(sem("r"), c + 1)
                        pool.wait_ge(read("GT"), at("GT", c, 1))
                        g.tensor_tensor(hv(osq), hv(gbuf), bch(o[:, 4, :]), ALU.mult).then_inc(sem("sgr"), 1)
                run(pool, body)

        end_program()

        with ExitStack() as c3:
            off3 = [0]

            def cutt(n):
                off3[0] += n
                assert off3[0] <= W_ARENA
                return arena[:, off3[0] - n:off3[0]]
            GW = GRP * P
            two = lambda: [cutt(GW) for _ in range(2)]
            xg, xpg = two(), two()
            sqg, mg, mTg, x1g, tg, tTg = cutt(GW), cutt(GW), cutt(GW), two(), cutt(GW), two()
            h1, h2 = cutt(NF * GW), cutt(NF * GW)
            wfc = cutt(DFF)
            wpj = cutt(NF * P).rearrange("p (j n) -> p j n", j=NF)
            gwT = cutt(NE)
            sm = cutt(12 * GRP).rearrange("p (k t) -> p k t", k=12)
            st3 = cutt(GRP * 6).rearrange("p (t s) -> p t s", s=6)
            gws = cutt(P)
            lg = cutt(T * NE).rearrange("p (t e) -> p t e", e=NE)
            t4 = lambda a: a.rearrange("p (t d) -> p t d", t=GRP)
            bcd = lambda a: a.rearrange("p (t a) -> p t a", a=1).broadcast_to([P, GRP, P])
            gsl = lambda d, g: d[bass.ds(g * GRP, GRP)].rearrange("t p d -> p t d")

            def groups(eng, body):
                for g in range(2):
                    body(g, g)
                with eng.Fori(2, NG - 1, 2) as g0:
                    body(g0, 0)
                    body(g0 + 1, 1)

            b3 = c3.enter_context(nc.Block())

            @b3.sync
            def _(sp):
                sp.dma_start(wfc, W_fc).then_inc(sem("m_w"), 16)
                sp.dma_start(wpj, W_proj.rearrange("(j p) n -> p j n", p=P)).then_inc(sem("m_w"), 16)
                sp.dma_start(gws[0:NE, :], gate_w).then_inc(sem("m_w"), 16)

                def body(g, k):
                    wait(sp, sem("m_x1"), g - 1)
                    sp.dma_start(t4(xg[k]), x_t[bass.ds(g * GW, GW), :].rearrange("(t p) d -> p t d", p=P)
                                 ).then_inc(sem(f"m_in{k}"), 16)
                    sp.dma_start(t4(xpg[k]), gsl(xp_d, g)).then_inc(sem(f"m_in{k}"), 16)
                groups(sp, body)

            @b3.gpsimd
            def _(pool):
                g_ = nc.gpsimd

                def body(g, k):
                    pool.wait_ge(sem(f"m_in{k}"), 16 * (g - k) + 32)
                    g_.tensor_tensor(sqg, xpg[k], xpg[k], ALU.mult).then_inc(sem("m_sq"), 1)
                    pool.wait_ge(sem("m_ms"), g + 1)
                    g_.tensor_tensor(sm[:, 1, :], sm[:, 0, :], mhalf[:, 0:GRP], ALU.pow).then_inc(sem("m_r"), 1)
                    for j in range(NF):
                        pool.wait_ge(sem("m_relu"), NF * g + j + 1)
                        if j == 0:
                            wait(pool, sem("m_pj"), g)
                        g_.tensor_tensor(h2[:, j * GW:(j + 1) * GW], h1[:, j * GW:(j + 1) * GW],
                                         h1[:, j * GW:(j + 1) * GW], ALU.mult).then_inc(sem("m_h2"), 1)
                    pool.wait_ge(sem("m_var"), g + 1)
                    g_.tensor_tensor(sm[:, 6, :], sm[:, 5, :], mhalf[:, 0:GRP], ALU.pow).then_inc(sem("m_r3"), 1)
                groups(pool, body)

            @b3.vector
            def _(dve):
                v = nc.vector
                NL = 8

                def body(g, k):
                    def link(ins, i):
                        ins.then_inc(sem("m_v"), 1)
                        dve.wait_ge(sem("m_v"), NL * g + i)
                    dve.wait_ge(sem("m_sq"), g + 1)
                    link(v.tensor_reduce(sm[:, 0, :], t4(sqg), AX.X, ALU.add), 1)
                    v.tensor_scalar(sm[:, 0, :], sm[:, 0, :], 1.0 / D, RMS_EPS, ALU.mult, ALU.add).then_inc(sem("m_ms"), 1)
                    dve.wait_ge(sem("m_r"), g + 1)
                    wait(dve, sem("m_mTp"), g)
                    v.tensor_tensor(t4(mg), t4(xpg[k]), bcd(sm[:, 1, :]), ALU.mult).then_inc(sem("m_m"), 1)
                    dve.wait_ge(sem("m_in0" if k == 0 else "m_in1"), 16 * (g - k) + 32)
                    wait(dve, sem(f"x1_out{k}"), 8 * (g - k))
                    link(v.tensor_tensor(x1g[k], xg[k], xpg[k], ALU.add), 2)
                    dve.wait_ge(sem("m_pj"), g + 1)
                    v.tensor_tensor(x1g[k], x1g[k], bank[6][:, :], ALU.add).then_inc(sem("m_x1"), 1)
                    dve.wait_ge(sem("m_x1"), g + 1)
                    for j in range(GRP):
                        ins = v.bn_stats(st3[:, j, :], x1g[k][:, j * P:j * P + P])
                    link(ins, 3)
                    v.tensor_tensor(sm[:, 2, :], st3[:, :, 1], st3[:, :, 4], ALU.add)
                    v.tensor_tensor(sm[:, 4, :], st3[:, :, 2], st3[:, :, 5], ALU.add)
                    link(v.tensor_tensor(sm[:, 3, :], st3[:, :, 1], st3[:, :, 4], ALU.subtract), 4)
                    v.tensor_scalar(sm[:, 7, :], sm[:, 2, :], 0.5, None, ALU.mult)
                    link(v.scalar_tensor_tensor(sm[:, 3, :], sm[:, 3, :], 0.25, sm[:, 3, :], ALU.mult, ALU.mult), 5)
                    link(v.scalar_tensor_tensor(sm[:, 5, :], sm[:, 4, :], 1.0 / D, sm[:, 3, :], ALU.mult, ALU.add), 6)
                    v.tensor_scalar(sm[:, 5, :], sm[:, 5, :], LN_EPS, None, ALU.add).then_inc(sem("m_var"), 1)
                    wait(dve, sem("m_tTp"), g)
                    link(v.tensor_tensor(t4(tg), t4(x1g[k]), bcd(sm[:, 7, :]), ALU.subtract), 7)
                    dve.wait_ge(sem("m_r3"), g + 1)
                    link(v.tensor_tensor(t4(tg), t4(tg), bcd(sm[:, 6, :]), ALU.mult), 8)
                    v.memset(sm[:, 8, :], 0.0).then_inc(sem("m_t"), 1)
                    dve.wait_ge(sem("m_lgp"), g + 1)
                    v.tensor_copy(lg[:, bass.ds(g * GRP, GRP), :].rearrange("p t e -> p (t e)"),
                                  bank[7][:, 0:GRP * NE]).then_inc(sem("m_lg"), 1)
                groups(dve, body)

            @b3.scalar
            def _(act):
                a_ = nc.scalar
                act.wait_ge(sem("m_gwp"), 1)
                a_.copy(gwT, bank[7][:, 0:NE]).then_inc(sem("m_gwT"), 1)

                def body(g, k):
                    act.wait_ge(sem("m_mTp"), g + 1)
                    wait(act, sem("m_fc"), NF * g)
                    a_.copy(mTg, bank[0][:, :]).then_inc(sem("m_mT"), 1)
                    for j in range(NF):
                        act.wait_ge(sem("m_fc"), NF * g + j + 1)
                        if j == 0:
                            wait(act, sem("m_h2"), NF * g)
                        a_.activation(h1[:, j * GW:(j + 1) * GW], bank[1 + j][:, :], ACT.Relu).then_inc(sem("m_relu"), 1)
                    act.wait_ge(sem("m_x1"), g + 1)
                    act.dma_start(gsl(x1_d, g), t4(x1g[k])).then_inc(sem(f"x1_out{k}"), 16)
                    act.wait_ge(sem("m_tTp"), g + 1)
                    wait(act, sem(f"tT_out{k}"), 8 * (g - k))
                    wait(act, sem("m_lgp"), g - 1)
                    a_.copy(tTg[k], bank[5][:, :]).then_inc(sem("m_tT"), 1)
                    act.wait_ge(sem("m_tT"), g + 1)
                    act.dma_start(gsl(tT_d, g), t4(tTg[k])).then_inc(sem(f"tT_out{k}"), 16)
                groups(act, body)
                for n in ("x1_out0", "x1_out1", "tT_out0", "tT_out1"):
                    act.wait_ge(sem(n), 8 * NG)

            @b3.tensor
            def _(pe):
                mm = nc.tensor.matmul
                pe.wait_ge(sem("m_w"), 48)
                nc.tensor.transpose(bank[7][:, 0:NE], gws[0:NE, :], ident[0:NE, 0:NE]).then_inc(sem("m_gwp"), 1)
                pe.wait_ge(sem("m_gwT"), 1)

                def body(g, k):
                    pe.wait_ge(sem("m_m"), g + 1)
                    for j in range(GRP):
                        ins = nc.tensor.transpose(bank[0][:, j * P:j * P + P], mg[:, j * P:j * P + P], ident[:])
                    ins.then_inc(sem("m_mTp"), 1)
                    pe.wait_ge(sem("m_mT"), g + 1)
                    for j in range(NF):
                        wait(pe, sem("m_relu"), NF * g - NF + j + 1)
                        mm(bank[1 + j][:, :], wfc[:, j * P:j * P + P], mTg, start=True, stop=True).then_inc(sem("m_fc"), 1)
                    pe.wait_ge(sem("m_h2"), NF * g + NF)
                    for t in range(GRP):
                        for j in range(NF):
                            ins = mm(bank[6][:, t * P:t * P + P], h2[:, j * GW + t * P:j * GW + (t + 1) * P], wpj[:, j, :],
                                     start=(j == 0), stop=(j == NF - 1))
                    ins.then_inc(sem("m_pj"), 1)
                    pe.wait_ge(sem("m_t"), g + 1)
                    for j in range(GRP):
                        ins = nc.tensor.transpose(bank[5][:, j * P:j * P + P], tg[:, j * P:j * P + P], ident[:])
                    ins.then_inc(sem("m_tTp"), 1)
                    pe.wait_ge(sem("m_tT"), g + 1)
                    wait(pe, sem("m_lg"), g)
                    for j in range(GRP):
                        ins = mm(bank[7][:, j * NE:(j + 1) * NE], tTg[k][:, j * P:j * P + P], gwT,
                                 start=(j == 0), stop=(j == GRP - 1), skip_group_check=True)
                    ins.then_inc(sem("m_lgp"), 1)
                groups(pe, body)

        end_program()

        with ExitStack() as c4:
            off4 = [T * NE]
            lgoff = off3[0] - T * NE

            def cute(n):
                off4[0] += n
                assert off4[0] <= W_ARENA
                return arena[:, off4[0] - n:off4[0]]
            lgf = arena[:, lgoff:lgoff + T * NE]
            off4[0] = lgoff + T * NE
            c8 = lambda a: a.rearrange("p (t e) -> p t e", e=NE)
            pr, wt, sc, oh1, oh2, io = (cute(T * NE) for _ in range(6))
            red = cute(T)
            bce = lambda a: a.rearrange("p (t a) -> p t a", a=1).broadcast_to([P, T, NE])
            off4[0] = 0
            EW = NE * P
            lim = lgoff
            ews, ewT, ebb = cute(EW), cute(EW), cute(EW)
            cws, cwT = cute(P), cute(P)
            pre, act_o, wtd = cute(EW), cute(EW), cute(EW)
            mix, mixT = cute(P), cute(P)
            tT4 = [cute(GW) for _ in range(2)]
            x14 = [cute(GW) for _ in range(2)]
            ot4 = [cute(GW) for _ in range(2)]
            assert off4[0] <= lim, (off4[0], lim)
            HE = NE // 2
            bE = c4.enter_context(nc.Block())

            @bE.sync
            def _(sp):
                sp.dma_start(ews.rearrange("p (e h) -> p e h", e=NE), expert_w.rearrange("e d h -> d e h")).then_inc(sem("e_w"), 16)
                sp.dma_start(cws, combine_w).then_inc(sem("e_w"), 16)
                sp.dma_start(ebb, expert_b.rearrange("(a e) d -> a (e d)", a=1).broadcast_to([P, EW])).then_inc(sem("e_w"), 16)

                def body(g, k):
                    wait(sp, sem("e_ot"), GRP * (g - 1))
                    sp.dma_start(t4(tT4[k]), gsl(tT_d, g)).then_inc(sem(f"e_in{k}"), 16)
                    sp.dma_start(t4(x14[k]), gsl(x1_d, g)).then_inc(sem(f"e_in{k}"), 16)
                groups(sp, body)

            @bE.gpsimd
            def _(pool):
                g_ = nc.gpsimd
                for e in range(NE):
                    ins = g_.memset(c8(io)[:, :, e:e + 1], float(NE - e))
                ins.then_inc(sem("e_io"), 1)
                pool.wait_ge(sem("e_wt"), 1)

                def body(g, k):
                    for j in range(GRP):
                        t = g * GRP + j
                        pool.wait_ge(sem("e_act"), t + 1)
                        wait(pool, sem("e_mix"), t)
                        g_.tensor_tensor(wtd.rearrange("p (e d) -> p e d", e=NE), act_o.rearrange("p (e d) -> p e d", e=NE),
                                         c8(wt)[:, bass.ds(t, 1), :].rearrange("p a (e o) -> p (a e) o", o=1)
                                         .broadcast_to([P, NE, P]), ALU.mult).then_inc(sem("e_wtd"), 1)
                groups(pool, body)

            @bE.vector
            def _(dve):
                v = nc.vector
                cnt = [0]

                def link(ins):
                    cnt[0] += 1
                    ins.then_inc(sem("e_v"), 1)
                    dve.wait_ge(sem("e_v"), cnt[0])
                link(v.tensor_reduce(red, c8(lgf), AX.X, ALU.max))
                v.tensor_tensor(c8(pr), c8(lgf), bce(red), ALU.subtract).then_inc(sem("e_sh"), 1)
                dve.wait_ge(sem("e_ex"), 1)
                link(v.tensor_reduce(red, c8(pr), AX.X, ALU.add))
                link(v.reciprocal(red, red))
                link(v.tensor_tensor(c8(pr), c8(pr), bce(red), ALU.mult))
                dve.wait_ge(sem("e_io"), 1)
                link(v.tensor_copy(wt, pr))
                for oh in (oh1, oh2):
                    link(v.tensor_reduce(red, c8(wt), AX.X, ALU.max))
                    link(v.tensor_tensor(c8(sc), c8(wt), bce(red), ALU.is_equal))
                    link(v.tensor_tensor(sc, sc, io, ALU.mult))
                    link(v.tensor_reduce(red, c8(sc), AX.X, ALU.max))
                    link(v.tensor_tensor(c8(oh), c8(sc), bce(red), ALU.is_equal))
                    link(v.scalar_tensor_tensor(wt, oh, -2.0, wt, ALU.mult, ALU.add))
                link(v.tensor_tensor(oh1, oh1, oh2, ALU.add))
                v.tensor_tensor(wt, oh1, pr, ALU.mult).then_inc(sem("e_wt"), 1)
                dve.wait_ge(sem("e_w"), 48)

                def body(g, k):
                    for j in range(GRP):
                        t = g * GRP + j
                        wait(dve, sem("e_act"), t)
                        for f in range(2):
                            dve.wait_ge(sem("e_hp"), 2 * t + f + 1)
                            v.tensor_tensor(hh(pre, f), bank[2 * (j % 2) + f][:, :], hh(ebb, f), ALU.add).then_inc(sem("e_pre"), 1)
                        dve.wait_ge(sem("e_wtd"), t + 1)
                        wait(dve, sem("e_mTp"), t)
                        v.tensor_reduce(mix, wtd.rearrange("p (e d) -> p d e", e=NE), AX.X, ALU.add).then_inc(sem("e_mix"), 1)
                        dve.wait_ge(sem("e_op"), t + 1)
                        if j == 0:
                            dve.wait_ge(sem(f"e_in{k}"), 16 * (g - k) + 32)
                            wait(dve, sem(f"o_out{k}"), 8 * (g - k))
                        v.tensor_tensor(ot4[k][:, j * P:j * P + P], bank[6][:, 0:P], x14[k][:, j * P:j * P + P],
                                        ALU.add).then_inc(sem("e_ot"), 1)
                groups(dve, body)

            @bE.scalar
            def _(act):
                a_ = nc.scalar
                act.wait_ge(sem("e_sh"), 1)
                a_.activation(pr, pr, ACT.Exp).then_inc(sem("e_ex"), 1)
                for f in range(2):
                    act.wait_ge(sem("e_wp"), f + 1)
                    a_.copy(hh(ewT, f), bank[f][:, :]).then_inc(sem("e_wT"), 1)
                act.wait_ge(sem("e_wp"), 3)
                a_.copy(cwT, bank[2][:, 0:P]).then_inc(sem("e_wT"), 1)

                def body(g, k):
                    for j in range(GRP):
                        t = g * GRP + j
                        act.wait_ge(sem("e_pre"), 2 * t + 2)
                        wait(act, sem("e_wtd"), t)
                        a_.activation(act_o, pre, ACT.Silu).then_inc(sem("e_act"), 1)
                        act.wait_ge(sem("e_mTp"), t + 1)
                        wait(act, sem("e_op"), t)
                        a_.copy(mixT, bank[5][:, 0:P]).then_inc(sem("e_mT"), 1)
                    act.wait_ge(sem("e_ot"), GRP * g + GRP)
                    act.dma_start(out_t[bass.ds(g * GW, GW), :].rearrange("(t p) d -> p t d", p=P), t4(ot4[k])
                                  ).then_inc(sem(f"o_out{k}"), 16)
                groups(act, body)
                for n in ("o_out0", "o_out1"):
                    act.wait_ge(sem(n), 8 * NG)

            @bE.tensor
            def _(pe):
                mm = nc.tensor.matmul
                pe.wait_ge(sem("e_w"), 48)
                for f in range(2):
                    for j in range(HE):
                        e = f * HE + j
                        ins = nc.tensor.transpose(bank[f][:, j * P:j * P + P], ews[:, e * P:e * P + P], ident[:])
                    ins.then_inc(sem("e_wp"), 1)
                nc.tensor.transpose(bank[2][:, 0:P], cws, ident[:]).then_inc(sem("e_wp"), 1)
                pe.wait_ge(sem("e_wT"), 3)

                def experts(t, g, k, j):
                    if j == 0:
                        pe.wait_ge(sem(f"e_in{k}"), 16 * (g - k) + 32)
                    for f in range(2):
                        wait(pe, sem("e_pre"), 2 * (t - 2) + f + 1)
                        mm(bank[2 * (j % 2) + f][:, :], tT4[k][:, j * P:j * P + P], hh(ewT, f), start=True, stop=True
                           ).then_inc(sem("e_hp"), 1)

                def body(g, k):
                    for j in range(GRP):
                        t = g * GRP + j
                        if j == 0:
                            experts(t, g, k, 0)
                        if j + 1 < GRP:
                            experts(t + 1, g, k, j + 1)
                        pe.wait_ge(sem("e_mix"), t + 1)
                        wait(pe, sem("e_mT"), t)
                        nc.tensor.transpose(bank[5][:, 0:P], mix, ident[:]).then_inc(sem("e_mTp"), 1)
                        pe.wait_ge(sem("e_mT"), t + 1)
                        wait(pe, sem("e_ot"), t)
                        mm(bank[6][:, 0:P], mixT, cwT, start=True, stop=True).then_inc(sem("e_op"), 1)
                groups(pe, body)

        end_program()


_INS = ["L0_attn_x", "L0_attn_Wq", "L0_attn_Wk", "L0_attn_Wv", "L0_attn_Wb", "L0_attn_Wa", "L0_attn_A_log",
        "L0_attn_dt_bias", "L0_attn_Wg", "L0_attn_o_norm_w", "L0_attn_Wo", "L0_attn_W_fc", "L0_attn_W_proj",
        "L0_ffn_gate_w", "L0_ffn_expert_w", "L0_ffn_expert_b", "L0_ffn_combine_w"]


def kernel(**inputs):
    import numpy as _np
    import concourse.bacc as _bacc
    from concourse.bass_utils import run_bass_kernel_spmd as _run

    nc = _bacc.Bacc("TRN2", target_bir_lowering=False, num_devices=1)
    arrays, args = {}, []
    for name in _INS:
        a = _np.ascontiguousarray(inputs[name])
        arrays[f"in_{name}"] = a
        args.append(nc.dram_tensor(f"in_{name}", a.shape, mybir.dt.from_np(a.dtype), kind="ExternalInput").ap())
    shape = arrays["in_L0_attn_x"].shape
    args.append(nc.dram_tensor("out_0", shape, F32, kind="ExternalOutput").ap())
    tiles = shape[0] * shape[1] // P
    dram = {k: nc.dram_tensor(f"scratch_{k}", s, F32, kind="Internal").ap() for k, s in (
        ("y", (tiles, P, P)), ("hT", (tiles, P, P)), ("xp", (tiles, P, P)), ("x1", (tiles, P, P)),
        ("tT", (tiles, P, P)), ("al", (tiles * H, P)), ("ce", (tiles * H,)))}
    delta_moe(nc, *args, dram)
    r = _run(nc, [arrays], core_ids=[0])
    return r.results[0]["out_0"]
```

```python
from contextlib import ExitStack

import concourse.bass as bass
from concourse import mybir

ALU = mybir.AluOpType
ACT = mybir.ActivationFunctionType
AX = mybir.AxisListType
F32 = mybir.dt.float32
F16 = mybir.dt.float16

P = 128
H = 8
HD = H * P
BANK = 512
HH = H // 2
GRP = 4
BLK = 16
ESC = 1024.0
LN_EPS, RMS_EPS = 1e-5, 1e-6

PAIR_USES = [("G", "b"), ("KS", "c"), ("K", "a"), ("D", "c"), ("PD", "c"), ("QS", "c"), ("SU", "c"),
             ("Q", "a"), ("QT", "a"), ("KT", "a"), ("GT", "c"), ("UB", "b"), ("X0", "b"), ("QK", "b"),
             ("T0", "b"), ("U0", "b"), ("X1", "b"), ("V", "a"), ("T1", "b"), ("U1", "b"), ("X2", "b"),
             ("OT", "c"), ("T2", "b"), ("U2", "b"), ("E", "b"), ("C", "b")]
STAGE = dict(PAIR_USES)
PAIR = {name: k % 3 for k, (name, _) in enumerate(PAIR_USES)}


def upto(t, half):
    return 2 * t + half + 1


def wait(eng, sem, value):
    if not isinstance(value, int) or value > 0:
        eng.wait_ge(sem, value)


def delta_moe(nc, x, Wq, Wk, Wv, Wb, Wa, A_log, dt_bias, Wg, o_norm_w, Wo, W_fc, W_proj,
              gate_w, expert_w, expert_b, combine_w, out, dram):
    B, S_LEN, D = x.shape
    T = B * S_LEN // P
    CH = S_LEN // P
    NG = T // GRP
    DFF = W_fc.shape[1]
    NF = DFF // P
    NE = gate_w.shape[0]
    TH = T * H
    NR = TH // P
    x_t = x.rearrange("b s d -> (b s) d")
    out_t = out.rearrange("b s d -> (b s) d")
    y_d, hT_d, xp_d, al_d, ce_d, x1_d, tT_d = (dram[k] for k in ("y", "hT", "xp", "al", "ce", "x1", "tT"))

    with ExitStack() as ctx:
        def sb(name, shape, dt=F32):
            return ctx.enter_context(nc.sbuf_tensor(name, shape, dt))

        sems = {}

        def sem(name):
            if name not in sems:
                sems[name] = nc.alloc_semaphore(name=name)
            return sems[name]

        def end_program():
            nc.clear_and_free_semaphores(list(sems.values()))
            sems.clear()
            nc.all_engine_barrier()

        bank = [ctx.enter_context(nc.psum_tensor(f"bank{i}", [P, BANK], F32)) for i in range(8)]

        ident = sb("ident", [P, P])
        ident16 = sb("ident16", [P, P], F16)
        negid16 = sb("negid16", [P, P], F16)
        ones = sb("ones", [P, 8])
        mhalf = sb("mhalf", [P, 64])
        keps, krt, kinv = (sb(n, [P, H]) for n in ("keps", "krt", "kinv"))
        mask = [sb(f"mask{i}", [P, P], F16) for i in range(3)]
        maskbd = sb("maskbd", [P, P], F16)
        identp = sb("identp", [P, BLK], F16)
        identp8 = sb("identp8", [P, H, BLK], F16)
        wq, wk, wv, wg, wo = (sb(n, [P, HD]) for n in ("wq", "wk", "wv", "wg", "wo"))
        onw = sb("onw", [P, 1])
        tab = sb("tab", [P, T, 4 * H])
        W_ARENA = 28 * HD
        arena = sb("arena", [P, W_ARENA])

        with ExitStack() as c1:
            bA = c1.enter_context(nc.Block())
            xs = arena[:, 0:T * P].rearrange("p (t d) -> p t d", t=T)
            off = [T * P]

            def cut(n):
                off[0] += n
                assert off[0] <= W_ARENA
                return arena[:, off[0] - n:off[0]]
            hst = cut(2 * BANK).rearrange("p (s k d) -> p s k d", s=2, k=GRP)
            hTs = cut(2 * BANK).rearrange("p (s k d) -> p s k d", s=2, k=GRP)
            st = cut(T * 6).rearrange("p (t s) -> p t s", s=6)
            mean, var, r1, r2, tmp1, tmp2 = (cut(T) for _ in range(6))
            wab = cut(2 * H)
            alog, dtb = cut(H), cut(H)
            z = cut(T * 2 * H).rearrange("p (t k) -> p t k", k=2 * H)
            za, nz, ez, den, sser, s2, pol, al = (cut(TH) for _ in range(8))
            eb = cut(TH)
            arow = cut(TH).rearrange("p (r i) -> p r i", i=P)
            crow = cut(TH).rearrange("p (r i) -> p r i", i=P)
            zrow = cut(P)
            rmask = cut(1)
            v3 = lambda a: a.rearrange("p (t h) -> p t h", h=H)

            @bA.sync
            def _(sp):
                for dst, src in ((wq, Wq), (wk, Wk), (wv, Wv), (wg, Wg)):
                    sp.dma_start(dst[:], src).then_inc(sem("w_in"), 16)
                sp.dma_start(wo[:].rearrange("p (h n) -> p h n", h=H),
                             Wo.rearrange("(h p) n -> p h n", p=P)).then_inc(sem("w_in"), 16)
                sp.wait_ge(sem("y_ready"), 1)
                sp.dma_start(y_d.rearrange("t p d -> p t d"), xs).then_inc(sem("y_out"), 16)
                for g in range(2):
                    sp.wait_ge(sem("hT_ready"), g + 1)
                    sp.dma_start(hT_d[g * GRP:g * GRP + GRP].rearrange("t p i -> p t i"),
                                 hTs[:, g % 2]).then_inc(sem(f"hT_out{g % 2}"), 16)
                with sp.Fori(2, NG - 1, 2) as g0:
                    for k in range(2):
                        sp.wait_ge(sem("hT_ready"), g0 + k + 1)
                        sp.dma_start(hT_d[bass.ds(g0 * GRP + k * GRP, GRP)].rearrange("t p i -> p t i"),
                                     hTs[:, k]).then_inc(sem(f"hT_out{k}"), 16)
                sp.wait_ge(sem("arow_ready"), 1)
                sp.dma_start(al_d.rearrange("(r p) i -> p r i", p=P), arow).then_inc(sem("al_out"), 16)
                sp.wait_ge(sem("crow_ready"), 1)
                with nc.allow_non_contiguous_dma("512 numbers, once"):
                    sp.dma_start(ce_d.rearrange("(r p) -> p r", p=P), crow[:, :, P - 1]).then_inc(sem("ce_out"), 16)
                sp.wait_ge(sem("ce_out"), 16)
                sp.dma_start(al, ce_d.rearrange("(a n) -> a n", a=1).broadcast_to([P, TH])).then_inc(sem("ce_in"), 16)
                for s, v in (("y_out", 16), ("hT_out0", 8 * NG), ("hT_out1", 8 * NG), ("al_out", 16),
                             ("w_in", 80), ("ce_in", 16)):
                    sp.wait_ge(sem(s), v)

            @bA.gpsimd
            def _(pool):
                pool.dma_start(xs, x_t.rearrange("(t p) d -> p t d", p=P)).then_inc(sem("x_in"), 16)
                pool.dma_start(wab[:, 0:H], Wa).then_inc(sem("small_in"), 16)
                pool.dma_start(wab[:, H:2 * H], Wb).then_inc(sem("small_in"), 16)
                pool.dma_start(alog, A_log.rearrange("(a n) -> a n", a=1).broadcast_to([P, H])).then_inc(sem("small_in"), 16)
                pool.dma_start(dtb, dt_bias.rearrange("(a n) -> a n", a=1).broadcast_to([P, H])).then_inc(sem("small_in"), 16)
                pool.dma_start(onw[:], o_norm_w.rearrange("(p a) -> p a", a=1)).then_inc(sem("small_in"), 16)
                n = 0
                g = nc.gpsimd

                def step(ins):
                    nonlocal n
                    n += 1
                    ins.then_inc(sem("const"), 1)
                    pool.wait_ge(sem("const"), n)
                step(g.memset(ident[:], 0.0))
                step(g.memset(ident16[:], 0.0))
                step(g.memset(negid16[:], 0.0))
                step(g.memset(ones[:], 1.0))
                step(g.memset(mhalf[:], -0.5))
                step(g.memset(keps[:], RMS_EPS))
                step(g.memset(krt[:], float(P) ** -0.5))
                step(g.memset(kinv[:], 1.0 / P))
                step(g.memset(maskbd[:], 1.0))
                for m in mask:
                    step(g.memset(m[:], 0.0))
                step(g.memset(zrow, 0.0))
                step(g.memset(rmask, 1.0))
                for m, v in ((ident, 1.0), (ident16, 1.0), (negid16, -1.0)):
                    step(g.affine_select(out=m[:], in_=m[:], compare_op=ALU.not_equal, fill=v, base=0,
                                         pattern=[[-1, P]], channel_multiplier=1))
                for r in range(0, P // H, CH):
                    step(g.memset(rmask[r * H:r * H + H, :], 0.0))
                mb = maskbd[:].rearrange("p (g c) -> p g c", c=BLK)
                step(g.affine_select(out=mb, in_=mb, compare_op=ALU.is_ge, fill=0.0, base=0,
                                     pattern=[[-BLK, P // BLK], [0, BLK]], channel_multiplier=1))
                step(g.affine_select(out=mb, in_=mb, compare_op=ALU.is_ge, fill=0.0, base=BLK - 1,
                                     pattern=[[BLK, P // BLK], [0, BLK]], channel_multiplier=-1))
                for i, m in enumerate(mask):
                    s = BLK << i
                    half = m[:].rearrange("p (g c) -> p g c", c=2 * s)[:, :, 0:s]
                    step(g.memset(half, 1.0))
                for i, m in enumerate(mask):
                    s = BLK << i
                    half = m[:].rearrange("p (g c) -> p g c", c=2 * s)[:, :, 0:s]
                    step(g.affine_select(out=half, in_=half, compare_op=ALU.is_ge, fill=0.0, base=-s,
                                         pattern=[[-2 * s, P // (2 * s)], [0, s]], channel_multiplier=1))
                for i, m in enumerate(mask):
                    s = BLK << i
                    half = m[:].rearrange("p (g c) -> p g c", c=2 * s)[:, :, 0:s]
                    step(g.affine_select(out=half, in_=half, compare_op=ALU.is_ge, fill=0.0, base=2 * s - 1,
                                         pattern=[[2 * s, P // (2 * s)], [0, s]], channel_multiplier=-1))
                g.memset(zrow[0:1, 0:1], 0.0).then_inc(sem("const_all"), 1)
                pool.wait_ge(sem("var_ready"), 1)
                g.tensor_tensor(r1, tmp1, mhalf[:, 0:T], ALU.pow).then_inc(sem("r1_ready"), 1)
                pool.wait_ge(sem("w_ready"), 1)
                g.tensor_tensor(r2, tmp2, mhalf[:, 0:T], ALU.pow).then_inc(sem("r2_ready"), 1)
                pool.wait_ge(sem("small_in"), 80)

            @bA.vector
            def _(dve):
                v = nc.vector
                cnt = [0]

                def link(ins):
                    cnt[0] += 1
                    ins.then_inc(sem("v1"), 1)
                    dve.wait_ge(sem("v1"), cnt[0])
                dve.wait_ge(sem("const_all"), 1)
                with nc.allow_low_precision("zeros and ones"):
                    link(v.tensor_reduce(identp[:], ident16[:].rearrange("p (g c) -> p c g", c=BLK), AX.X, ALU.add))
                link(v.tensor_copy(identp8[:], identp[:].rearrange("p (a c) -> p a c", a=1).broadcast_to([P, H, BLK])))
                dve.wait_ge(sem("x_in"), 16)
                with dve.Fori(0, T) as t:
                    v.bn_stats(st[:, bass.ds(t, 1), :].rearrange("p a s -> p (a s)"),
                               xs[:, bass.ds(t, 1), :].rearrange("p a d -> p (a d)")).then_inc(sem("st"), 1)
                dve.wait_ge(sem("st"), T)
                v.tensor_tensor(mean, st[:, :, 1], st[:, :, 4], ALU.add)
                link(v.tensor_tensor(tmp1, st[:, :, 1], st[:, :, 4], ALU.subtract))
                link(v.tensor_scalar(mean, mean, 0.5, None, ALU.mult))
                link(v.scalar_tensor_tensor(tmp1, tmp1, 0.25, tmp1, ALU.mult, ALU.mult))
                link(v.tensor_tensor(tmp2, st[:, :, 2], st[:, :, 5], ALU.add))
                link(v.scalar_tensor_tensor(var, tmp2, 1.0 / D, tmp1, ALU.mult, ALU.add))
                v.tensor_scalar(tmp1, var, LN_EPS, None, ALU.add).then_inc(sem("var_ready"), 1)
                bc = lambda a: a.rearrange("p (t a) -> p t a", a=1).broadcast_to([P, T, P])
                link(v.tensor_tensor(xs, xs, bc(mean), ALU.subtract))
                dve.wait_ge(sem("r1_ready"), 1)
                link(v.tensor_tensor(tmp2, r1, r1, ALU.mult))
                link(v.tensor_tensor(tmp2, tmp2, var, ALU.mult))
                v.tensor_scalar(tmp2, tmp2, RMS_EPS, None, ALU.add).then_inc(sem("w_ready"), 1)
                v.tensor_tensor(xs, xs, bc(r1), ALU.mult).then_inc(sem("y_ready"), 1)
                dve.wait_ge(sem("w_in"), 80)
                dve.wait_ge(sem("small_in"), 80)
                v.tensor_scalar(wo[:], wo[:], onw[:, 0:1], None, ALU.mult).then_inc(sem("wo_scaled"), 1)
                dve.wait_ge(sem("r2_ready"), 1)
                dve.wait_ge(sem("y_ready"), 1)

                def h_group(g, k):
                    if isinstance(g, int) and g < 2:
                        pass
                    else:
                        dve.wait_ge(sem("hTp"), g - 1)
                    for j in range(GRP):
                        t = g * GRP + j
                        ins = v.tensor_scalar(hst[:, k, j, :], xs[:, bass.ds(t, 1), :].rearrange("p a d -> p (a d)"),
                                              r2[:, bass.ds(t, 1)], None, ALU.mult)
                    ins.then_inc(sem("h_ready"), 1)
                h_group(0, 0)
                h_group(1, 1)
                with dve.Fori(2, NG - 1, 2) as g0:
                    for k in range(2):
                        h_group(g0 + k, k)
                dve.wait_ge(sem("z_ready"), NG)
                v.tensor_scalar(v3(eb), z[:, :, H:2 * H], -1.0, None, ALU.mult).then_inc(sem("eb_in"), 1)
                link(v.tensor_tensor(v3(za), z[:, :, 0:H], dtb.rearrange("p (a h) -> p a h", a=1).broadcast_to([P, T, H]), ALU.add))
                link(v.tensor_scalar(nz, za, -1.0, None, ALU.mult))
                v.tensor_tensor(nz, nz, za, ALU.min).then_inc(sem("nz_ready"), 1)
                dve.wait_ge(sem("ez_ready"), 1)
                dve.wait_ge(sem("alog"), 1)
                link(v.tensor_scalar(den, ez, 2.0, None, ALU.add))
                link(v.reciprocal(den, den))
                link(v.tensor_tensor(sser, ez, den, ALU.mult))
                link(v.tensor_tensor(s2, sser, sser, ALU.mult))
                link(v.tensor_scalar(pol, s2, 1.0 / 15, None, ALU.mult))
                for k in (13, 11, 9, 7, 5, 3):
                    link(v.scalar_tensor_tensor(pol, pol, 1.0 / k, s2, ALU.add, ALU.mult))
                link(v.scalar_tensor_tensor(pol, pol, 1.0, sser, ALU.add, ALU.mult))
                link(v.tensor_scalar(za, za, 0.0, None, ALU.max))
                link(v.scalar_tensor_tensor(za, pol, 2.0, za, ALU.mult, ALU.add))
                v.scalar_tensor_tensor(v3(nz), v3(za), -1.0, alog.rearrange("p (a h) -> p a h", a=1).broadcast_to([P, T, H]),
                                       ALU.mult, ALU.mult).then_inc(sem("g_ready"), 1)
                dve.wait_ge(sem("ez_ready"), 2)
                link(v.tensor_scalar(eb, eb, 1.0, None, ALU.add))
                v.reciprocal(tab[:, :, 0:H], v3(eb)).then_inc(sem("beta"), 1)
                dve.wait_ge(sem("arow_made"), 1)
                link(v.tensor_copy(arow, bank[0][:, 0:TH].rearrange("p (r i) -> p r i", i=P)))
                for r in range(NR):
                    ins = v.tensor_tensor_scan(crow[:, r, :], arow[:, r, :], zrow, 1.0, ALU.mult, ALU.add)
                link(ins)
                v.tensor_scalar(crow, crow, rmask, None, ALU.mult).then_inc(sem("crow_ready"), 1)
                v.memset(arow[:, :, 0:1], 0.0).then_inc(sem("arow_ready"), 1)
                dve.wait_ge(sem("ctab_made"), 1)
                v.tensor_copy(tab[:, :, H:2 * H], v3(bank[1][:, 0:TH]))
                v.tensor_scalar(tab[:, :, 2 * H:3 * H], v3(bank[1][:, 0:TH]), -1.0, None, ALU.mult)
                dve.wait_ge(sem("ce_in"), 16)
                v.tensor_copy(tab[:, :, 3 * H:4 * H], v3(al)).then_inc(sem("tab_done"), 1)

            @bA.scalar
            def _(act):
                a = nc.scalar
                act.wait_ge(sem("small_in"), 80)
                a.activation(alog, alog, ACT.Exp).then_inc(sem("alog"), 1)

                def z_group(g, k):
                    act.wait_ge(sem("hTp"), g + 1)
                    if not (isinstance(g, int) and g < 2):
                        act.wait_ge(sem(f"hT_out{k}"), 8 * (g - k))
                        act.wait_ge(sem("zp"), g - 1)
                    a.copy(hTs[:, k].rearrange("p k i -> p (k i)"), bank[2 + k][:, :]).then_inc(sem("hT_ready"), 1)
                    act.wait_ge(sem("zp"), g + 1)
                    a.copy(z[:, bass.ds(g * GRP, GRP), :].rearrange("p t k -> p (t k)"),
                           bank[4 + k][:, 0:GRP * 2 * H]).then_inc(sem("z_ready"), 1)
                z_group(0, 0)
                z_group(1, 1)
                with act.Fori(2, NG - 1, 2) as g0:
                    for k in range(2):
                        z_group(g0 + k, k)
                act.wait_ge(sem("nz_ready"), 1)
                a.activation(ez, nz, ACT.Exp).then_inc(sem("ez_ready"), 1)
                act.wait_ge(sem("eb_in"), 1)
                act.wait_ge(sem("alog"), 1)
                a.activation(eb, eb, ACT.Exp).then_inc(sem("ez_ready"), 1)
                act.wait_ge(sem("g_ready"), 1)
                a.activation(al, nz, ACT.Exp).then_inc(sem("alpha"), 1)

            @bA.tensor
            def _(pe):
                pe.wait_ge(sem("const_all"), 1)
                pe.wait_ge(sem("small_in"), 80)

                def h_group(g, k):
                    pe.wait_ge(sem("h_ready"), g + 1)
                    if not (isinstance(g, int) and g < 2):
                        pe.wait_ge(sem("z_ready"), g - 1)
                    for j in range(GRP):
                        ins = nc.tensor.transpose(bank[2 + k][:, j * P:j * P + P], hst[:, k, j, :], ident[:])
                    ins.then_inc(sem("hTp"), 1)
                    pe.wait_ge(sem("hT_ready"), g + 1)
                    for j in range(GRP):
                        ins = nc.tensor.matmul(bank[4 + k][:, j * 2 * H:(j + 1) * 2 * H], hTs[:, k, j, :], wab,
                                               start=(j == 0), stop=(j == GRP - 1), skip_group_check=True)
                    ins.then_inc(sem("zp"), 1)
                h_group(0, 0)
                h_group(1, 1)
                with pe.Fori(2, NG - 1, 2) as g0:
                    for k in range(2):
                        h_group(g0 + k, k)
                pe.wait_ge(sem("alpha"), 1)
                for r in range(NR):
                    ins = nc.tensor.transpose(bank[0][:, r * P:r * P + P], al[:, r * P:r * P + P], ident[:])
                ins.then_inc(sem("arow_made"), 1)
                pe.wait_ge(sem("crow_ready"), 1)
                for r in range(NR):
                    ins = nc.tensor.transpose(bank[1][:, r * P:r * P + P], crow[:, r, :], ident[:])
                ins.then_inc(sem("ctab_made"), 1)

        end_program()

        with ExitStack() as c2:
            off2 = [0]

            def cutd(dt=F32, n=HD):
                w = n if dt == F32 else n // 2
                off2[0] += w
                assert off2[0] <= W_ARENA, off2[0]
                r = arena[:, off2[0] - w:off2[0]]
                return r if dt == F32 else r.bitcast(dt)

            kbuf = cutd()
            sq = cutd()
            khT = [cutd() for _ in range(2)]
            qT = [cutd() for _ in range(2)]
            vbuf = [cutd() for _ in range(2)]
            gbuf = cutd()
            qbuf = cutd()
            Eb = cutd()
            N32 = cutd()
            UF = cutd()
            Pm = [cutd() for _ in range(2)]
            kw = [cutd() for _ in range(2)]
            St = cutd()
            Rb = cutd()
            Db = cutd()
            Ob = cutd()
            osq = cutd()
            onT = cutd()
            Nhi, Nlo, Nbd, Tm, Um, Xm, Em = (cutd(F16) for _ in range(7))
            alb = c2.enter_context(nc.sbuf_tensor("alb", [P, HD], F32))
            bI = c2.enter_context(nc.sbuf_tensor("bI", [P, HD], F32))
            hT = c2.enter_context(nc.sbuf_tensor("hT", [P, 2, P], F32))
            hTc = c2.enter_context(nc.sbuf_tensor("hTc", [P, P], F32))
            ident4 = c2.enter_context(nc.sbuf_tensor("ident4", [P, HH, P], F16))
            yt = c2.enter_context(nc.sbuf_tensor("yt", [P, P], F32))
            xpt = c2.enter_context(nc.sbuf_tensor("xpt", [P, P], F32))
            Tp = c2.enter_context(nc.sbuf_tensor("Tp", [P, H, BLK], F16))
            cur = c2.enter_context(nc.sbuf_tensor("cur", [P, 4 * H], F32))
            qsum = c2.enter_context(nc.sbuf_tensor("qsum", [P, H], F32))
            ksum = c2.enter_context(nc.sbuf_tensor("ksum", [P, H], F32))
            rk = c2.enter_context(nc.sbuf_tensor("rk", [P, H], F32))
            osum = c2.enter_context(nc.sbuf_tensor("osum", [P, H], F32))
            small = c2.enter_context(nc.sbuf_tensor("small", [P, 5, H], F32))
            ssq = c2.enter_context(nc.sbuf_tensor("ssq", [P, T, H], F32))
            bB = c2.enter_context(nc.Block())

            hv = lambda a: a.rearrange("p (h c) -> p h c", h=H)
            hh = lambda a, f: a[:, f * BANK:(f + 1) * BANK]
            h4 = lambda a: a.rearrange("p (h c) -> p h c", h=HH)
            ps = lambda name, f: bank[2 * PAIR[name] + f][:, :]
            SUB, AUX = bank[7], bank[6]
            kind = lambda name: name.rstrip("012")
            made = lambda name: sem("made_" + kind(name))
            read = lambda name: sem("read_" + kind(name))

            def at(name, t, f):
                return upto(t, f) if name[-1] not in "012" else 6 * t + 2 * int(name[-1]) + f + 1
            bcm = lambda m: m[:].rearrange("p (a c) -> p a c", a=1).broadcast_to([P, HH, P])

            def tile_of(stage, tau):
                return {"a": tau + 1, "b": tau, "c": tau - 1}[stage]

            def live(stage, tau):
                return not isinstance(tau, int) or 0 <= tile_of(stage, tau) < T

            def claim(pe, name, tau, f):
                k = [n for n, _ in PAIR_USES].index(name)
                for back in range(1, 2 * len(PAIR_USES) + 1):
                    n, s = PAIR_USES[(k - back) % len(PAIR_USES)]
                    when = tau - (0 if k - back >= 0 else 1 if k - back >= -len(PAIR_USES) else 2)
                    if PAIR[n] == PAIR[name] and live(s, when):
                        wait(pe, read(n), at(n, tile_of(s, when), f))
                        return

            def each(body):
                return body

            def run(eng, body):
                for tau in (-1, 0, 1, 2):
                    body(tau, tau % 2)
                with eng.Fori(3, T - 2, 2) as i:
                    body(i, 1)
                    body(i + 1, 0)
                for tau in (T - 1, T):
                    body(tau, tau % 2)

            @bB.sync
            def _(sp):
                def load_h(t, p):
                    wait(sp, made("V"), at("V", t - 2, 1))
                    sp.dma_start(hT[:, p, :], hT_d[bass.ds(t, 1)].rearrange("a p i -> p (a i)")
                                 ).then_inc(sem(f"hT_in{p}"), 16)

                def body(tau, p):
                    a, c = tau + 1, tau - 1
                    if isinstance(tau, int) and tau == -1:
                        load_h(0, 0)
                    if live("a", tau):
                        wait(sp, sem("scan"), a)
                        sp.dma_start(alb[:], al_d[bass.ds(a * H, H)].rearrange("(o h) i -> o (h i)", o=1)
                                     .broadcast_to([P, HD])).then_inc(sem("al_in"), 16)
                        if not isinstance(tau, int) or a + 1 < T:
                            load_h(a + 1, p)
                    if live("c", tau):
                        wait(sp, sem("xp_ready"), c)
                        wait(sp, made("GT"), at("GT", c - 1, 1))
                        sp.dma_start(hTc[:], hT_d[bass.ds(c, 1)].rearrange("a p i -> p (a i)")).then_inc(sem("hTc_in"), 16)
                        sp.dma_start(yt[:], y_d[bass.ds(c, 1)].rearrange("a p i -> p (a i)")).then_inc(sem("y_in"), 16)
                        sp.wait_ge(sem("xp_ready"), c + 1)
                        sp.dma_start(xp_d[bass.ds(c, 1)].rearrange("a p i -> p (a i)"), xpt[:]).then_inc(sem("xp_out"), 16)
                for tau in (-1, 0, 1, 2):
                    body(tau, tau % 2)
                with sp.Fori(3, T - 4, 2) as i:
                    body(i, 1)
                    body(i + 1, 0)
                for tau in (T - 3, T - 2, T - 1, T):
                    body(tau, tau % 2)
                sp.wait_ge(sem("xp_out"), 16 * T)

            @bB.tensor
            def _(pe):
                mm = nc.tensor.matmul

                def heads(name, tau, f, t, lhs, rhs):
                    claim(pe, name, tau, f)
                    for j in range(HH):
                        h = f * HH + j
                        ins = mm(ps(name, f)[:, j * P:j * P + P], lhs(h), rhs(h), start=(j == 0), stop=(j == HH - 1),
                                 skip_group_check=True)
                    ins.then_inc(made(name), 1)

                def col(buf):
                    return lambda h: buf[:, h * P:h * P + P]

                def project(name, tau, f, w, lhs):
                    claim(pe, name, tau, f)
                    mm(ps(name, f), lhs, hh(w, f), start=True, stop=True).then_inc(made(name), 1)

                def merged(name, tau, f, base, lhs, rhs):
                    claim(pe, name, tau, f)
                    mm(ps(name, f), ident16[:], hh(base, f), start=True, stop=False, skip_group_check=True)
                    for j in range(HH):
                        h = f * HH + j
                        ins = mm(ps(name, f)[:, j * P:j * P + P], col(lhs)(h), col(rhs)(h), start=False,
                                 stop=(j == HH - 1), skip_group_check=True)
                    ins.then_inc(made(name), 1)

                def transposes(name, tau, f, src):
                    claim(pe, name, tau, f)
                    for j in range(HH):
                        h = f * HH + j
                        ins = nc.tensor.transpose(ps(name, f)[:, j * P:j * P + P], col(src)(h), ident[:])
                    ins.then_inc(made(name), 1)

                def body(tau, p):
                    A, Bs, C = (live(s, tau) for s in "abc")
                    a, b, c = tau + 1, tau, tau - 1
                    q = 1 - p
                    if Bs:
                        for f in range(2):
                            pe.wait_ge(read("KT"), at("KT", b, f))
                            heads("G", tau, f, b, col(khT[p]), col(khT[p]))
                    if C:
                        for f in range(2):
                            wait(pe, read("SU"), at("SU", c - 1, f))
                            if isinstance(c, int) and c == 0:
                                pe.wait_ge(sem("state0"), 2)
                            heads("KS", tau, f, c, col(khT[q]), col(St))
                    if A:
                        pe.wait_ge(sem(f"hT_in{q}"), 8 * (a - q) + 16)
                        for f in range(2):
                            project("K", tau, f, wk, hT[:, q, :])
                    for n in range(BLK - 1):
                        if Bs:
                            if n == 0:
                                pe.wait_ge(sem("Nbd"), b + 1)
                                wait(pe, sem("Tbd"), b)
                            else:
                                pe.wait_ge(sem("sub"), (BLK - 1) * b + n)
                            mm(SUB[:, 0:P], ident16[:], identp8[:].rearrange("p h c -> p (h c)"), start=True, stop=False,
                               skip_group_check=True)
                            for h in range(H):
                                rhs = identp[:] if n == 0 else Tp[:, h, :]
                                ins = mm(SUB[:, h * BLK:(h + 1) * BLK], col(Nbd)(h), rhs, start=False, stop=(h == H - 1),
                                         skip_group_check=True)
                            ins.then_inc(sem("sub_made"), 1)
                        f = n % 2
                        if C and n < 2:
                            pe.wait_ge(read("KS"), at("KS", c, f))
                            pe.wait_ge(read("C"), at("C", c, f))
                            heads("D", tau, f, c, col(UF), col(Rb))
                        elif C and n < 4:
                            pe.wait_ge(read("D"), at("D", c, f))
                            pe.wait_ge(read("QK"), at("QK", c, f))
                            heads("PD", tau, f, c, col(Pm[q]), col(Db))
                        elif C and n < 6:
                            heads("QS", tau, f, c, col(qT[q]), col(St))
                        elif C and n < 8:
                            if f == 0:
                                pe.wait_ge(sem("kw"), c + 1)
                            heads("SU", tau, f, c, col(kw[q]), col(Db))
                        elif A and 8 <= n < 10:
                            project("Q", tau, f, wq, hT[:, q, :])
                        elif A and 10 <= n < 12:
                            pe.wait_ge(read("Q"), at("Q", a, f))
                            transposes("QT", tau, f, qbuf)
                        elif A and 12 <= n < 14:
                            pe.wait_ge(sem("kh"), a + 1)
                            transposes("KT", tau, f, kbuf)
                    if C:
                        pe.wait_ge(sem("hTc_in"), 16 * c + 16)
                        for f in range(2):
                            project("GT", tau, f, wg, hTc[:])
                    if Bs:
                        pe.wait_ge(sem("Tbd"), b + 1)
                        for f in range(2):
                            heads("UB", tau, f, b, col(Tm), lambda h: ident16[:])
                    for lv in range(3):
                        if Bs:
                            for f in range(2):
                                if lv == 0:
                                    pe.wait_ge(sem("Nhi"), upto(b, f))
                                else:
                                    pe.wait_ge(read(f"T{lv - 1}"), at(f"T{lv - 1}", b, f))
                                heads(f"X{lv}", tau, f, b, col(Nhi), col(Tm))
                        if Bs and lv == 0:
                            for f in range(2):
                                heads("QK", tau, f, b, col(khT[p]), col(qT[p]))
                        if A and lv == 1:
                            for f in range(2):
                                project("V", tau, f, wv, hT[:, q, :])
                        if C and lv == 2:
                            pe.wait_ge(sem("on"), c + 1)
                            for f in range(2):
                                transposes("OT", tau, f, Ob)
                        if Bs:
                            for f in range(2):
                                pe.wait_ge(read(f"X{lv}"), at(f"X{lv}", b, f))
                                U = "UB" if lv == 0 else f"U{lv - 1}"
                                pe.wait_ge(read(U), at(U, b, f))
                                merged(f"T{lv}", tau, f, Tm, Um, Xm)
                            for f in range(2):
                                merged(f"U{lv}", tau, f, Um, Xm, Um)
                    if Bs:
                        pe.wait_ge(sem("Nlo"), b + 1)
                        for f in range(2):
                            pe.wait_ge(read("T2"), at("T2", b, f))
                            claim(pe, "E", tau, f)
                            o = ps("E", f)
                            mm(o, negid16[:], hh(Tm, f), start=True, stop=False, skip_group_check=True)
                            mm(o, ident16[:], ident4[:].rearrange("p h c -> p (h c)"), start=False, stop=False,
                               skip_group_check=True)
                            for j in range(HH):
                                h = f * HH + j
                                oj = o[:, j * P:j * P + P]
                                mm(oj, col(Nhi)(h), col(Tm)(h), start=False, stop=False, skip_group_check=True)
                                ins = mm(oj, col(Nlo)(h), col(Tm)(h), start=False, stop=(j == HH - 1), skip_group_check=True)
                            ins.then_inc(made("E"), 1)
                    if C:
                        for f in range(2):
                            pe.wait_ge(read("OT"), at("OT", c, f))
                        wait(pe, sem("xp_ready"), c)
                        for h in range(H):
                            ins = mm(AUX[:, 0:P], col(onT)(h), col(wo)(h), start=(h == 0), stop=(h == H - 1))
                        ins.then_inc(sem("att_made"), 1)
                    if Bs:
                        for f in range(2):
                            pe.wait_ge(read("E"), at("E", b, f))
                            pe.wait_ge(read("U2"), at("U2", b, f))
                            heads("C", tau, f, b, col(Em), col(Um))
                run(pe, body)

            @bB.scalar
            def _(act):
                a_ = nc.scalar

                def body(tau, p):
                    A, Bs, C = (live(s, tau) for s in "abc")
                    a, b, c = tau + 1, tau, tau - 1
                    q = 1 - p

                    def take(name, t, f, dst, func=ACT.Copy, scale=1.0):
                        act.wait_ge(made(name), at(name, t, f))
                        a_.activation(hh(dst, f), ps(name, f), func, scale=scale).then_inc(read(name), 1)
                    if Bs:
                        for f in range(2):
                            act.wait_ge(read("G"), at("G", b, f))
                            wait(act, made("E"), at("E", b - 1, 1))
                            wait(act, sem("Nlo"), b)
                            a_.copy(hh(Nhi, f), hh(N32, f)).then_inc(sem("Nhi"), 1)
                    if A:
                        for f in range(2):
                            wait(act, made("KT"), at("KT", a - 1, 1))
                            wait(act, sem("kw"), a)
                            take("K", a, f, kbuf, ACT.Silu)
                    for n in range(BLK - 1):
                        if Bs:
                            act.wait_ge(sem("sub_made"), (BLK - 1) * b + n + 1)
                            a_.copy(Tp[:].rearrange("p h c -> p (h c)"), SUB[:, 0:P]).then_inc(sem("sub"), 1)
                        f = n % 2
                        if C and n < 2:
                            wait(act, made("SU"), at("SU", c - 1, f))
                            take("D", c, f, Db)
                        elif C and n < 4:
                            wait(act, made("OT"), at("OT", c - 1, f))
                            take("PD", c, f, Ob)
                        elif A and 8 <= n < 10:
                            wait(act, made("QT"), at("QT", a - 1, 1))
                            wait(act, sem("qsq"), a)
                            take("Q", a, f, qbuf, ACT.Silu)
                        elif A and 10 <= n < 12:
                            wait(act, made("QS"), at("QS", a - 2, f))
                            take("QT", a, f, qT[q])
                        elif A and 12 <= n < 14:
                            wait(act, made("KS"), at("KS", a - 2, f))
                            take("KT", a, f, khT[q])
                    if C:
                        for f in range(2):
                            wait(act, sem("sgr"), c)
                            take("GT", c, f, gbuf, ACT.Silu)
                    if Bs:
                        for f in range(2):
                            wait(act, made("C"), at("C", b - 1, f))
                            take("UB", b, f, Um)
                    for lv in range(3):
                        if A and lv == 1:
                            for f in range(2):
                                wait(act, read("KS"), at("KS", a - 2, f))
                                take("V", a, f, vbuf[q], ACT.Silu)
                        if C and lv == 2:
                            for f in range(2):
                                wait(act, sem("att_made"), c)
                                take("OT", c, f, onT)
                        if Bs:
                            for f in range(2):
                                take(f"T{lv}", b, f, Tm)
                            for f in range(2):
                                take(f"U{lv}", b, f, Um)
                    if Bs:
                        for f in range(2):
                            wait(act, made("C"), at("C", b - 1, f))
                            take("E", b, f, Em, scale=ESC)
                run(act, body)

            @bB.vector
            def _(dve):
                v = nc.vector

                def body(tau, p):
                    A, Bs, C = (live(s, tau) for s in "abc")
                    a, b, c = tau + 1, tau, tau - 1
                    q = 1 - p
                    if isinstance(tau, int) and tau == -1:
                        v.memset(St, 0.0).then_inc(sem("state0"), 1)
                        v.tensor_copy(ident4[:], bcm(ident16)).then_inc(sem("state0"), 1)
                    if Bs:
                        for f in range(2):
                            dve.wait_ge(made("G"), at("G", b, f))
                            dve.wait_ge(sem("Ebn"), b + 1)
                            v.tensor_tensor(hh(N32, f), ps("G", f), hh(N32, f), ALU.mult).then_inc(read("G"), 1)
                    if C:
                        wait(dve, read("SU"), at("SU", c - 1, 1))
                        v.tensor_copy(cur[:], tab[:, bass.ds(c, 1), :].rearrange("p a k -> p (a k)")).then_inc(sem("cur"), 1)
                        dve.wait_ge(sem("cur"), c + 1)
                        for f in range(2):
                            dve.wait_ge(made("KS"), at("KS", c, f))
                            wait(dve, made("D"), at("D", c - 1, f))
                            dve.wait_ge(read("V"), at("V", c, f))
                            for j in range(HH):
                                h = f * HH + j
                                ins = v.scalar_tensor_tensor(hv(Rb)[:, h, :], ps("KS", f)[:, j * P:j * P + P],
                                                             cur[:, 2 * H + h:2 * H + h + 1], hv(vbuf[q])[:, h, :],
                                                             ALU.mult, ALU.add)
                            ins.then_inc(read("KS"), 1)
                    for n in range(BLK - 1):
                        f = n % 2
                        if A and n == 2:
                            dve.wait_ge(sem("ksq"), a + 1)
                            wait(dve, sem("rk"), a)
                            v.tensor_reduce(ksum[:], hv(sq), AX.X, ALU.add).then_inc(sem("ksum"), 1)
                        elif C and 4 <= n < 6:
                            dve.wait_ge(made("QS"), at("QS", c, f))
                            dve.wait_ge(read("PD"), at("PD", c, f))
                            for j in range(HH):
                                h = f * HH + j
                                ins = v.scalar_tensor_tensor(hv(Ob)[:, h, :], ps("QS", f)[:, j * P:j * P + P],
                                                             cur[:, H + h:H + h + 1], hv(Ob)[:, h, :], ALU.mult, ALU.add)
                            ins.then_inc(read("QS"), 1)
                        elif C and 6 <= n < 8:
                            dve.wait_ge(made("SU"), at("SU", c, f))
                            for j in range(HH):
                                h = f * HH + j
                                ins = v.scalar_tensor_tensor(hv(St)[:, h, :], hv(St)[:, h, :],
                                                             cur[:, 3 * H + h:3 * H + h + 1],
                                                             ps("SU", f)[:, j * P:j * P + P], ALU.mult, ALU.add)
                            ins.then_inc(read("SU"), 1)
                        elif C and n == 12:
                            dve.wait_ge(sem("osq"), c + 1)
                            v.tensor_reduce(osum[:], hv(osq), AX.X, ALU.add).then_inc(sem("osum"), 1)
                        elif A and n == 13:
                            dve.wait_ge(sem("qsq"), a + 1)
                            v.tensor_reduce(qsum[:], hv(sq), AX.X, ALU.add).then_inc(sem("qsum"), 1)
                            dve.wait_ge(sem("qsum"), a + 1)
                            v.tensor_scalar(ssq[:, bass.ds(a, 1), :].rearrange("p a h -> p (a h)"), qsum[:], RMS_EPS, None,
                                            ALU.add).then_inc(sem("ssq_ready"), 1)
                    if Bs:
                        dve.wait_ge(sem("sub"), (BLK - 1) * (b + 1))
                        wait(dve, made("E"), at("E", b - 1, 1))
                        v.tensor_tensor(Tm.rearrange("p (h g c) -> p h g c", h=H, c=BLK),
                                        Tp[:].rearrange("p h (a c) -> p h a c", a=1).broadcast_to([P, H, P // BLK, BLK]),
                                        maskbd[:].rearrange("p (a g c) -> p a g c", a=1, c=BLK).broadcast_to([P, H, P // BLK, BLK]),
                                        ALU.mult).then_inc(sem("Tbd"), 1)
                    for lv in range(3):
                        if Bs:
                            for f in range(2):
                                dve.wait_ge(made(f"X{lv}"), at(f"X{lv}", b, f))
                                if lv == 0:
                                    wait(dve, made("U2"), at("U2", b - 1, f))
                                else:
                                    dve.wait_ge(made(f"U{lv - 1}"), at(f"U{lv - 1}", b, f))
                                v.tensor_tensor(h4(hh(Xm, f)), h4(ps(f"X{lv}", f)), bcm(mask[lv]), ALU.mult
                                                ).then_inc(read(f"X{lv}"), 1)
                        if Bs and lv == 0:
                            for f in range(2):
                                dve.wait_ge(made("QK"), at("QK", b, f))
                                wait(dve, made("PD"), at("PD", b - 2, f))
                                v.tensor_tensor(hh(Pm[p], f), ps("QK", f), hh(Eb, f), ALU.mult).then_inc(read("QK"), 1)
                        if A and lv == 0:
                            dve.wait_ge(sem("bI"), a + 1)
                            dve.wait_ge(sem("al_in"), 16 * a + 16)
                            if Bs:
                                dve.wait_ge(read("QK"), at("QK", b, 1))
                            wait(dve, sem("kw"), a)
                            v.tensor_tensor_scan(Eb, alb[:], bI[:], 0.0, ALU.mult, ALU.add).then_inc(sem("scan"), 1)
                        if C and lv == 1:
                            dve.wait_ge(sem("sgr"), c + 1)
                            dve.wait_ge(read("QS"), at("QS", c, 1))
                            v.tensor_tensor(Ob, Ob, osq, ALU.mult).then_inc(sem("on"), 1)
                    if C:
                        dve.wait_ge(sem("att_made"), c + 1)
                        dve.wait_ge(sem("y_in"), 16 * c + 16)
                        wait(dve, sem("xp_out"), 16 * c)
                        v.tensor_tensor(xpt[:], AUX[:, 0:P], yt[:], ALU.add).then_inc(sem("xp_ready"), 1)
                    if Bs:
                        for f in range(2):
                            dve.wait_ge(made("C"), at("C", b, f))
                            wait(dve, made("D"), at("D", b - 1, f))
                            v.scalar_tensor_tensor(hh(UF, f), ps("C", f), 1.0 / ESC, hh(Um, f), ALU.mult, ALU.add
                                                   ).then_inc(read("C"), 1)
                run(dve, body)

            @bB.gpsimd
            def _(pool):
                g = nc.gpsimd
                bch = lambda cols: cols.rearrange("p (h a) -> p h a", a=1).broadcast_to([P, H, P])

                def body(tau, p):
                    A, Bs, C = (live(s, tau) for s in "abc")
                    a, b, c = tau + 1, tau, tau - 1
                    q = 1 - p
                    if Bs:
                        pool.wait_ge(sem("Nhi"), upto(b, 1))
                        wait(pool, sem("sub_made"), (BLK - 1) * b)
                        g.tensor_tensor(hv(Nbd), hv(Nhi), maskbd[:].rearrange("p (a c) -> p a c", a=1).broadcast_to([P, H, P]),
                                        ALU.mult).then_inc(sem("Nbd"), 1)
                        g.tensor_tensor(Nlo, N32, Nhi, ALU.subtract).then_inc(sem("Nlo"), 1)
                    if A:
                        pool.wait_ge(read("K"), at("K", a, 1))
                        wait(pool, sem("qsum"), a)
                        g.tensor_tensor(sq, kbuf, kbuf, ALU.mult).then_inc(sem("ksq"), 1)
                        wait(pool, sem("scan"), a)
                        wait(pool, sem("Ebn"), a)
                        g.tensor_tensor(hv(bI[:]), ident[:].rearrange("p (a c) -> p a c", a=1).broadcast_to([P, H, P]),
                                        bch(tab[:, bass.ds(a, 1), 0:H].rearrange("p a h -> p (a h)")), ALU.mult
                                        ).then_inc(sem("bI"), 1)
                        pool.wait_ge(sem("ksum"), a + 1)
                        g.tensor_tensor(ksum[:], ksum[:], keps[:], ALU.add).then_inc(sem("kpe"), 1)
                        pool.wait_ge(sem("kpe"), a + 1)
                        g.tensor_tensor(rk[:], ksum[:], mhalf[:, 0:H], ALU.pow).then_inc(sem("rk"), 1)
                        pool.wait_ge(sem("rk"), a + 1)
                        g.tensor_tensor(hv(kbuf), hv(kbuf), bch(rk[:]), ALU.mult).then_inc(sem("kh"), 1)
                    if C:
                        for f in range(2):
                            pool.wait_ge(read("QS"), at("QS", c, f))
                        wait(pool, sem("on"), c)
                        g.tensor_tensor(osq, Ob, Ob, ALU.mult).then_inc(sem("osq"), 1)
                    if A:
                        pool.wait_ge(read("Q"), at("Q", a, 1))
                        pool.wait_ge(sem("ksum"), a + 1)
                        g.tensor_tensor(sq, qbuf, qbuf, ALU.mult).then_inc(sem("qsq"), 1)
                    if C:
                        o = small[:]

                        def step(ins, k):
                            ins.then_inc(sem("r_chain"), 1)
                            pool.wait_ge(sem("r_chain"), 6 * c + k)
                        pool.wait_ge(sem("ssq_ready"), c + 1)
                        step(g.tensor_tensor(o[:, 0, :], ssq[:, bass.ds(c, 1), :].rearrange("p a h -> p (a h)"),
                                             mhalf[:, 0:H], ALU.pow), 1)
                        g.tensor_tensor(o[:, 1, :], o[:, 0, :], krt[:], ALU.mult)
                        step(g.tensor_tensor(o[:, 2, :], o[:, 0, :], kinv[:], ALU.mult), 2)
                        step(g.tensor_tensor(o[:, 2, :], o[:, 2, :], o[:, 2, :], ALU.mult), 3)
                        pool.wait_ge(sem("osum"), c + 1)
                        step(g.tensor_tensor(o[:, 3, :], o[:, 2, :], osum[:], ALU.mult), 4)
                        step(g.tensor_tensor(o[:, 3, :], o[:, 3, :], keps[:], ALU.add), 5)
                        step(g.tensor_tensor(o[:, 4, :], o[:, 3, :], mhalf[:, 0:H], ALU.pow), 6)
                        g.tensor_tensor(o[:, 4, :], o[:, 4, :], o[:, 1, :], ALU.mult).then_inc(sem("r"), 1)
                        pool.wait_ge(sem("r"), c + 1)
                        pool.wait_ge(read("GT"), at("GT", c, 1))
                        g.tensor_tensor(hv(osq), hv(gbuf), bch(o[:, 4, :]), ALU.mult).then_inc(sem("sgr"), 1)
                    if A:
                        pool.wait_ge(sem("scan"), a + 1)
                        g.tensor_tensor(N32, bI[:], Eb, ALU.subtract).then_inc(sem("Ebn"), 1)
                        wait(pool, made("SU"), at("SU", a - 2, 1))
                        pool.wait_ge(sem("kh"), a + 1)
                        g.tensor_tensor(hv(kw[q]), hv(kbuf), hv(Eb)[:, :, P - 1:P].broadcast_to([P, H, P]), ALU.mult
                                        ).then_inc(sem("kw"), 1)
                run(pool, body)

        end_program()

        def groups(eng, body, lag):
            first = lag + 2 - lag % 2
            last = NG - 2 + NG % 2
            for g in range(first):
                body(g, g % 2)
            with eng.Fori(first, last - 1, 2) as g0:
                body(g0, 0)
                body(g0 + 1, 1)
            for g in range(last, NG + lag):
                body(g, g % 2)

        def within(g):
            return not isinstance(g, int) or 0 <= g < NG

        GW = GRP * P
        t4 = lambda a: a.rearrange("p (t d) -> p t d", t=GRP)
        gsl = lambda d, g: d[bass.ds(g * GRP, GRP)].rearrange("t p d -> p t d")
        with ExitStack() as c3:
            off3 = [0]

            def cutt(n):
                off3[0] += n
                assert off3[0] <= W_ARENA
                return arena[:, off3[0] - n:off3[0]]
            xg, xpg = ([cutt(GW) for _ in range(2)] for _ in range(2))
            xsg = [cutt(GW) for _ in range(2)]
            x1g, tTg = ([cutt(GW) for _ in range(2)] for _ in range(2))
            sqg, mg, mTg, tg = (cutt(GW) for _ in range(4))
            h1, h2 = cutt(NF * GW), cutt(NF * GW)
            wfc = cutt(DFF)
            wpj = cutt(NF * P).rearrange("p (j n) -> p j n", j=NF)
            gwT = cutt(NE)
            smalls = lambda: [cutt(GRP) for _ in range(2)]
            ms, rx = smalls(), smalls()
            mean, var, rt = smalls(), smalls(), smalls()
            msum, vsum, mdif = cutt(GRP), cutt(GRP), cutt(GRP)
            st3 = cutt(GRP * 6).rearrange("p (t s) -> p t s", s=6)
            gws = cutt(P)
            lg = cutt(T * NE).rearrange("p (t e) -> p t e", e=NE)
            bcd = lambda a: a.rearrange("p (t a) -> p t a", a=1).broadcast_to([P, GRP, P])
            b3 = c3.enter_context(nc.Block())


            @b3.sync
            def _(sp):
                sp.dma_start(wfc, W_fc).then_inc(sem("m_w"), 16)
                sp.dma_start(wpj, W_proj.rearrange("(j p) n -> p j n", p=P)).then_inc(sem("m_w"), 16)
                sp.dma_start(gws[0:NE, :], gate_w).then_inc(sem("m_w"), 16)

                def body(g, k):
                    if within(g):
                        wait(sp, sem("xs_sum"), g - 1)
                        sp.dma_start(t4(xg[k]), x_t[bass.ds(g * GW, GW), :].rearrange("(t p) d -> p t d", p=P)
                                     ).then_inc(sem(f"m_in{k}"), 16)
                        sp.dma_start(t4(xpg[k]), gsl(xp_d, g)).then_inc(sem(f"m_in{k}"), 16)
                    if within(g - 4):
                        sp.wait_ge(sem("m_x1"), g - 3)
                        sp.dma_start(gsl(x1_d, g - 4), t4(x1g[k])).then_inc(sem(f"x1_out{k}"), 16)
                    if within(g - 5):
                        sp.wait_ge(sem("m_tT"), g - 4)
                        sp.dma_start(gsl(tT_d, g - 5), t4(tTg[1 - k])).then_inc(sem(f"tT_out{1 - k}"), 16)
                groups(sp, body, 5)
                for n in ("x1_out0", "x1_out1", "tT_out0", "tT_out1"):
                    sp.wait_ge(sem(n), 8 * NG)

            @b3.gpsimd
            def _(pool):
                g_ = nc.gpsimd

                def body(g, k):
                    if within(g):
                        pool.wait_ge(sem(f"m_in{k}"), 16 * (g - k) + 32)
                        wait(pool, sem("m_ssum"), g)
                        g_.tensor_tensor(sqg, xpg[k], xpg[k], ALU.mult).then_inc(sem("m_sq"), 1)
                        pool.wait_ge(sem("m_ms"), g + 1)
                        wait(pool, sem("m_m"), g - 1)
                        g_.tensor_tensor(rx[k], ms[k], mhalf[:, 0:GRP], ALU.pow).then_inc(sem("m_r"), 1)
                    if within(g - 3):
                        pool.wait_ge(sem("m_var"), g - 2)
                        wait(pool, sem("m_t"), g - 4)
                        g_.tensor_tensor(rt[1 - k], var[1 - k], mhalf[:, 0:GRP], ALU.pow).then_inc(sem("m_r3"), 1)
                groups(pool, body, 5)

            @b3.vector
            def _(dve):
                v = nc.vector

                def body(g, k):
                    if within(g - 1):
                        dve.wait_ge(sem("m_r"), g)
                        wait(dve, sem("m_mTp"), g - 1)
                        v.tensor_tensor(t4(mg), t4(xpg[1 - k]), bcd(rx[1 - k]), ALU.mult).then_inc(sem("m_m"), 1)
                    if within(g - 4):
                        dve.wait_ge(sem("m_r3"), g - 3)
                        wait(dve, sem("m_tTp"), g - 4)
                        for j in range(GRP):
                            ins = v.tensor_scalar(tg[:, j * P:j * P + P], x1g[k][:, j * P:j * P + P], mean[k][:, j:j + 1],
                                                  rt[k][:, j:j + 1], ALU.subtract, ALU.mult)
                        ins.then_inc(sem("m_t"), 1)
                    if within(g - 5):
                        dve.wait_ge(sem("m_lgp"), g - 4)
                        v.tensor_copy(lg[:, bass.ds((g - 5) * GRP, GRP), :].rearrange("p t e -> p (t e)"),
                                      bank[7][:, 0:GRP * NE]).then_inc(sem("m_lg"), 1)
                    if within(g):
                        dve.wait_ge(sem("m_sq"), g + 1)
                        wait(dve, sem("m_r"), g - 1)
                        v.tensor_reduce(ms[k], t4(sqg), AX.X, ALU.add).then_inc(sem("m_ssum"), 1)
                        dve.wait_ge(sem("m_ssum"), g + 1)
                        v.tensor_scalar(ms[k], ms[k], 1.0 / D, RMS_EPS, ALU.mult, ALU.add).then_inc(sem("m_ms"), 1)
                    if within(g - 3):
                        c, kc = g - 3, 1 - k

                        def link(ins, i):
                            ins.then_inc(sem("m_v"), 1)
                            dve.wait_ge(sem("m_v"), 4 * c + i)
                        dve.wait_ge(sem("m_pj"), c + 1)
                        wait(dve, sem(f"x1_out{kc}"), 8 * (c - kc))
                        dve.wait_ge(sem("xs_sum"), c + 1)
                        v.tensor_tensor(x1g[kc], xsg[kc], bank[6][:, :], ALU.add).then_inc(sem("m_x1"), 1)
                        dve.wait_ge(sem("m_x1"), c + 1)
                        for j in range(GRP):
                            ins = v.bn_stats(st3[:, j, :], x1g[kc][:, j * P:j * P + P])
                        link(ins, 1)
                        v.tensor_tensor(msum, st3[:, :, 1], st3[:, :, 4], ALU.add)
                        v.tensor_tensor(vsum, st3[:, :, 2], st3[:, :, 5], ALU.add)
                        link(v.tensor_tensor(mdif, st3[:, :, 1], st3[:, :, 4], ALU.subtract), 2)
                        v.tensor_scalar(mean[kc], msum, 0.5, None, ALU.mult)
                        link(v.scalar_tensor_tensor(mdif, mdif, 0.25, mdif, ALU.mult, ALU.mult), 3)
                        link(v.scalar_tensor_tensor(var[kc], vsum, 1.0 / D, mdif, ALU.mult, ALU.add), 4)
                        v.tensor_scalar(var[kc], var[kc], LN_EPS, None, ALU.add).then_inc(sem("m_var"), 1)
                    if within(g - 1):
                        v.tensor_tensor(xsg[1 - k], xg[1 - k], xpg[1 - k], ALU.add).then_inc(sem("xs_sum"), 1)
                groups(dve, body, 5)

            @b3.scalar
            def _(act):
                a_ = nc.scalar
                act.wait_ge(sem("m_gwp"), 1)
                a_.copy(gwT, bank[7][:, 0:NE]).then_inc(sem("m_gwT"), 1)

                def body(g, k):
                    if within(g - 2):
                        def square(j):
                            act.wait_ge(sem("m_relu"), NF * (g - 2) + j + 1)
                            if j == 0:
                                wait(act, sem("m_pj"), g - 2)
                            cols = slice(j * GW, (j + 1) * GW)
                            a_.activation(h2[:, cols], h1[:, cols], ACT.Square).then_inc(sem("m_h2"), 1)
                        for j in range(NF):
                            act.wait_ge(sem("m_fc"), NF * (g - 2) + j + 1)
                            a_.activation(h1[:, j * GW:(j + 1) * GW], bank[1 + j][:, :], ACT.Relu).then_inc(sem("m_relu"), 1)
                            if j > 0:
                                square(j - 1)
                        square(NF - 1)
                    if within(g - 1):
                        act.wait_ge(sem("m_mTp"), g)
                        wait(act, sem("m_fc"), NF * (g - 1))
                        a_.copy(mTg, bank[0][:, :]).then_inc(sem("m_mT"), 1)
                    if within(g - 4):
                        act.wait_ge(sem("m_tTp"), g - 3)
                        wait(act, sem(f"tT_out{k}"), 8 * (g - 4 - k))
                        wait(act, sem("m_lgp"), g - 5)
                        a_.copy(tTg[k], bank[5][:, :]).then_inc(sem("m_tT"), 1)
                groups(act, body, 5)

            @b3.tensor
            def _(pe):
                mm = nc.tensor.matmul
                pe.wait_ge(sem("m_w"), 48)
                nc.tensor.transpose(bank[7][:, 0:NE], gws[0:NE, :], ident[0:NE, 0:NE]).then_inc(sem("m_gwp"), 1)
                pe.wait_ge(sem("m_gwT"), 1)

                def body(g, k):
                    if within(g - 5):
                        pe.wait_ge(sem("m_tT"), g - 4)
                        wait(pe, sem("m_lg"), g - 5)
                        for j in range(GRP):
                            ins = mm(bank[7][:, j * NE:(j + 1) * NE], tTg[1 - k][:, j * P:j * P + P], gwT,
                                     start=(j == 0), stop=(j == GRP - 1), skip_group_check=True)
                        ins.then_inc(sem("m_lgp"), 1)
                    if within(g - 3):
                        pe.wait_ge(sem("m_h2"), NF * (g - 2))
                        wait(pe, sem("m_x1"), g - 3)
                        for t in range(GRP):
                            for j in range(NF):
                                ins = mm(bank[6][:, t * P:t * P + P], h2[:, j * GW + t * P:j * GW + (t + 1) * P], wpj[:, j, :],
                                         start=(j == 0), stop=(j == NF - 1))
                        ins.then_inc(sem("m_pj"), 1)
                    if within(g - 2):
                        pe.wait_ge(sem("m_mT"), g - 1)
                        for j in range(NF):
                            wait(pe, sem("m_relu"), NF * (g - 3) + j + 1)
                            mm(bank[1 + j][:, :], wfc[:, j * P:j * P + P], mTg, start=True, stop=True).then_inc(sem("m_fc"), 1)
                    if within(g - 1):
                        pe.wait_ge(sem("m_m"), g)
                        wait(pe, sem("m_mT"), g - 1)
                        for j in range(GRP):
                            ins = nc.tensor.transpose(bank[0][:, j * P:j * P + P], mg[:, j * P:j * P + P], ident[:])
                        ins.then_inc(sem("m_mTp"), 1)
                    if within(g - 4):
                        pe.wait_ge(sem("m_t"), g - 3)
                        wait(pe, sem("m_tT"), g - 4)
                        for j in range(GRP):
                            ins = nc.tensor.transpose(bank[5][:, j * P:j * P + P], tg[:, j * P:j * P + P], ident[:])
                        ins.then_inc(sem("m_tTp"), 1)
                groups(pe, body, 5)

        end_program()

        with ExitStack() as c4:
            lgoff = off3[0] - T * NE
            lgf = arena[:, lgoff:lgoff + T * NE]
            off4 = [lgoff + T * NE]

            def cute(n):
                off4[0] += n
                assert off4[0] <= W_ARENA
                return arena[:, off4[0] - n:off4[0]]
            c8 = lambda a: a.rearrange("p (t e) -> p t e", e=NE)
            pr, wt, sc, oh1, oh2, io = (cute(T * NE) for _ in range(6))
            red = cute(T)
            bce = lambda a: a.rearrange("p (t a) -> p t a", a=1).broadcast_to([P, T, NE])
            off4[0] = 0
            EW = NE * P
            ews, ewT = cute(EW), cute(EW)
            cws, cwT = cute(P), cute(P)
            act_o = [cute(EW) for _ in range(2)]
            wtd = [cute(EW) for _ in range(2)]
            mix4 = [cute(GW) for _ in range(2)]
            mixT = cute(GW)
            tT4 = [cute(GW) for _ in range(2)]
            x14 = [cute(GW) for _ in range(2)]
            ot4 = [cute(GW) for _ in range(2)]
            brow = arena[:, off4[0] - EW:off4[0]]
            assert off4[0] <= lgoff
            HE = NE // 2
            BF = mybir.dt.bfloat16
            R1, R2 = 64, 96
            bpart = c4.enter_context(nc.sbuf_tensor("bpart", [P, EW], BF))
            pick = c4.enter_context(nc.sbuf_tensor("pick", [P, P], BF))
            bE = c4.enter_context(nc.Block())

            @bE.sync
            def _(sp):
                sp.dma_start(ews.rearrange("p (e h) -> p e h", e=NE), expert_w.rearrange("e d h -> d e h")).then_inc(sem("e_w"), 16)
                sp.dma_start(cws, combine_w).then_inc(sem("e_w"), 16)
                sp.dma_start(brow[0:R2 + 1, :], expert_b.rearrange("(a e) d -> a (e d)", a=1).broadcast_to([R2 + 1, EW])
                             ).then_inc(sem("e_w"), 16)

                def body(g, k):
                    if within(g):
                        wait(sp, sem("e_hp"), 2 * GRP * (g - 1))
                        sp.dma_start(t4(tT4[k]), gsl(tT_d, g)).then_inc(sem(f"e_tT{k}"), 16)
                    wait(sp, sem("e_ot"), g - 1)
                    if within(g):
                        sp.dma_start(t4(x14[k]), gsl(x1_d, g)).then_inc(sem(f"e_x1{k}"), 16)
                    if within(g - 2):
                        sp.dma_start(out_t[bass.ds((g - 2) * GW, GW), :].rearrange("(t p) d -> p t d", p=P), t4(ot4[k])
                                     ).then_inc(sem(f"o_out{k}"), 16)
                groups(sp, body, 2)
                for n in ("o_out0", "o_out1"):
                    sp.wait_ge(sem(n), 8 * NG)

            @bE.gpsimd
            def _(pool):
                g_ = nc.gpsimd
                g_.memset(pick[:], 0.0).then_inc(sem("e_one"), 1)
                pool.wait_ge(sem("e_one"), 1)
                for i, r in enumerate((0, R1, R2)):
                    g_.memset(pick[r:r + 1, :], 1.0).then_inc(sem("e_one"), 1)
                    pool.wait_ge(sem("e_one"), i + 2)
                for e in range(NE):
                    ins = g_.memset(c8(io)[:, :, e:e + 1], float(NE - e))
                ins.then_inc(sem("e_io"), 1)
                pool.wait_ge(sem("e_wt"), 1)

                def body(g, k):
                    for j in range(GRP):
                        t = g * GRP + j
                        pool.wait_ge(sem("e_act"), t * 2 + 2)
                        wait(pool, sem("e_mix"), t - 1)
                        g_.tensor_tensor(wtd[j % 2].rearrange("p (e d) -> p e d", e=NE),
                                         act_o[j % 2].rearrange("p (e d) -> p e d", e=NE),
                                         c8(wt)[:, bass.ds(t, 1), :].rearrange("p a (e o) -> p (a e) o", o=1)
                                         .broadcast_to([P, NE, P]), ALU.mult).then_inc(sem("e_wtd"), 1)
                groups(pool, body, 0)

            @bE.vector
            def _(dve):
                v = nc.vector
                cnt = [0]

                def link(ins):
                    cnt[0] += 1
                    ins.then_inc(sem("e_v"), 1)
                    dve.wait_ge(sem("e_v"), cnt[0])
                dve.wait_ge(sem("e_w"), 48)
                for r in (0, R1, R2):
                    if r:
                        link(v.tensor_tensor(brow[r:R2 + 1, :], brow[r:R2 + 1, :], bpart[r:R2 + 1, :], ALU.subtract))
                    with nc.allow_low_precision("exact parts"):
                        link(v.tensor_copy(bpart[r:R2 + 1, :], brow[r:R2 + 1, :]))
                v.memset(red, 0.0).then_inc(sem("e_bias"), 1)
                dve.wait_ge(sem("e_bias"), 1)
                link(v.tensor_reduce(red, c8(lgf), AX.X, ALU.max))
                v.tensor_tensor(c8(pr), c8(lgf), bce(red), ALU.subtract).then_inc(sem("e_sh"), 1)
                dve.wait_ge(sem("e_ex"), 1)
                link(v.tensor_reduce(red, c8(pr), AX.X, ALU.add))
                link(v.reciprocal(red, red))
                link(v.tensor_tensor(c8(pr), c8(pr), bce(red), ALU.mult))
                dve.wait_ge(sem("e_io"), 1)
                link(v.tensor_copy(wt, pr))
                for oh in (oh1, oh2):
                    link(v.tensor_reduce(red, c8(wt), AX.X, ALU.max))
                    link(v.tensor_tensor(c8(sc), c8(wt), bce(red), ALU.is_equal))
                    link(v.tensor_tensor(sc, sc, io, ALU.mult))
                    link(v.tensor_reduce(red, c8(sc), AX.X, ALU.max))
                    link(v.tensor_tensor(c8(oh), c8(sc), bce(red), ALU.is_equal))
                    link(v.scalar_tensor_tensor(wt, oh, -2.0, wt, ALU.mult, ALU.add))
                link(v.tensor_tensor(oh1, oh1, oh2, ALU.add))
                v.tensor_tensor(wt, oh1, pr, ALU.mult).then_inc(sem("e_wt"), 1)

                def body(g, k):
                    if within(g):
                        for j in range(GRP):
                            t = g * GRP + j
                            dve.wait_ge(sem("e_wtd"), t + 1)
                            if j == 0:
                                wait(dve, sem("e_mTp"), g - 1)
                            v.tensor_reduce(mix4[k][:, j * P:j * P + P], wtd[j % 2].rearrange("p (e d) -> p d e", e=NE),
                                            AX.X, ALU.add).then_inc(sem("e_mix"), 1)
                            if j == 2 and within(g - 1):
                                c, kc = g - 1, 1 - k
                                dve.wait_ge(sem("e_op"), c + 1)
                                dve.wait_ge(sem(f"e_x1{kc}"), 8 * (c - kc) + 16)
                                wait(dve, sem(f"o_out{kc}"), 8 * (c - kc))
                                v.tensor_tensor(ot4[kc], bank[6][:, :], x14[kc], ALU.add).then_inc(sem("e_ot"), 1)
                    elif within(g - 1):
                        c, kc = g - 1, 1 - k
                        dve.wait_ge(sem("e_op"), c + 1)
                        dve.wait_ge(sem(f"e_x1{kc}"), 8 * (c - kc) + 16)
                        wait(dve, sem(f"o_out{kc}"), 8 * (c - kc))
                        v.tensor_tensor(ot4[kc], bank[6][:, :], x14[kc], ALU.add).then_inc(sem("e_ot"), 1)
                groups(dve, body, 1)

            @bE.scalar
            def _(act):
                a_ = nc.scalar
                act.wait_ge(sem("e_sh"), 1)
                a_.activation(pr, pr, ACT.Exp).then_inc(sem("e_ex"), 1)
                for f in range(2):
                    act.wait_ge(sem("e_wp"), f + 1)
                    a_.copy(hh(ewT, f), bank[f][:, :]).then_inc(sem("e_wT"), 1)
                act.wait_ge(sem("e_wp"), 3)
                a_.copy(cwT, bank[2][:, 0:P]).then_inc(sem("e_wT"), 1)

                def body(g, k):
                    if within(g):
                        for j in range(GRP):
                            t = g * GRP + j
                            wait(act, sem("e_wtd"), t - 1)
                            for f in range(2):
                                act.wait_ge(sem("e_hp"), 2 * t + f + 1)
                                a_.activation(hh(act_o[j % 2], f), bank[2 * (j % 2) + f][:, :], ACT.Silu).then_inc(sem("e_act"), 1)
                            if j == 2 and within(g - 1):
                                act.wait_ge(sem("e_mTp"), g)
                                wait(act, sem("e_op"), g - 1)
                                a_.copy(mixT, bank[5][:, :]).then_inc(sem("e_mT"), 1)
                    elif within(g - 1):
                        act.wait_ge(sem("e_mTp"), g)
                        wait(act, sem("e_op"), g - 1)
                        a_.copy(mixT, bank[5][:, :]).then_inc(sem("e_mT"), 1)
                groups(act, body, 1)

            @bE.tensor
            def _(pe):
                mm = nc.tensor.matmul
                pe.wait_ge(sem("e_w"), 48)
                for f in range(2):
                    for j in range(HE):
                        e = f * HE + j
                        ins = nc.tensor.transpose(bank[f][:, j * P:j * P + P], ews[:, e * P:e * P + P], ident[:])
                    ins.then_inc(sem("e_wp"), 1)
                nc.tensor.transpose(bank[2][:, 0:P], cws, ident[:]).then_inc(sem("e_wp"), 1)
                pe.wait_ge(sem("e_wT"), 3)
                pe.wait_ge(sem("e_bias"), 1)
                pe.wait_ge(sem("e_one"), 4)

                def mixed(c, kc):
                    pe.wait_ge(sem("e_mix"), GRP * c + GRP)
                    wait(pe, sem("e_mT"), c)
                    for j in range(GRP):
                        ins = nc.tensor.transpose(bank[5][:, j * P:j * P + P], mix4[kc][:, j * P:j * P + P], ident[:])
                    ins.then_inc(sem("e_mTp"), 1)

                def combine(c):
                    pe.wait_ge(sem("e_mT"), c + 1)
                    wait(pe, sem("e_ot"), c)
                    for j in range(GRP):
                        ins = mm(bank[6][:, j * P:j * P + P], mixT[:, j * P:j * P + P], cwT, start=(j == 0), stop=(j == GRP - 1),
                                 skip_group_check=True)
                    ins.then_inc(sem("e_op"), 1)

                def body(g, k):
                    if within(g):
                        pe.wait_ge(sem(f"e_tT{k}"), 8 * (g - k) + 16)
                        for j in range(GRP):
                            t = g * GRP + j
                            for f in range(2):
                                wait(pe, sem("e_act"), 2 * (t - 2) + f + 1)
                                o = bank[2 * (j % 2) + f][:, :]
                                mm(o, tT4[k][:, j * P:j * P + P], hh(ewT, f), start=True, stop=False)
                                mm(o, pick[0:R2 + 1, :], hh(bpart, f)[0:R2 + 1, :], start=False, stop=True).then_inc(sem("e_hp"), 1)
                            if j == 2 and within(g - 1):
                                mixed(g - 1, 1 - k)
                            if j == 3 and within(g - 1):
                                combine(g - 1)
                    elif within(g - 1):
                        mixed(g - 1, 1 - k)
                        combine(g - 1)
                groups(pe, body, 1)

        end_program()


_INS = ["L0_attn_x", "L0_attn_Wq", "L0_attn_Wk", "L0_attn_Wv", "L0_attn_Wb", "L0_attn_Wa", "L0_attn_A_log",
        "L0_attn_dt_bias", "L0_attn_Wg", "L0_attn_o_norm_w", "L0_attn_Wo", "L0_attn_W_fc", "L0_attn_W_proj",
        "L0_ffn_gate_w", "L0_ffn_expert_w", "L0_ffn_expert_b", "L0_ffn_combine_w"]


def kernel(**inputs):
    import numpy as _np
    import concourse.bacc as _bacc
    from concourse.bass_utils import run_bass_kernel_spmd as _run

    nc = _bacc.Bacc("TRN2", target_bir_lowering=False, num_devices=1)
    arrays, args = {}, []
    for name in _INS:
        a = _np.ascontiguousarray(inputs[name])
        arrays[f"in_{name}"] = a
        args.append(nc.dram_tensor(f"in_{name}", a.shape, mybir.dt.from_np(a.dtype), kind="ExternalInput").ap())
    shape = arrays["in_L0_attn_x"].shape
    args.append(nc.dram_tensor("out_0", shape, F32, kind="ExternalOutput").ap())
    tiles = shape[0] * shape[1] // P
    dram = {k: nc.dram_tensor(f"scratch_{k}", s, F32, kind="Internal").ap() for k, s in (
        ("y", (tiles, P, P)), ("hT", (tiles, P, P)), ("xp", (tiles, P, P)), ("x1", (tiles, P, P)),
        ("tT", (tiles, P, P)), ("al", (tiles * H, P)), ("ce", (tiles * H,)))}
    delta_moe(nc, *args, dram)
    r = _run(nc, [arrays], core_ids=[0])
    return r.results[0]["out_0"]
```

```python
from contextlib import ExitStack

import concourse.bass as bass
from concourse import mybir

ALU = mybir.AluOpType
ACT = mybir.ActivationFunctionType
AX = mybir.AxisListType
F32 = mybir.dt.float32
F16 = mybir.dt.float16
F32R = mybir.dt.float32r

P = 128
H = 8
HD = H * P
BANK = 512
HH = H // 2
GRP = 4
BLK = 8
NLV = 4
ESC = 1024.0
LN_EPS, RMS_EPS = 1e-5, 1e-6

PAIR_USES = [("G", "b"), ("C", "c"), ("KS", "c"), ("K", "a"), ("D", "c"), ("PD", "c"), ("QS", "c"), ("SU", "c"),
             ("Q", "a"), ("UB", "b"), ("X0", "b"), ("KT", "a"), ("T0", "b"), ("U0", "b"), ("V", "a"), ("X1", "b"),
             ("T1", "b"), ("U1", "b"), ("QT", "a"), ("X2", "b"), ("QK", "b"), ("T2", "b"), ("U2", "b"), ("GT", "a"),
             ("X3", "b"), ("T3", "b"), ("OT", "c"), ("U3", "b"), ("E", "b")]
PAIR = {name: k % 3 for k, (name, _) in enumerate(PAIR_USES)}


def upto(t, half):
    return 2 * t + half + 1


def wait(eng, sem, value):
    if not isinstance(value, int) or value > 0:
        eng.wait_ge(sem, value)


def delta_moe(nc, x, Wq, Wk, Wv, Wb, Wa, A_log, dt_bias, Wg, o_norm_w, Wo, W_fc, W_proj,
              gate_w, expert_w, expert_b, combine_w, out, dram):
    B, S_LEN, D = x.shape
    T = B * S_LEN // P
    CH = S_LEN // P
    NG = T // GRP
    DFF = W_fc.shape[1]
    NF = DFF // P
    NE = gate_w.shape[0]
    TH = T * H
    NR = TH // P
    x_t = x.rearrange("b s d -> (b s) d")
    out_t = out.rearrange("b s d -> (b s) d")
    hT_d, xp_d, al_d, x1_d, tT_d = (dram[k] for k in ("hT", "xp", "al", "x1", "tT"))

    with ExitStack() as ctx:
        def sb(name, shape, dt=F32):
            return ctx.enter_context(nc.sbuf_tensor(name, shape, dt))

        sems = {}

        def sem(name):
            if name not in sems:
                sems[name] = nc.alloc_semaphore(name=name)
            return sems[name]

        def end_program():
            nc.clear_and_free_semaphores(list(sems.values()))
            sems.clear()
            nc.all_engine_barrier()

        bank = [ctx.enter_context(nc.psum_tensor(f"bank{i}", [P, BANK], F32)) for i in range(8)]

        def groups(eng, body, lag, n):
            first = lag + 2 - lag % 2
            last = n - 2 + n % 2
            for g in range(first):
                body(g, g % 2)
            with eng.Fori(first, last - 1, 2) as g0:
                body(g0, 0)
                body(g0 + 1, 1)
            for g in range(last, n + lag):
                body(g, g % 2)

        def inside(g, n):
            return not isinstance(g, int) or 0 <= g < n

        ident = sb("ident", [P, P])
        ident16 = sb("ident16", [P, P], F16)
        negid16 = sb("negid16", [P, P], F16)
        mhalf = sb("mhalf", [P, 64])
        keps, krt, kinv = (sb(n, [P, H]) for n in ("keps", "krt", "kinv"))
        mask = [sb(f"mask{i}", [P, P], F16) for i in range(NLV)]
        maskbd = sb("maskbd", [P, P], F16)
        identp = sb("identp", [P, BLK], F16)
        identp8 = sb("identp8", [P, H, BLK], F16)
        wh, wl = ([sb(f"{part}_{n}", [P, HD], F32R) for n in ("wq", "wk", "wv", "wg")] for part in ("high", "low"))
        wo = sb("wo", [P, HD])
        onw = sb("onw", [P, 1])
        tab = sb("tab", [P, T, 4 * H + 2])
        W_ARENA = 30 * HD
        arena = sb("arena", [P, W_ARENA])

        with ExitStack() as c1:
            bA = c1.enter_context(nc.Block())
            xs = arena[:, 0:T * P].rearrange("p (t d) -> p t d", t=T)
            off = [T * P]

            def cut(n):
                off[0] += n
                assert off[0] <= W_ARENA
                return arena[:, off[0] - n:off[0]]
            NSTEP = T // (2 * GRP)
            ST = 2 * GRP
            hst = cut(2 * BANK).rearrange("p (f j d) -> p f j d", f=2, j=GRP)
            hTs = [cut(2 * BANK).rearrange("p (f n) -> p f n", f=2) for _ in range(2)]
            st = cut(ST * 6).rearrange("p (t s) -> p t s", s=6)
            msum, mdif, vsum, var, rv = (cut(ST) for _ in range(5))
            vv, rr = ([cut(2 * ST) for _ in range(2)] for _ in range(2))
            r12, mean8 = cut(ST), [cut(ST) for _ in range(2)]
            wab = cut(2 * H)
            alog, dtb = cut(H), cut(H)
            z = cut(T * 2 * H).rearrange("p (t k) -> p t k", k=2 * H)
            za, nz, ez, den, sser, s2, pol, al = (cut(TH) for _ in range(8))
            eb = cut(TH)
            ctab = cut(TH)
            arow = cut(TH).rearrange("p (r i) -> p r i", i=P)
            crow = cut(TH).rearrange("p (r i) -> p r i", i=P)
            zrow = cut(P)
            wraw = [cut(HD) for _ in range(4)]
            rmask = cut(1)
            v3 = lambda a: a.rearrange("p (t h) -> p t h", h=H)

            @bA.sync
            def _(sp):
                def body(s, k):
                    wait(sp, sem("stats"), s - 1)
                    sp.dma_start(xs[:, bass.ds(s * ST, ST), :],
                                 x_t[bass.ds(s * ST * P, ST * P), :].rearrange("(t p) d -> p t d", p=P)).then_inc(sem(f"x_in{k}"), 16)
                groups(sp, body, 0, NSTEP)
                for dst, src in zip(wraw, (Wq, Wk, Wv, Wg)):
                    sp.dma_start(dst, src).then_inc(sem("w_in"), 16)
                sp.dma_start(wo[:].rearrange("p (h n) -> p h n", h=H),
                             Wo.rearrange("(h p) n -> p h n", p=P)).then_inc(sem("w_in"), 16)
                sp.wait_ge(sem("arow_ready"), 1)
                sp.dma_start(al_d.rearrange("(r p) i -> p r i", p=P), arow).then_inc(sem("al_out"), 16)
                for name, v in (("al_out", 16), ("w_in", 80)):
                    sp.wait_ge(sem(name), v)

            @bA.gpsimd
            def _(pool):
                pool.dma_start(wab[:, 0:H], Wa).then_inc(sem("small_in"), 16)
                pool.dma_start(wab[:, H:2 * H], Wb).then_inc(sem("small_in"), 16)
                pool.dma_start(alog, A_log.rearrange("(a n) -> a n", a=1).broadcast_to([P, H])).then_inc(sem("small_in"), 16)
                pool.dma_start(dtb, dt_bias.rearrange("(a n) -> a n", a=1).broadcast_to([P, H])).then_inc(sem("small_in"), 16)
                pool.dma_start(onw[:], o_norm_w.rearrange("(p a) -> p a", a=1)).then_inc(sem("small_in"), 16)
                n = 0
                g = nc.gpsimd

                def step(ins):
                    nonlocal n
                    n += 1
                    ins.then_inc(sem("const"), 1)
                    pool.wait_ge(sem("const"), n)
                step(g.memset(mhalf[:], -0.5))
                step(g.memset(ident[:], 0.0))
                g.affine_select(out=ident[:], in_=ident[:], compare_op=ALU.not_equal, fill=1.0, base=0,
                                pattern=[[-1, P]], channel_multiplier=1).then_inc(sem("ident_made"), 1)
                pool.wait_ge(sem("ident_made"), 1)

                def body(s, k):
                    pool.wait_ge(sem("var_ready"), s + 1)
                    wait(pool, sem("r12"), s - 1)
                    g.tensor_tensor(rr[k], vv[k], mhalf[:, 0:2 * ST], ALU.pow).then_inc(sem("r_ready"), 1)
                groups(pool, body, 0, NSTEP)
                step(g.memset(ident16[:], 0.0))
                step(g.memset(negid16[:], 0.0))
                step(g.memset(keps[:], RMS_EPS))
                step(g.memset(krt[:], float(P) ** -0.5))
                step(g.memset(kinv[:], 1.0 / P))
                step(g.memset(maskbd[:], 1.0))
                for m in mask:
                    step(g.memset(m[:], 0.0))
                step(g.memset(zrow, 0.0))
                step(g.memset(rmask, 1.0))
                for m, v in ((ident16, 1.0), (negid16, -1.0)):
                    step(g.affine_select(out=m[:], in_=m[:], compare_op=ALU.not_equal, fill=v, base=0,
                                         pattern=[[-1, P]], channel_multiplier=1))
                for r in range(0, P // H, CH):
                    step(g.memset(rmask[r * H:r * H + H, :], 0.0))
                mb = maskbd[:].rearrange("p (g c) -> p g c", c=BLK)
                step(g.affine_select(out=mb, in_=mb, compare_op=ALU.is_ge, fill=0.0, base=0,
                                     pattern=[[-BLK, P // BLK], [0, BLK]], channel_multiplier=1))
                step(g.affine_select(out=mb, in_=mb, compare_op=ALU.is_ge, fill=0.0, base=BLK - 1,
                                     pattern=[[BLK, P // BLK], [0, BLK]], channel_multiplier=-1))
                for i, m in enumerate(mask):
                    s = BLK << i
                    half = m[:].rearrange("p (g c) -> p g c", c=2 * s)[:, :, 0:s]
                    step(g.memset(half, 1.0))
                for i, m in enumerate(mask):
                    s = BLK << i
                    half = m[:].rearrange("p (g c) -> p g c", c=2 * s)[:, :, 0:s]
                    step(g.affine_select(out=half, in_=half, compare_op=ALU.is_ge, fill=0.0, base=-s,
                                         pattern=[[-2 * s, P // (2 * s)], [0, s]], channel_multiplier=1))
                for i, m in enumerate(mask):
                    s = BLK << i
                    half = m[:].rearrange("p (g c) -> p g c", c=2 * s)[:, :, 0:s]
                    step(g.affine_select(out=half, in_=half, compare_op=ALU.is_ge, fill=0.0, base=2 * s - 1,
                                         pattern=[[2 * s, P // (2 * s)], [0, s]], channel_multiplier=-1))
                g.memset(zrow[0:1, 0:1], 0.0).then_inc(sem("const_all"), 1)
                for i in range(4):
                    pool.wait_ge(sem("w_high"), i + 1)
                    g.tensor_tensor(wl[i][:], wraw[i], wh[i][:].bitcast(F32), ALU.subtract).then_inc(sem("w_low"), 1)
                    pool.wait_ge(sem("w_low"), i + 1)
                pool.wait_ge(sem("small_in"), 80)

            @bA.vector
            def _(dve):
                v = nc.vector
                cnt = [0]

                def link(ins):
                    cnt[0] += 1
                    ins.then_inc(sem("v1"), 1)
                    dve.wait_ge(sem("v1"), cnt[0])

                def body(s, k):
                    if inside(s, NSTEP):
                        dve.wait_ge(sem(f"x_in{k}"), 8 * (s - k) + 16)
                        for j in range(ST):
                            ins = v.bn_stats(st[:, j, :], xs[:, bass.ds(s * ST + j, 1), :].rearrange("p a d -> p (a d)"))
                        ins.then_inc(sem("stats"), 1)
                        dve.wait_ge(sem("stats"), s + 1)

                        def chain(ins, i):
                            ins.then_inc(sem("mom"), 1)
                            dve.wait_ge(sem("mom"), 5 * s + i)
                        v.tensor_tensor(msum, st[:, :, 1], st[:, :, 4], ALU.add)
                        v.tensor_tensor(vsum, st[:, :, 2], st[:, :, 5], ALU.add)
                        chain(v.tensor_tensor(mdif, st[:, :, 1], st[:, :, 4], ALU.subtract), 1)
                        v.tensor_scalar(mean8[k], msum, 0.5, None, ALU.mult)
                        chain(v.scalar_tensor_tensor(mdif, mdif, 0.25, mdif, ALU.mult, ALU.mult), 2)
                        chain(v.scalar_tensor_tensor(var, vsum, 1.0 / D, mdif, ALU.mult, ALU.add), 3)
                        chain(v.tensor_scalar(vv[k][:, 0:ST], var, LN_EPS, None, ALU.add), 4)
                        chain(v.reciprocal(rv, vv[k][:, 0:ST]), 5)
                        v.tensor_tensor(rv, rv, var, ALU.mult).then_inc(sem("ratio"), 1)
                        dve.wait_ge(sem("ratio"), s + 1)
                        v.tensor_scalar(vv[k][:, ST:2 * ST], rv, RMS_EPS, None, ALU.add).then_inc(sem("var_ready"), 1)
                    if inside(s - 1, NSTEP):
                        wait(dve, sem("h_ready"), 2 * (s - 1))
                        dve.wait_ge(sem("r_ready"), s)
                        v.tensor_tensor(r12, rr[1 - k][:, 0:ST], rr[1 - k][:, ST:2 * ST], ALU.mult)
                        v.tensor_copy(tab[:, bass.ds((s - 1) * ST, ST), 4 * H], mean8[1 - k])
                        v.tensor_copy(tab[:, bass.ds((s - 1) * ST, ST), 4 * H + 1], rr[1 - k][:, 0:ST]).then_inc(sem("r12"), 1)
                        dve.wait_ge(sem("r12"), s)
                        for f in range(2):
                            wait(dve, sem("hTp"), 2 * (s - 2) + f + 1)
                            for j in range(GRP):
                                i = f * GRP + j
                                ins = v.tensor_scalar(hst[:, f, j, :],
                                                      xs[:, bass.ds((s - 1) * ST + i, 1), :].rearrange("p a d -> p (a d)"),
                                                      mean8[1 - k][:, i:i + 1], r12[:, i:i + 1], ALU.subtract, ALU.mult)
                            ins.then_inc(sem("h_ready"), 1)
                groups(dve, body, 1, NSTEP)
                dve.wait_ge(sem("w_in"), 80)
                dve.wait_ge(sem("small_in"), 80)
                v.tensor_scalar(wo[:], wo[:], onw[:, 0:1], None, ALU.mult).then_inc(sem("wo_scaled"), 1)
                dve.wait_ge(sem("z_ready"), NG)
                link(v.tensor_tensor(v3(za), z[:, :, 0:H], dtb.rearrange("p (a h) -> p a h", a=1).broadcast_to([P, T, H]), ALU.add))
                v.scalar_tensor_tensor(nz, za, -1.0, za, ALU.mult, ALU.min).then_inc(sem("nz_ready"), 1)
                dve.wait_ge(sem("ez_ready"), 1)
                dve.wait_ge(sem("alog"), 1)
                link(v.tensor_scalar(den, ez, 2.0, None, ALU.add))
                link(v.reciprocal(den, den))
                link(v.tensor_tensor(sser, ez, den, ALU.mult))
                link(v.tensor_tensor(s2, sser, sser, ALU.mult))
                link(v.tensor_scalar(pol, s2, 1.0 / 15, None, ALU.mult))
                for k in (13, 11, 9, 7, 5, 3):
                    link(v.scalar_tensor_tensor(pol, pol, 1.0 / k, s2, ALU.add, ALU.mult))
                link(v.scalar_tensor_tensor(pol, pol, 1.0, sser, ALU.add, ALU.mult))
                link(v.tensor_scalar(za, za, 0.0, None, ALU.max))
                link(v.scalar_tensor_tensor(za, pol, 2.0, za, ALU.mult, ALU.add))
                v.scalar_tensor_tensor(v3(nz), v3(za), -1.0, alog.rearrange("p (a h) -> p a h", a=1).broadcast_to([P, T, H]),
                                       ALU.mult, ALU.mult).then_inc(sem("g_ready"), 1)
                dve.wait_ge(sem("const_all"), 1)
                with nc.allow_low_precision("zeros and ones"):
                    link(v.tensor_reduce(identp[:], ident16[:].rearrange("p (g c) -> p c g", c=BLK), AX.X, ALU.add))
                link(v.tensor_copy(identp8[:], identp[:].rearrange("p (a c) -> p a c", a=1).broadcast_to([P, H, BLK])))
                dve.wait_ge(sem("arow_made"), 1)
                link(v.tensor_copy(arow, bank[0][:, 0:TH].rearrange("p (r i) -> p r i", i=P)))
                for r in range(NR):
                    ins = v.tensor_tensor_scan(crow[:, r, :], arow[:, r, :], zrow, 1.0, ALU.mult, ALU.add)
                link(ins)
                v.tensor_scalar(crow, crow, rmask, None, ALU.mult).then_inc(sem("crow_ready"), 1)
                v.memset(arow[:, :, 0:1], 0.0).then_inc(sem("arow_ready"), 1)
                dve.wait_ge(sem("ez_ready"), 2)
                link(v.tensor_scalar(eb, eb, 1.0, None, ALU.add))
                v.reciprocal(tab[:, :, 0:H], v3(eb)).then_inc(sem("beta"), 1)
                dve.wait_ge(sem("ctab_made"), 1)
                v.tensor_copy(ctab, bank[1][:, 0:TH]).then_inc(sem("ctab"), 1)
                v.tensor_copy(tab[:, :, H:2 * H], v3(bank[1][:, 0:TH]))
                v.tensor_scalar(tab[:, :, 2 * H:3 * H], v3(bank[1][:, 0:TH]), -1.0, None, ALU.mult)
                dve.wait_ge(sem("ce_made"), 1)
                v.tensor_copy(tab[:, :, 3 * H:4 * H], v3(bank[6][:, 0:TH])).then_inc(sem("tab_done"), 1)

            @bA.scalar
            def _(act):
                a = nc.scalar
                act.wait_ge(sem("small_in"), 80)
                a.activation(alog, alog, ACT.Exp).then_inc(sem("alog"), 1)

                def take_z(g, f):
                    act.wait_ge(sem("zp"), g + 1)
                    a.copy(z[:, bass.ds(g * GRP, GRP), :].rearrange("p t k -> p (t k)"),
                           bank[4 + f][:, 0:GRP * 2 * H]).then_inc(sem("z_ready"), 1)

                def body(s, k):
                    for f in range(2):
                        g = 2 * s + f
                        act.wait_ge(sem("hTp"), g + 1)
                        wait(act, sem(f"hT_out{k}{f}"), 8 * (s - k))
                        wait(act, sem("zp"), g - 3)
                        a.copy(hTs[k][:, f, :], bank[2 + f][:, :]).then_inc(sem("hT_ready"), 1)
                        if not isinstance(g, int) or g > 0:
                            take_z(g - 1, 1 - f)
                        act.wait_ge(sem("hT_ready"), g + 1)
                        act.dma_start(hT_d[bass.ds(g * GRP, GRP)].rearrange("t p i -> p t i"),
                                      hTs[k][:, f, :].rearrange("p (t i) -> p t i", t=GRP)).then_inc(sem(f"hT_out{k}{f}"), 16)
                groups(act, body, 0, NSTEP)
                take_z(NG - 1, 1)
                act.wait_ge(sem("w_in"), 80)
                for i in range(4):
                    a.copy(wh[i][:], wraw[i]).then_inc(sem("w_high"), 1)
                act.wait_ge(sem("nz_ready"), 1)
                a.activation(ez, nz, ACT.Exp).then_inc(sem("ez_ready"), 1)
                act.wait_ge(sem("alog"), 1)
                a.activation(v3(eb), z[:, :, H:2 * H], ACT.Exp, scale=-1.0).then_inc(sem("ez_ready"), 1)
                act.wait_ge(sem("g_ready"), 1)
                a.activation(al, nz, ACT.Exp).then_inc(sem("alpha"), 1)
                for n in ("hT_out00", "hT_out01", "hT_out10", "hT_out11"):
                    act.wait_ge(sem(n), 8 * NSTEP)

            @bA.tensor
            def _(pe):
                pe.wait_ge(sem("ident_made"), 1)
                pe.wait_ge(sem("small_in"), 80)

                def make_z(g, k, f):
                    pe.wait_ge(sem("hT_ready"), g + 1)
                    wait(pe, sem("z_ready"), g - 1)
                    for j in range(GRP):
                        ins = nc.tensor.matmul(bank[4 + f][:, j * 2 * H:(j + 1) * 2 * H], hTs[k][:, f, j * P:j * P + P], wab,
                                               start=(j == 0), stop=(j == GRP - 1), skip_group_check=True)
                    ins.then_inc(sem("zp"), 1)

                def body(s, k):
                    for f in range(2):
                        g = 2 * s + f
                        pe.wait_ge(sem("h_ready"), g + 1)
                        wait(pe, sem("hT_ready"), g - 1)
                        for j in range(GRP):
                            ins = nc.tensor.transpose(bank[2 + f][:, j * P:j * P + P], hst[:, f, j, :], ident[:])
                        ins.then_inc(sem("hTp"), 1)
                        if not isinstance(g, int) or g > 0:
                            make_z(g - 1, k if f else 1 - k, 1 - f)
                groups(pe, body, 0, NSTEP)
                make_z(NG - 1, 1, 1)
                pe.wait_ge(sem("alpha"), 1)
                for r in range(NR):
                    ins = nc.tensor.transpose(bank[0][:, r * P:r * P + P], al[:, r * P:r * P + P], ident[:])
                ins.then_inc(sem("arow_made"), 1)
                pe.wait_ge(sem("crow_ready"), 1)
                for r in range(NR):
                    ins = nc.tensor.transpose(bank[1][:, r * P:r * P + P], crow[:, r, :], ident[:])
                ins.then_inc(sem("ctab_made"), 1)
                pe.wait_ge(sem("ctab"), 1)
                nc.tensor.matmul(bank[6][:, 0:TH], ident[:, P - 1:P].broadcast_to([P, P]), ctab, start=True, stop=True
                                 ).then_inc(sem("ce_made"), 1)

        end_program()

        with ExitStack() as c2:
            off2 = [0]

            def cutd(dt=F32, n=HD):
                w = n if dt == F32 else n // 2
                off2[0] += w
                assert off2[0] <= W_ARENA, off2[0]
                r = arena[:, off2[0] - w:off2[0]]
                return r if dt == F32 else r.bitcast(dt)

            kbuf = cutd()
            sq, sqq = cutd(), cutd()
            khT = [cutd() for _ in range(2)]
            qT = [cutd() for _ in range(2)]
            vbuf = [cutd() for _ in range(2)]
            gbuf = [cutd() for _ in range(2)]
            qbuf = cutd()
            Eb = cutd()
            N32 = cutd()
            UF = cutd()
            Pm = [cutd() for _ in range(2)]
            kw = [cutd() for _ in range(2)]
            St = cutd()
            Rb = cutd()
            Db = cutd()
            Ob = cutd()
            osq = cutd()
            onT = cutd()
            Nhi, Nlo, Nbd, Tm, Um, Em = (cutd(F16) for _ in range(6))
            Xm = [cutd(F16) for _ in range(3)]
            alb = c2.enter_context(nc.sbuf_tensor("alb", [P, HD], F32))
            bI = c2.enter_context(nc.sbuf_tensor("bI", [P, HD], F32))
            hT = c2.enter_context(nc.sbuf_tensor("hT", [P, 2, P], F32))
            hTh = c2.enter_context(nc.sbuf_tensor("hTh", [P, 2, P], F32R))
            hTl = c2.enter_context(nc.sbuf_tensor("hTl", [P, 2, P], F32R))
            ident4 = c2.enter_context(nc.sbuf_tensor("ident4", [P, HH, P], F16))
            xt = c2.enter_context(nc.sbuf_tensor("xt", [P, P], F32))
            xpt = c2.enter_context(nc.sbuf_tensor("xpt", [P, P], F32))
            Tp = c2.enter_context(nc.sbuf_tensor("Tp", [P, H, BLK], F16))
            cur = c2.enter_context(nc.sbuf_tensor("cur", [P, 4 * H + 2], F32))
            qsum = c2.enter_context(nc.sbuf_tensor("qsum", [P, H], F32))
            ksum = c2.enter_context(nc.sbuf_tensor("ksum", [P, H], F32))
            rk = c2.enter_context(nc.sbuf_tensor("rk", [P, H], F32))
            osum = c2.enter_context(nc.sbuf_tensor("osum", [P, H], F32))
            small = c2.enter_context(nc.sbuf_tensor("small", [P, 5, H], F32))
            ssq = c2.enter_context(nc.sbuf_tensor("ssq", [P, T, H], F32))
            bB = c2.enter_context(nc.Block())

            hv = lambda a: a.rearrange("p (h c) -> p h c", h=H)
            hh = lambda a, f: a[:, f * BANK:(f + 1) * BANK]
            h4 = lambda a: a.rearrange("p (h c) -> p h c", h=HH)
            ps = lambda name, f: bank[2 * PAIR[name] + f][:, :]
            SUB, AUX = bank[7], bank[6]
            kind = lambda name: name.rstrip("0123")
            made = lambda name: sem("made_" + kind(name))
            read = lambda name: sem("read_" + kind(name))

            def at(name, t, f):
                return upto(t, f) if name[-1] not in "0123" else upto(NLV * t + int(name[-1]), f)
            HP = P // 2
            xm = lambda lv: Xm[min(lv, 2)]

            def halves(a, lv, part):
                s = BLK << lv
                return a.rearrange("p (q c) -> p q c", c=2 * s)[:, :, part * s:part * s + s]
            bcm = lambda m: m[:].rearrange("p (a c) -> p a c", a=1).broadcast_to([P, HH, P])

            def tile_of(stage, tau):
                return {"a": tau + 1, "b": tau, "c": tau - 1}[stage]

            def live(stage, tau):
                return not isinstance(tau, int) or 0 <= tile_of(stage, tau) < T

            def claim(pe, name, tau, f):
                k = [n for n, _ in PAIR_USES].index(name)
                for back in range(1, 2 * len(PAIR_USES) + 1):
                    n, s = PAIR_USES[(k - back) % len(PAIR_USES)]
                    when = tau - (0 if k - back >= 0 else 1 if k - back >= -len(PAIR_USES) else 2)
                    if PAIR[n] == PAIR[name] and live(s, when):
                        wait(pe, read(n), at(n, tile_of(s, when), f))
                        return

            def run(eng, body, ahead=0):
                for tau in (-1, 0, 1, 2):
                    body(tau, tau % 2)
                with eng.Fori(3, T - 2 - ahead, 2) as i:
                    body(i, 1)
                    body(i + 1, 0)
                for tau in range(T - 1 - ahead, T + 1):
                    body(tau, tau % 2)

            @bB.sync
            def _(sp):
                def load_h(t, p):
                    wait(sp, sem("hT_split"), t - 1)
                    sp.dma_start(hT[:, p, :], hT_d[bass.ds(t, 1)].rearrange("a p i -> p (a i)")
                                 ).then_inc(sem(f"hT_in{p}"), 16)

                def body(tau, p):
                    a, c = tau + 1, tau - 1
                    if isinstance(tau, int) and tau == -1:
                        load_h(0, 0)
                    if live("a", tau):
                        wait(sp, sem("scan"), a)
                        sp.dma_start(alb[:], al_d[bass.ds(a * H, H)].rearrange("(o h) i -> o (h i)", o=1)
                                     .broadcast_to([P, HD])).then_inc(sem("al_in"), 16)
                        if not isinstance(tau, int) or a + 1 < T:
                            load_h(a + 1, p)
                    if live("c", tau):
                        wait(sp, sem("xp_ready"), c)
                        sp.dma_start(xt[:], x_t[bass.ds(c * P, P), :]).then_inc(sem("x_in"), 16)
                        sp.wait_ge(sem("xp_ready"), c + 1)
                        sp.dma_start(xp_d[bass.ds(c, 1)].rearrange("a p i -> p (a i)"), xpt[:]).then_inc(sem("xp_out"), 16)
                run(sp, body, ahead=2)
                sp.wait_ge(sem("xp_out"), 16 * T)

            @bB.tensor
            def _(pe):
                mm = nc.tensor.matmul

                def heads(name, tau, f, t, lhs, rhs):
                    claim(pe, name, tau, f)
                    for j in range(HH):
                        h = f * HH + j
                        ins = mm(ps(name, f)[:, j * P:j * P + P], lhs(h), rhs(h), start=(j == 0), stop=(j == HH - 1),
                                 skip_group_check=True)
                    ins.then_inc(made(name), 1)

                def col(buf):
                    return lambda h: buf[:, h * P:h * P + P]

                def project(name, tau, f, w, p):
                    claim(pe, name, tau, f)
                    o = ps(name, f)
                    mm(o, hTh[:, p, :], hh(wh[w], f), start=True, stop=False)
                    mm(o, hTh[:, p, :], hh(wl[w], f), start=False, stop=False)
                    mm(o, hTl[:, p, :], hh(wh[w], f), start=False, stop=True).then_inc(made(name), 1)

                def products(name, tau, f, lv, part, lhs, rhs, base=None):
                    claim(pe, name, tau, f)
                    o = ps(name, f)[:, 0:BANK // 2]
                    if base is not None:
                        mm(o.rearrange("p (q c) -> p q c", c=BLK << lv), ident16[:], halves(hh(base, f), lv, part),
                           start=True, stop=False, skip_group_check=True)
                    for j in range(HH):
                        h = f * HH + j
                        ins = mm(o[:, j * HP:(j + 1) * HP].rearrange("p (g c) -> p g c", c=BLK << lv), col(lhs)(h),
                                 halves(col(rhs)(h), lv, part), start=(base is None and j == 0), stop=(j == HH - 1),
                                 skip_group_check=True)
                    ins.then_inc(made(name), 1)

                def transposes(name, tau, f, src):
                    claim(pe, name, tau, f)
                    for j in range(HH):
                        h = f * HH + j
                        ins = nc.tensor.transpose(ps(name, f)[:, j * P:j * P + P], col(src)(h), ident[:])
                    ins.then_inc(made(name), 1)

                def body(tau, p):
                    A, Bs, C = (live(s, tau) for s in "abc")
                    a, b, c = tau + 1, tau, tau - 1
                    q = 1 - p
                    if Bs:
                        for f in range(2):
                            pe.wait_ge(read("KT"), at("KT", b, f))
                            heads("G", tau, f, b, col(khT[p]), col(khT[p]))
                    if C:
                        for f in range(2):
                            pe.wait_ge(read("E"), at("E", c, f))
                            pe.wait_ge(read("U3"), at("U3", c, f))
                            heads("C", tau, f, c, col(Em), col(Um))
                        for f in range(2):
                            wait(pe, read("SU"), at("SU", c - 1, f))
                            if isinstance(c, int) and c == 0:
                                pe.wait_ge(sem("state0"), 5)
                            heads("KS", tau, f, c, col(khT[q]), col(St))
                    if A:
                        pe.wait_ge(sem("hT_split"), a + 1)
                        for f in range(2):
                            project("K", tau, f, 1, q)
                    for n in range(BLK - 1):
                        if Bs:
                            if n == 0:
                                pe.wait_ge(sem("Nbd"), upto(b, 1))
                                wait(pe, sem("Tbd"), b)
                            else:
                                pe.wait_ge(sem("sub"), (BLK - 1) * b + n)
                            mm(SUB[:, 0:H * BLK], ident16[:], identp8[:].rearrange("p h c -> p (h c)"), start=True, stop=False,
                               skip_group_check=True)
                            for h in range(H):
                                rhs = identp[:] if n == 0 else Tp[:, h, :]
                                ins = mm(SUB[:, h * BLK:(h + 1) * BLK], col(Nbd)(h), rhs, start=False, stop=(h == H - 1),
                                         skip_group_check=True)
                            ins.then_inc(sem("sub_made"), 1)
                        f = n % 2
                        if C and n < 2:
                            pe.wait_ge(read("KS"), at("KS", c, f))
                            pe.wait_ge(read("C"), at("C", c, f))
                            heads("D", tau, f, c, col(UF), col(Rb))
                        elif C and n < 4:
                            pe.wait_ge(read("D"), at("D", c, f))
                            pe.wait_ge(read("QK"), at("QK", c, f))
                            heads("PD", tau, f, c, col(Pm[q]), col(Db))
                        elif C and n < 6:
                            heads("QS", tau, f, c, col(qT[q]), col(St))
                        elif C and n == 6:
                            pe.wait_ge(sem("kw"), c + 1)
                            heads("SU", tau, 0, c, col(kw[q]), col(Db))
                    if C:
                        heads("SU", tau, 1, c, col(kw[q]), col(Db))
                    if A:
                        for f in range(2):
                            project("Q", tau, f, 0, q)
                    if Bs:
                        pe.wait_ge(sem("Tbd"), b + 1)
                        for f in range(2):
                            heads("UB", tau, f, b, col(Tm), lambda h: ident16[:])
                    for lv in range(NLV):
                        if A and lv == 1:
                            project("V", tau, 0, 2, q)
                        if A and lv == 2:
                            for f in range(2):
                                pe.wait_ge(read("Q"), at("Q", a, f))
                                transposes("QT", tau, f, qbuf)
                        if Bs and lv == 3:
                            heads("QK", tau, 1, b, col(khT[p]), col(qT[p]))
                        if Bs:
                            for f in range(2):
                                if lv == 0:
                                    pe.wait_ge(sem("Nhi"), upto(b, f))
                                else:
                                    pe.wait_ge(read(f"T{lv - 1}"), at(f"T{lv - 1}", b, f))
                                products(f"X{lv}", tau, f, lv, 0, Nhi, Tm)
                        if A and lv == 0:
                            pe.wait_ge(sem("kh"), a + 1)
                            for f in range(2):
                                transposes("KT", tau, f, kbuf)
                        if A and lv == 1:
                            project("V", tau, 1, 2, q)
                        if Bs and lv == 2:
                            heads("QK", tau, 0, b, col(khT[p]), col(qT[p]))
                        if A and lv == 3:
                            for f in range(2):
                                project("GT", tau, f, 3, q)
                        if Bs:
                            added = BLK << lv < 32
                            for f in range(2):
                                pe.wait_ge(read(f"X{lv}"), at(f"X{lv}", b, f))
                                U = "UB" if lv == 0 else f"U{lv - 1}"
                                pe.wait_ge(read(U), at(U, b, f))
                                products(f"T{lv}", tau, f, lv, 0, Um, xm(lv), Tm if added else None)
                            for f in range(2):
                                products(f"U{lv}", tau, f, lv, 1, xm(lv), Um, Um if added else None)
                    if C:
                        pe.wait_ge(sem("on"), c + 1)
                        for f in range(2):
                            transposes("OT", tau, f, Ob)
                    if Bs:
                        pe.wait_ge(sem("Nlo"), b + 1)
                        for f in range(2):
                            pe.wait_ge(read("T3"), at("T3", b, f))
                            claim(pe, "E", tau, f)
                            o = ps("E", f)
                            mm(o, negid16[:], hh(Tm, f), start=True, stop=False, skip_group_check=True)
                            mm(o, ident16[:], ident4[:].rearrange("p h c -> p (h c)"), start=False, stop=False,
                               skip_group_check=True)
                            for j in range(HH):
                                h = f * HH + j
                                oj = o[:, j * P:j * P + P]
                                mm(oj, col(Nhi)(h), col(Tm)(h), start=False, stop=False, skip_group_check=True)
                                ins = mm(oj, col(Nlo)(h), col(Tm)(h), start=False, stop=(j == HH - 1), skip_group_check=True)
                            ins.then_inc(made("E"), 1)
                    if C:
                        for f in range(2):
                            pe.wait_ge(read("OT"), at("OT", c, f))
                        wait(pe, sem("xp_ready"), c)
                        for h in range(H):
                            ins = mm(AUX[:, 0:P], col(onT)(h), col(wo)(h), start=(h == 0), stop=(h == H - 1))
                        ins.then_inc(sem("att_made"), 1)
                run(pe, body)

            @bB.scalar
            def _(act):
                a_ = nc.scalar

                def body(tau, p):
                    A, Bs, C = (live(s, tau) for s in "abc")
                    a, b, c = tau + 1, tau, tau - 1
                    q = 1 - p

                    def take(name, t, f, dst, func=ACT.Copy, scale=1.0):
                        act.wait_ge(made(name), at(name, t, f))
                        a_.activation(hh(dst, f), ps(name, f), func, scale=scale).then_inc(read(name), 1)

                    def take_blocks(which, lv, t, f, dst, part):
                        name, s = f"{which}{lv}", BLK << lv
                        act.wait_ge(made(name), at(name, t, f))
                        src = ps(name, f)[:, 0:BANK // 2]
                        if s < 32:
                            ins = a_.copy(halves(hh(dst, f), lv, part), src.rearrange("p (q c) -> p q c", c=s))
                        else:
                            for g in range(P // (2 * s)):
                                rows = slice(2 * s * g + s * (1 - part), 2 * s * g + s * (2 - part))
                                ins = a_.copy(h4(hh(dst, f))[rows, :, 2 * s * g + s * part:2 * s * g + s * (part + 1)],
                                              src.rearrange("p (h c) -> p h c", h=HH)[rows, :, g * s:(g + 1) * s])
                        ins.then_inc(read(name), 1)
                    if Bs:
                        for f in range(2):
                            act.wait_ge(read("G"), at("G", b, f))
                            wait(act, made("E"), at("E", b - 1, 1))
                            wait(act, sem("Nlo"), b)
                            a_.copy(hh(Nhi, f), hh(N32, f)).then_inc(sem("Nhi"), 1)
                    if A:
                        for f in range(2):
                            wait(act, made("KT"), at("KT", a - 1, 1))
                            wait(act, sem("kw"), a)
                            take("K", a, f, kbuf, ACT.Silu)
                    for n in range(BLK - 1):
                        if Bs:
                            act.wait_ge(sem("sub_made"), (BLK - 1) * b + n + 1)
                            a_.copy(Tp[:].rearrange("p h c -> p (h c)"), SUB[:, 0:H * BLK]).then_inc(sem("sub"), 1)
                        f = n % 2
                        if A and 1 <= n < 3:
                            act.wait_ge(read("K"), at("K", a, n - 1))
                            wait(act, sem("ksum"), a)
                            ins = a_.activation(hh(sq, n - 1), hh(kbuf, n - 1), ACT.Square)
                            if n == 2:
                                ins.then_inc(sem("ksq"), 1)
                        if C and n < 2:
                            wait(act, made("SU"), at("SU", c - 1, f))
                            take("D", c, f, Db)
                        elif C and n < 4:
                            wait(act, made("OT"), at("OT", c - 1, f))
                            take("PD", c, f, Ob)
                    if A:
                        for f in range(2):
                            wait(act, made("QT"), at("QT", a - 1, 1))
                            wait(act, sem("qsq"), a)
                            take("Q", a, f, qbuf, ACT.Silu)
                    if Bs:
                        for f in range(2):
                            wait(act, read("C"), at("C", b - 1, f))
                            take("UB", b, f, Um)
                    for lv in range(NLV):
                        if A and lv == 0:
                            for f in range(2):
                                wait(act, made("KS"), at("KS", a - 2, f))
                                take("KT", a, f, khT[q])
                        if A and lv == 1:
                            for f in range(2):
                                wait(act, read("KS"), at("KS", a - 2, f))
                                take("V", a, f, vbuf[q], ACT.Silu)
                        if A and lv == 2:
                            for f in range(2):
                                wait(act, made("QS"), at("QS", a - 2, f))
                                take("QT", a, f, qT[q])
                        if A and lv == 3:
                            for f in range(2):
                                wait(act, sem("sgr"), a - 1)
                                take("GT", a, f, gbuf[q], ACT.Silu)
                        if Bs:
                            for f in range(2):
                                take_blocks("T", lv, b, f, Tm, 0)
                            for f in range(2):
                                take_blocks("U", lv, b, f, Um, 1)
                    if C:
                        for f in range(2):
                            wait(act, sem("att_made"), c)
                            take("OT", c, f, onT)
                    if Bs:
                        for f in range(2):
                            wait(act, made("C"), at("C", b - 1, f))
                            take("E", b, f, Em, scale=ESC)
                    if A:
                        wait(act, sem("qsum"), a)
                        act.wait_ge(read("Q"), at("Q", a, 1))
                        a_.activation(sqq, qbuf, ACT.Square).then_inc(sem("qsq"), 1)
                run(act, body)

            @bB.vector
            def _(dve):
                v = nc.vector

                def body(tau, p):
                    A, Bs, C = (live(s, tau) for s in "abc")
                    a, b, c = tau + 1, tau, tau - 1
                    q = 1 - p

                    def split(t, k):
                        dve.wait_ge(sem(f"hT_in{k}"), 8 * (t - k) + 16)
                        wait(dve, made("GT"), at("GT", t - 2, 1))
                        v.tensor_copy(hTh[:, k, :], hT[:, k, :]).then_inc(sem("hT_high"), 1)
                        dve.wait_ge(sem("hT_high"), t + 1)
                        v.tensor_tensor(hTl[:, k, :], hT[:, k, :], hTh[:, k, :].bitcast(F32), ALU.subtract
                                        ).then_inc(sem("hT_split"), 1)
                    if isinstance(tau, int) and tau == -1:
                        split(0, 0)
                        v.memset(St, 0.0).then_inc(sem("state0"), 1)
                        v.tensor_copy(ident4[:], bcm(ident16)).then_inc(sem("state0"), 1)
                        for m in Xm:
                            v.memset(m, 0.0).then_inc(sem("state0"), 1)
                    if Bs:
                        for f in range(2):
                            dve.wait_ge(made("G"), at("G", b, f))
                            dve.wait_ge(sem("Ebn"), b + 1)
                            v.tensor_tensor(hh(N32, f), ps("G", f), hh(N32, f), ALU.mult).then_inc(read("G"), 1)
                    if C:
                        for f in range(2):
                            dve.wait_ge(made("C"), at("C", c, f))
                            wait(dve, made("D"), at("D", c - 1, f))
                            v.scalar_tensor_tensor(hh(UF, f), ps("C", f), 1.0 / ESC, hh(Um, f), ALU.mult, ALU.add
                                                   ).then_inc(read("C"), 1)
                        wait(dve, read("SU"), at("SU", c - 1, 1))
                        v.tensor_copy(cur[:], tab[:, bass.ds(c, 1), :].rearrange("p a k -> p (a k)")).then_inc(sem("cur"), 1)
                        dve.wait_ge(sem("cur"), c + 1)
                        for f in range(2):
                            dve.wait_ge(made("KS"), at("KS", c, f))
                            wait(dve, made("D"), at("D", c - 1, f))
                            dve.wait_ge(read("V"), at("V", c, f))
                            for j in range(HH):
                                h = f * HH + j
                                ins = v.scalar_tensor_tensor(hv(Rb)[:, h, :], ps("KS", f)[:, j * P:j * P + P],
                                                             cur[:, 2 * H + h:2 * H + h + 1], hv(vbuf[q])[:, h, :],
                                                             ALU.mult, ALU.add)
                            ins.then_inc(read("KS"), 1)
                    for n in range(BLK - 1):
                        f = n % 2
                        if Bs and n == 1:
                            dve.wait_ge(sem("qsq"), b + 1)
                            v.tensor_reduce(qsum[:], hv(sqq), AX.X, ALU.add).then_inc(sem("qsum"), 1)
                            dve.wait_ge(sem("qsum"), b + 1)
                            v.tensor_scalar(ssq[:, bass.ds(b, 1), :].rearrange("p a h -> p (a h)"), qsum[:], RMS_EPS, None,
                                            ALU.add).then_inc(sem("ssq_ready"), 1)
                        if A and n == 2:
                            dve.wait_ge(sem("ksq"), a + 1)
                            wait(dve, sem("rk"), a)
                            v.tensor_reduce(ksum[:], hv(sq), AX.X, ALU.add).then_inc(sem("ksum"), 1)
                        elif C and 4 <= n < 6:
                            dve.wait_ge(made("QS"), at("QS", c, f))
                            dve.wait_ge(read("PD"), at("PD", c, f))
                            for j in range(HH):
                                h = f * HH + j
                                ins = v.scalar_tensor_tensor(hv(Ob)[:, h, :], ps("QS", f)[:, j * P:j * P + P],
                                                             cur[:, H + h:H + h + 1], hv(Ob)[:, h, :], ALU.mult, ALU.add)
                            ins.then_inc(read("QS"), 1)

                    def take_su(f):
                        dve.wait_ge(made("SU"), at("SU", c, f))
                        for j in range(HH):
                            h = f * HH + j
                            ins = v.scalar_tensor_tensor(hv(St)[:, h, :], hv(St)[:, h, :],
                                                         cur[:, 3 * H + h:3 * H + h + 1],
                                                         ps("SU", f)[:, j * P:j * P + P], ALU.mult, ALU.add)
                        ins.then_inc(read("SU"), 1)
                    if Bs:
                        dve.wait_ge(sem("sub"), (BLK - 1) * (b + 1))
                        wait(dve, made("E"), at("E", b - 1, 1))
                        v.tensor_tensor(Tm.rearrange("p (h g c) -> p h g c", h=H, c=BLK),
                                        Tp[:].rearrange("p h (a c) -> p h a c", a=1).broadcast_to([P, H, P // BLK, BLK]),
                                        maskbd[:].rearrange("p (a g c) -> p a g c", a=1, c=BLK).broadcast_to([P, H, P // BLK, BLK]),
                                        ALU.mult).then_inc(sem("Tbd"), 1)
                    if C:
                        take_su(0)
                        take_su(1)
                    for lv in range(NLV):
                        if C and lv == 1:
                            dve.wait_ge(sem("osq"), c + 1)
                            v.tensor_reduce(osum[:], hv(osq), AX.X, ALU.add).then_inc(sem("osum"), 1)
                        if C and lv == 3:
                            dve.wait_ge(sem("sgr"), c + 1)
                            dve.wait_ge(read("QS"), at("QS", c, 1))
                            v.tensor_tensor(Ob, Ob, osq, ALU.mult).then_inc(sem("on"), 1)
                        if Bs and lv == 3:
                            for f in range(2):
                                dve.wait_ge(made("QK"), at("QK", b, f))
                                wait(dve, made("PD"), at("PD", b - 2, f))
                                v.tensor_tensor(hh(Pm[p], f), ps("QK", f), hh(Eb, f), ALU.mult).then_inc(read("QK"), 1)
                        if Bs:
                            for f in range(2):
                                dve.wait_ge(made(f"X{lv}"), at(f"X{lv}", b, f))
                                if lv == 3:
                                    dve.wait_ge(made("U2"), at("U2", b, f))
                                else:
                                    last = "U3" if lv == 2 else f"U{lv}"
                                    wait(dve, made(last), at(last, b - 1, f))
                                s = BLK << lv
                                v.tensor_tensor(hh(xm(lv), f).rearrange("p (h g c) -> p h g c", h=HH, c=2 * s)[:, :, :, 0:s],
                                                ps(f"X{lv}", f)[:, 0:BANK // 2].rearrange("p (h g c) -> p h g c", h=HH, c=s),
                                                halves(mask[lv][:], lv, 0).rearrange("p (a g) c -> p a g c", a=1)
                                                .broadcast_to([P, HH, HP // s, s]), ALU.mult).then_inc(read(f"X{lv}"), 1)
                    if A:
                        dve.wait_ge(sem("bI"), a + 1)
                        dve.wait_ge(sem("al_in"), 16 * a + 16)
                        if Bs:
                            dve.wait_ge(read("QK"), at("QK", b, 1))
                        wait(dve, sem("kw"), a)
                        v.tensor_tensor_scan(Eb, alb[:], bI[:], 0.0, ALU.mult, ALU.add).then_inc(sem("scan"), 1)
                    if live("a", tau) and (not isinstance(tau, int) or a + 1 < T):
                        split(a + 1, p)
                    if C:
                        dve.wait_ge(sem("x_in"), 16 * c + 16)
                        v.tensor_scalar(xt[:], xt[:], cur[:, 4 * H:4 * H + 1], cur[:, 4 * H + 1:4 * H + 2],
                                        ALU.subtract, ALU.mult).then_inc(sem("y"), 1)
                    if C:
                        dve.wait_ge(sem("att_made"), c + 1)
                        dve.wait_ge(sem("y"), c + 1)
                        wait(dve, sem("xp_out"), 16 * c)
                        v.tensor_tensor(xpt[:], AUX[:, 0:P], xt[:], ALU.add).then_inc(sem("xp_ready"), 1)
                run(dve, body, ahead=2)

            @bB.gpsimd
            def _(pool):
                g = nc.gpsimd
                bch = lambda cols: cols.rearrange("p (h a) -> p h a", a=1).broadcast_to([P, H, P])

                def body(tau, p):
                    A, Bs, C = (live(s, tau) for s in "abc")
                    a, b, c = tau + 1, tau, tau - 1
                    q = 1 - p
                    if Bs:
                        wait(pool, sem("sub_made"), (BLK - 1) * b)
                        for f in range(2):
                            pool.wait_ge(sem("Nhi"), upto(b, f))
                            g.tensor_tensor(h4(hh(Nbd, f)), h4(hh(Nhi, f)), bcm(maskbd), ALU.mult).then_inc(sem("Nbd"), 1)
                        g.tensor_tensor(Nlo, N32, Nhi, ALU.subtract).then_inc(sem("Nlo"), 1)
                    if A:
                        wait(pool, sem("scan"), a)
                        wait(pool, sem("Ebn"), a)
                        g.tensor_tensor(hv(bI[:]), ident[:].rearrange("p (a c) -> p a c", a=1).broadcast_to([P, H, P]),
                                        bch(tab[:, bass.ds(a, 1), 0:H].rearrange("p a h -> p (a h)")), ALU.mult
                                        ).then_inc(sem("bI"), 1)
                        pool.wait_ge(sem("ksum"), a + 1)
                        g.tensor_tensor(ksum[:], ksum[:], keps[:], ALU.add).then_inc(sem("kpe"), 1)
                        pool.wait_ge(sem("kpe"), a + 1)
                        g.tensor_tensor(rk[:], ksum[:], mhalf[:, 0:H], ALU.pow).then_inc(sem("rk"), 1)
                        pool.wait_ge(sem("rk"), a + 1)
                        g.tensor_tensor(hv(kbuf), hv(kbuf), bch(rk[:]), ALU.mult).then_inc(sem("kh"), 1)
                    if C:
                        for f in range(2):
                            pool.wait_ge(read("QS"), at("QS", c, f))
                        wait(pool, sem("on"), c)
                        g.tensor_tensor(osq, Ob, Ob, ALU.mult).then_inc(sem("osq"), 1)
                    if C:
                        o = small[:]

                        def step(ins, k):
                            ins.then_inc(sem("r_chain"), 1)
                            pool.wait_ge(sem("r_chain"), 3 * c + k)
                        pool.wait_ge(sem("s_chain"), 3 * c + 3)
                        pool.wait_ge(sem("osum"), c + 1)
                        step(g.tensor_tensor(o[:, 3, :], o[:, 2, :], osum[:], ALU.mult), 1)
                        step(g.tensor_tensor(o[:, 3, :], o[:, 3, :], keps[:], ALU.add), 2)
                        step(g.tensor_tensor(o[:, 4, :], o[:, 3, :], mhalf[:, 0:H], ALU.pow), 3)
                        g.tensor_tensor(o[:, 4, :], o[:, 4, :], o[:, 1, :], ALU.mult).then_inc(sem("r"), 1)
                        pool.wait_ge(sem("r"), c + 1)
                        pool.wait_ge(read("GT"), at("GT", c, 1))
                        g.tensor_tensor(hv(osq), hv(gbuf[q]), bch(o[:, 4, :]), ALU.mult).then_inc(sem("sgr"), 1)
                    if Bs:
                        def sstep(ins, k):
                            ins.then_inc(sem("s_chain"), 1)
                            pool.wait_ge(sem("s_chain"), 3 * b + k)
                        o = small[:]
                        if C:
                            pool.wait_ge(sem("r"), c + 1)
                        pool.wait_ge(sem("ssq_ready"), b + 1)
                        sstep(g.tensor_tensor(o[:, 0, :], ssq[:, bass.ds(b, 1), :].rearrange("p a h -> p (a h)"),
                                              mhalf[:, 0:H], ALU.pow), 1)
                        g.tensor_tensor(o[:, 1, :], o[:, 0, :], krt[:], ALU.mult)
                        sstep(g.tensor_tensor(o[:, 2, :], o[:, 0, :], kinv[:], ALU.mult), 2)
                        sstep(g.tensor_tensor(o[:, 2, :], o[:, 2, :], o[:, 2, :], ALU.mult), 3)
                    if A:
                        pool.wait_ge(sem("scan"), a + 1)
                        g.tensor_tensor(N32, bI[:], Eb, ALU.subtract).then_inc(sem("Ebn"), 1)
                        wait(pool, made("SU"), at("SU", a - 2, 1))
                        pool.wait_ge(sem("kh"), a + 1)
                        g.tensor_tensor(hv(kw[q]), hv(kbuf), hv(Eb)[:, :, P - 1:P].broadcast_to([P, H, P]), ALU.mult
                                        ).then_inc(sem("kw"), 1)
                run(pool, body)

        end_program()

        def within(g):
            return inside(g, NG)

        GW = GRP * P
        t4 = lambda a: a.rearrange("p (t d) -> p t d", t=GRP)
        gsl = lambda d, g: d[bass.ds(g * GRP, GRP)].rearrange("t p d -> p t d")
        with ExitStack() as c3:
            off3 = [0]

            def cutt(n):
                off3[0] += n
                assert off3[0] <= W_ARENA
                return arena[:, off3[0] - n:off3[0]]
            xg, xpg = ([cutt(GW) for _ in range(2)] for _ in range(2))
            xsg = [cutt(GW) for _ in range(2)]
            x1g, tTg = ([cutt(GW) for _ in range(2)] for _ in range(2))
            sqg, mg, tg = (cutt(GW) for _ in range(3))
            h1, h2 = cutt(NF * GW), cutt(NF * GW)
            wfc = cutt(DFF)
            wpj = cutt(NF * P).rearrange("p (j n) -> p j n", j=NF)
            gwT = cutt(NE)
            smalls = lambda: [cutt(GRP) for _ in range(2)]
            ms, rx = smalls(), smalls()
            mean, var, rt = smalls(), smalls(), smalls()
            msum, vsum, mdif = cutt(GRP), cutt(GRP), cutt(GRP)
            st3 = cutt(GRP * 6).rearrange("p (t s) -> p t s", s=6)
            gws = cutt(P)
            lg = cutt(T * NE).rearrange("p (t e) -> p t e", e=NE)
            bcd = lambda a: a.rearrange("p (t a) -> p t a", a=1).broadcast_to([P, GRP, P])
            wfh, wfl = (c3.enter_context(nc.sbuf_tensor(n, [P, DFF], F32R)) for n in ("wfh", "wfl"))
            mTh, mTl = (c3.enter_context(nc.sbuf_tensor(n, [P, GW], F32R)) for n in ("mTh", "mTl"))
            b3 = c3.enter_context(nc.Block())


            @b3.sync
            def _(sp):
                sp.dma_start(wfc, W_fc).then_inc(sem("m_w"), 16)
                sp.dma_start(wpj, W_proj.rearrange("(j p) n -> p j n", p=P)).then_inc(sem("m_w"), 16)
                sp.dma_start(gws[0:NE, :], gate_w).then_inc(sem("m_w"), 16)

                def body(g, k):
                    if within(g):
                        wait(sp, sem("xs_sum"), g - 1)
                        sp.dma_start(t4(xg[k]), x_t[bass.ds(g * GW, GW), :].rearrange("(t p) d -> p t d", p=P)
                                     ).then_inc(sem(f"m_in{k}"), 16)
                        sp.dma_start(t4(xpg[k]), gsl(xp_d, g)).then_inc(sem(f"m_in{k}"), 16)
                    if within(g - 4):
                        sp.wait_ge(sem("m_x1"), g - 3)
                        sp.dma_start(gsl(x1_d, g - 4), t4(x1g[k])).then_inc(sem(f"x1_out{k}"), 16)
                    if within(g - 5):
                        sp.wait_ge(sem("m_tT"), g - 4)
                        sp.dma_start(gsl(tT_d, g - 5), t4(tTg[1 - k])).then_inc(sem(f"tT_out{1 - k}"), 16)
                groups(sp, body, 5, NG)
                for n in ("x1_out0", "x1_out1", "tT_out0", "tT_out1"):
                    sp.wait_ge(sem(n), 8 * NG)

            @b3.gpsimd
            def _(pool):
                g_ = nc.gpsimd

                def body(g, k):
                    if within(g):
                        pool.wait_ge(sem(f"m_in{k}"), 16 * (g - k) + 32)
                        wait(pool, sem("m_ssum"), g)
                        g_.tensor_tensor(sqg, xpg[k], xpg[k], ALU.mult).then_inc(sem("m_sq"), 1)
                        pool.wait_ge(sem("m_ms"), g + 1)
                        wait(pool, sem("m_m"), g - 1)
                        g_.tensor_tensor(rx[k], ms[k], mhalf[:, 0:GRP], ALU.pow).then_inc(sem("m_r"), 1)
                    if within(g - 3):
                        pool.wait_ge(sem("m_var"), g - 2)
                        wait(pool, sem("m_t"), g - 4)
                        g_.tensor_tensor(rt[1 - k], var[1 - k], mhalf[:, 0:GRP], ALU.pow).then_inc(sem("m_r3"), 1)
                groups(pool, body, 5, NG)

            @b3.vector
            def _(dve):
                v = nc.vector

                dve.wait_ge(sem("m_w"), 48)
                v.tensor_copy(wfh[:], wfc).then_inc(sem("m_wsplit"), 1)
                dve.wait_ge(sem("m_wsplit"), 1)
                v.tensor_tensor(wfl[:], wfc, wfh[:].bitcast(F32), ALU.subtract).then_inc(sem("m_wsplit"), 1)

                def body(g, k):
                    if within(g - 2):
                        dve.wait_ge(sem("m_mT"), g - 1)
                        wait(dve, sem("m_fc"), NF * (g - 2))
                        v.tensor_tensor(mTl[:], bank[0][:, :], mTh[:].bitcast(F32), ALU.subtract).then_inc(sem("m_mTl"), 1)
                    if within(g - 1):
                        dve.wait_ge(sem("m_r"), g)
                        wait(dve, sem("m_mTp"), g - 1)
                        v.tensor_tensor(t4(mg), t4(xpg[1 - k]), bcd(rx[1 - k]), ALU.mult).then_inc(sem("m_m"), 1)
                    if within(g - 4):
                        dve.wait_ge(sem("m_r3"), g - 3)
                        wait(dve, sem("m_tTp"), g - 4)
                        for j in range(GRP):
                            ins = v.tensor_scalar(tg[:, j * P:j * P + P], x1g[k][:, j * P:j * P + P], mean[k][:, j:j + 1],
                                                  rt[k][:, j:j + 1], ALU.subtract, ALU.mult)
                        ins.then_inc(sem("m_t"), 1)
                    if within(g):
                        dve.wait_ge(sem("m_sq"), g + 1)
                        wait(dve, sem("m_r"), g - 1)
                        v.tensor_reduce(ms[k], t4(sqg), AX.X, ALU.add).then_inc(sem("m_ssum"), 1)
                        dve.wait_ge(sem("m_ssum"), g + 1)
                        v.tensor_scalar(ms[k], ms[k], 1.0 / D, RMS_EPS, ALU.mult, ALU.add).then_inc(sem("m_ms"), 1)
                    if within(g - 3):
                        c, kc = g - 3, 1 - k

                        def link(ins, i):
                            ins.then_inc(sem("m_v"), 1)
                            dve.wait_ge(sem("m_v"), 4 * c + i)
                        dve.wait_ge(sem("m_pj"), c + 1)
                        wait(dve, sem(f"x1_out{kc}"), 8 * (c - kc))
                        dve.wait_ge(sem("xs_sum"), c + 1)
                        v.tensor_tensor(x1g[kc], xsg[kc], bank[6][:, :], ALU.add).then_inc(sem("m_x1"), 1)
                        dve.wait_ge(sem("m_x1"), c + 1)
                        for j in range(GRP):
                            ins = v.bn_stats(st3[:, j, :], x1g[kc][:, j * P:j * P + P])
                        link(ins, 1)
                        v.tensor_tensor(msum, st3[:, :, 1], st3[:, :, 4], ALU.add)
                        v.tensor_tensor(vsum, st3[:, :, 2], st3[:, :, 5], ALU.add)
                        link(v.tensor_tensor(mdif, st3[:, :, 1], st3[:, :, 4], ALU.subtract), 2)
                        v.tensor_scalar(mean[kc], msum, 0.5, None, ALU.mult)
                        link(v.scalar_tensor_tensor(mdif, mdif, 0.25, mdif, ALU.mult, ALU.mult), 3)
                        link(v.scalar_tensor_tensor(var[kc], vsum, 1.0 / D, mdif, ALU.mult, ALU.add), 4)
                        v.tensor_scalar(var[kc], var[kc], LN_EPS, None, ALU.add).then_inc(sem("m_var"), 1)
                    if within(g - 1):
                        v.tensor_tensor(xsg[1 - k], xg[1 - k], xpg[1 - k], ALU.add).then_inc(sem("xs_sum"), 1)
                    if within(g - 5):
                        dve.wait_ge(sem("m_lgp"), g - 4)
                        v.tensor_copy(lg[:, bass.ds((g - 5) * GRP, GRP), :].rearrange("p t e -> p (t e)"),
                                      bank[7][:, 0:GRP * NE]).then_inc(sem("m_lg"), 1)
                groups(dve, body, 5, NG)

            @b3.scalar
            def _(act):
                a_ = nc.scalar
                act.wait_ge(sem("m_gwp"), 1)
                a_.copy(gwT, bank[7][:, 0:NE]).then_inc(sem("m_gwT"), 1)

                def body(g, k):
                    if within(g - 2):
                        def square(j):
                            act.wait_ge(sem("m_relu"), NF * (g - 2) + j + 1)
                            if j == 0:
                                wait(act, sem("m_pj"), g - 2)
                            cols = slice(j * GW, (j + 1) * GW)
                            a_.activation(h2[:, cols], h1[:, cols], ACT.Square).then_inc(sem("m_h2"), 1)
                        for j in range(NF):
                            act.wait_ge(sem("m_fc"), NF * (g - 2) + j + 1)
                            a_.activation(h1[:, j * GW:(j + 1) * GW], bank[1 + j][:, :], ACT.Relu).then_inc(sem("m_relu"), 1)
                            if j > 0:
                                square(j - 1)
                        square(NF - 1)
                    if within(g - 1):
                        act.wait_ge(sem("m_mTp"), g)
                        wait(act, sem("m_fc"), NF * (g - 1))
                        a_.copy(mTh[:], bank[0][:, :]).then_inc(sem("m_mT"), 1)
                    if within(g - 4):
                        act.wait_ge(sem("m_tTp"), g - 3)
                        wait(act, sem(f"tT_out{k}"), 8 * (g - 4 - k))
                        wait(act, sem("m_lgp"), g - 5)
                        a_.copy(tTg[k], bank[5][:, :]).then_inc(sem("m_tT"), 1)
                groups(act, body, 5, NG)

            @b3.tensor
            def _(pe):
                mm = nc.tensor.matmul
                pe.wait_ge(sem("m_w"), 48)
                nc.tensor.transpose(bank[7][:, 0:NE], gws[0:NE, :], ident[0:NE, 0:NE]).then_inc(sem("m_gwp"), 1)
                pe.wait_ge(sem("m_gwT"), 1)
                pe.wait_ge(sem("m_wsplit"), 2)

                def body(g, k):
                    if within(g - 3):
                        pe.wait_ge(sem("m_h2"), NF * (g - 2))
                        wait(pe, sem("m_x1"), g - 3)
                        for t in range(GRP):
                            for j in range(NF):
                                ins = mm(bank[6][:, t * P:t * P + P], h2[:, j * GW + t * P:j * GW + (t + 1) * P], wpj[:, j, :],
                                         start=(j == 0), stop=(j == NF - 1))
                        ins.then_inc(sem("m_pj"), 1)
                    if within(g - 2):
                        pe.wait_ge(sem("m_mTl"), g - 1)
                        for j in range(NF):
                            wait(pe, sem("m_relu"), NF * (g - 3) + j + 1)
                            o, cols = bank[1 + j][:, :], slice(j * P, j * P + P)
                            mm(o, wfh[:, cols], mTh[:], start=True, stop=False)
                            mm(o, wfh[:, cols], mTl[:], start=False, stop=False)
                            mm(o, wfl[:, cols], mTh[:], start=False, stop=True).then_inc(sem("m_fc"), 1)
                    if within(g - 1):
                        pe.wait_ge(sem("m_m"), g)
                        wait(pe, sem("m_mTl"), g - 1)
                        for j in range(GRP):
                            ins = nc.tensor.transpose(bank[0][:, j * P:j * P + P], mg[:, j * P:j * P + P], ident[:])
                        ins.then_inc(sem("m_mTp"), 1)
                    if within(g - 4):
                        pe.wait_ge(sem("m_t"), g - 3)
                        wait(pe, sem("m_tT"), g - 4)
                        for j in range(GRP):
                            ins = nc.tensor.transpose(bank[5][:, j * P:j * P + P], tg[:, j * P:j * P + P], ident[:])
                        ins.then_inc(sem("m_tTp"), 1)
                    if within(g - 5):
                        pe.wait_ge(sem("m_tT"), g - 4)
                        wait(pe, sem("m_lg"), g - 5)
                        for j in range(GRP):
                            ins = mm(bank[7][:, j * NE:(j + 1) * NE], tTg[1 - k][:, j * P:j * P + P], gwT,
                                     start=(j == 0), stop=(j == GRP - 1), skip_group_check=True)
                        ins.then_inc(sem("m_lgp"), 1)
                groups(pe, body, 5, NG)

        end_program()

        with ExitStack() as c4:
            lgoff = off3[0] - T * NE
            lgf = arena[:, lgoff:lgoff + T * NE]
            off4 = [lgoff + T * NE]

            def cute(n):
                off4[0] += n
                assert off4[0] <= W_ARENA
                return arena[:, off4[0] - n:off4[0]]
            c8 = lambda a: a.rearrange("p (t e) -> p t e", e=NE)
            pr, wt, sc, oh1, oh2, io = (cute(T * NE) for _ in range(6))
            red = cute(T)
            PARTS = ((0, 2 * GRP), (2 * GRP, T))
            EW = NE * P
            act_o, wtd = ([cute(EW) for _ in range(GRP)] for _ in range(2))
            off4[0] = 0
            ews = cute(EW)
            cws, cwT = cute(P), cute(P)
            mix4 = [cute(GW) for _ in range(2)]
            mixT = cute(GW)
            tT4 = [cute(GW) for _ in range(2)]
            x14 = [cute(GW) for _ in range(2)]
            ot4 = [cute(GW) for _ in range(2)]
            brow = arena[:, off4[0] - EW:off4[0]]
            assert off4[0] <= lgoff
            HE = NE // 2
            ewh, ewl = (c4.enter_context(nc.sbuf_tensor(n, [P, EW], F32R)) for n in ("ewh", "ewl"))
            tTh, tTl = (c4.enter_context(nc.sbuf_tensor(n, [P, 2, GW], F32R)) for n in ("tTh", "tTl"))
            BF = mybir.dt.bfloat16
            R1, R2 = 64, 96
            bpart = c4.enter_context(nc.sbuf_tensor("bpart", [P, EW], BF))
            pick = c4.enter_context(nc.sbuf_tensor("pick", [P, P], BF))
            bE = c4.enter_context(nc.Block())

            @bE.sync
            def _(sp):
                sp.dma_start(ews.rearrange("p (e h) -> p e h", e=NE), expert_w.rearrange("e d h -> d e h")).then_inc(sem("e_w"), 16)
                sp.dma_start(cws, combine_w).then_inc(sem("e_w"), 16)
                sp.dma_start(brow[0:R2 + 1, :], expert_b.rearrange("(a e) d -> a (e d)", a=1).broadcast_to([R2 + 1, EW])
                             ).then_inc(sem("e_w"), 16)

                def body(g, k):
                    if within(g):
                        wait(sp, sem("tT_split"), g - 1)
                        sp.dma_start(t4(tT4[k]), gsl(tT_d, g)).then_inc(sem(f"e_tT{k}"), 16)
                    wait(sp, sem("e_ot"), g - 1)
                    if within(g):
                        sp.dma_start(t4(x14[k]), gsl(x1_d, g)).then_inc(sem(f"e_x1{k}"), 16)
                    if within(g - 2):
                        sp.dma_start(out_t[bass.ds((g - 2) * GW, GW), :].rearrange("(t p) d -> p t d", p=P), t4(ot4[k])
                                     ).then_inc(sem(f"o_out{k}"), 16)
                groups(sp, body, 2, NG)
                for n in ("o_out0", "o_out1"):
                    sp.wait_ge(sem(n), 8 * NG)

            @bE.gpsimd
            def _(pool):
                g_ = nc.gpsimd
                g_.memset(pick[:], 0.0).then_inc(sem("e_one"), 1)
                pool.wait_ge(sem("e_one"), 1)
                for i, r in enumerate((0, R1, R2)):
                    g_.memset(pick[r:r + 1, :], 1.0).then_inc(sem("e_one"), 1)
                    pool.wait_ge(sem("e_one"), i + 2)
                for e in range(NE):
                    ins = g_.memset(c8(io)[:, :, e:e + 1], float(NE - e))
                ins.then_inc(sem("e_io"), 1)

                def body(g, k):
                    if isinstance(g, int) and g * GRP in (PARTS[0][0], PARTS[1][0]):
                        pool.wait_ge(sem("e_wt"), 1 if g == 0 else 2)
                    for j in range(GRP):
                        t = g * GRP + j
                        pool.wait_ge(sem("e_act"), t * 2 + 2)
                        wait(pool, sem("e_mix"), t - GRP + 1)
                        g_.tensor_tensor(wtd[j].rearrange("p (e d) -> p e d", e=NE),
                                         act_o[j].rearrange("p (e d) -> p e d", e=NE),
                                         c8(wt)[:, bass.ds(t, 1), :].rearrange("p a (e o) -> p (a e) o", o=1)
                                         .broadcast_to([P, NE, P]), ALU.mult).then_inc(sem("e_wtd"), 1)
                groups(pool, body, 0, NG)

            @bE.vector
            def _(dve):
                v = nc.vector
                cnt = [0]

                def link(ins):
                    cnt[0] += 1
                    ins.then_inc(sem("e_v"), 1)
                    dve.wait_ge(sem("e_v"), cnt[0])
                link(v.tensor_reduce(red, c8(lgf), AX.X, ALU.max))
                v.tensor_tensor(c8(pr), c8(lgf), red.rearrange("p (t a) -> p t a", a=1).broadcast_to([P, T, NE]),
                                ALU.subtract).then_inc(sem("e_sh"), 1)
                def split(g, k):
                    dve.wait_ge(sem(f"e_tT{k}"), 8 * (g - k) + 16)
                    wait(dve, sem("e_hp"), 2 * GRP * (g - 1))
                    v.tensor_copy(tTh[:, k, :], tT4[k]).then_inc(sem("tT_high"), 1)
                    dve.wait_ge(sem("tT_high"), g + 1)
                    v.tensor_tensor(tTl[:, k, :], tT4[k], tTh[:, k, :].bitcast(F32), ALU.subtract).then_inc(sem("tT_split"), 1)

                for f in range(2):
                    dve.wait_ge(sem("e_wT"), f + 1)
                    v.tensor_tensor(hh(ewl, f), bank[f][:, :], hh(ewh, f).bitcast(F32), ALU.subtract).then_inc(sem("e_wlow"), 1)
                split(0, 0)
                dve.wait_ge(sem("e_w"), 48)
                for r in (0, R1, R2):
                    if r:
                        link(v.tensor_tensor(brow[r:R2 + 1, :], brow[r:R2 + 1, :], bpart[r:R2 + 1, :], ALU.subtract))
                    with nc.allow_low_precision("exact parts"):
                        link(v.tensor_copy(bpart[r:R2 + 1, :], brow[r:R2 + 1, :]))
                v.memset(red, 0.0).then_inc(sem("e_bias"), 1)
                dve.wait_ge(sem("e_bias"), 1)
                dve.wait_ge(sem("e_ex"), 1)
                def route(i):
                    t3 = lambda a: c8(a)[:, PARTS[i][0]:PARTS[i][1], :]
                    r = red[:, PARTS[i][0]:PARTS[i][1]]
                    rb = r.rearrange("p (t a) -> p t a", a=1).broadcast_to([P, PARTS[i][1] - PARTS[i][0], NE])
                    link(v.tensor_reduce(r, t3(pr), AX.X, ALU.add))
                    link(v.reciprocal(r, r))
                    link(v.tensor_tensor(t3(pr), t3(pr), rb, ALU.mult))
                    dve.wait_ge(sem("e_io"), 1)
                    link(v.tensor_copy(t3(wt), t3(pr)))
                    for oh in (oh1, oh2):
                        link(v.tensor_reduce(r, t3(wt), AX.X, ALU.max))
                        link(v.tensor_tensor(t3(sc), t3(wt), rb, ALU.is_equal))
                        link(v.tensor_tensor(t3(sc), t3(sc), t3(io), ALU.mult))
                        link(v.tensor_reduce(r, t3(sc), AX.X, ALU.max))
                        link(v.tensor_tensor(t3(oh), t3(sc), rb, ALU.is_equal))
                        link(v.scalar_tensor_tensor(t3(wt), t3(oh), -2.0, t3(wt), ALU.mult, ALU.add))
                    link(v.tensor_tensor(t3(oh1), t3(oh1), t3(oh2), ALU.add))
                    v.tensor_tensor(t3(wt), t3(oh1), t3(pr), ALU.mult).then_inc(sem("e_wt"), 1)
                route(0)

                def body(g, k):
                    if within(g):
                        for j in range(GRP):
                            t = g * GRP + j
                            if j == 1 and (not isinstance(g, int) or g + 1 < NG):
                                split(g + 1, 1 - k)
                            dve.wait_ge(sem("e_wtd"), t + 1)
                            if j == 0:
                                wait(dve, sem("e_mTp"), g - 1)
                            v.tensor_reduce(mix4[k][:, j * P:j * P + P], wtd[j].rearrange("p (e d) -> p d e", e=NE),
                                            AX.X, ALU.add).then_inc(sem("e_mix"), 1)
                            if j == 2 and within(g - 1):
                                c, kc = g - 1, 1 - k
                                dve.wait_ge(sem("e_op"), c + 1)
                                dve.wait_ge(sem(f"e_x1{kc}"), 8 * (c - kc) + 16)
                                wait(dve, sem(f"o_out{kc}"), 8 * (c - kc))
                                v.tensor_tensor(ot4[kc], bank[6][:, :], x14[kc], ALU.add).then_inc(sem("e_ot"), 1)
                    elif within(g - 1):
                        c, kc = g - 1, 1 - k
                        dve.wait_ge(sem("e_op"), c + 1)
                        dve.wait_ge(sem(f"e_x1{kc}"), 8 * (c - kc) + 16)
                        wait(dve, sem(f"o_out{kc}"), 8 * (c - kc))
                        v.tensor_tensor(ot4[kc], bank[6][:, :], x14[kc], ALU.add).then_inc(sem("e_ot"), 1)
                    if isinstance(g, int) and g == 0:
                        route(1)
                groups(dve, body, 1, NG)

            @bE.scalar
            def _(act):
                a_ = nc.scalar
                act.wait_ge(sem("e_sh"), 1)
                a_.activation(pr, pr, ACT.Exp).then_inc(sem("e_ex"), 1)
                for f in range(2):
                    act.wait_ge(sem("e_wp"), f + 1)
                    a_.copy(hh(ewh, f), bank[f][:, :]).then_inc(sem("e_wT"), 1)
                act.wait_ge(sem("e_wp"), 3)
                a_.copy(cwT, bank[2][:, 0:P]).then_inc(sem("e_wT"), 1)

                def body(g, k):
                    if within(g):
                        for j in range(GRP):
                            t = g * GRP + j
                            wait(act, sem("e_wtd"), t - GRP + 1)
                            for f in range(2):
                                act.wait_ge(sem("e_hp"), 2 * t + f + 1)
                                a_.activation(hh(act_o[j], f), bank[2 * (j % 2) + f][:, :], ACT.Silu).then_inc(sem("e_act"), 1)
                            if j == 2 and within(g - 1):
                                act.wait_ge(sem("e_mTp"), g)
                                wait(act, sem("e_op"), g - 1)
                                a_.copy(mixT, bank[5][:, :]).then_inc(sem("e_mT"), 1)
                    elif within(g - 1):
                        act.wait_ge(sem("e_mTp"), g)
                        wait(act, sem("e_op"), g - 1)
                        a_.copy(mixT, bank[5][:, :]).then_inc(sem("e_mT"), 1)
                groups(act, body, 1, NG)

            @bE.tensor
            def _(pe):
                mm = nc.tensor.matmul
                pe.wait_ge(sem("e_w"), 48)
                for f in range(2):
                    for j in range(HE):
                        e = f * HE + j
                        ins = nc.tensor.transpose(bank[f][:, j * P:j * P + P], ews[:, e * P:e * P + P], ident[:])
                    ins.then_inc(sem("e_wp"), 1)
                nc.tensor.transpose(bank[2][:, 0:P], cws, ident[:]).then_inc(sem("e_wp"), 1)
                pe.wait_ge(sem("e_wT"), 3)
                pe.wait_ge(sem("e_wlow"), 2)
                pe.wait_ge(sem("e_bias"), 1)
                pe.wait_ge(sem("e_one"), 4)

                def mixed(c, kc):
                    pe.wait_ge(sem("e_mix"), GRP * c + GRP)
                    wait(pe, sem("e_mT"), c)
                    for j in range(GRP):
                        ins = nc.tensor.transpose(bank[5][:, j * P:j * P + P], mix4[kc][:, j * P:j * P + P], ident[:])
                    ins.then_inc(sem("e_mTp"), 1)

                def combine(c):
                    pe.wait_ge(sem("e_mT"), c + 1)
                    wait(pe, sem("e_ot"), c)
                    for j in range(GRP):
                        ins = mm(bank[6][:, j * P:j * P + P], mixT[:, j * P:j * P + P], cwT, start=(j == 0), stop=(j == GRP - 1),
                                 skip_group_check=True)
                    ins.then_inc(sem("e_op"), 1)

                def body(g, k):
                    if within(g):
                        pe.wait_ge(sem("tT_split"), g + 1)
                        for j in range(GRP):
                            t = g * GRP + j
                            for f in range(2):
                                wait(pe, sem("e_act"), 2 * (t - 2) + f + 1)
                                o = bank[2 * (j % 2) + f][:, :]
                                cols = slice(j * P, j * P + P)
                                mm(o, tTh[:, k, cols], hh(ewh, f), start=True, stop=False)
                                mm(o, tTh[:, k, cols], hh(ewl, f), start=False, stop=False)
                                mm(o, tTl[:, k, cols], hh(ewh, f), start=False, stop=False)
                                mm(o, pick[0:R2 + 1, :], hh(bpart, f)[0:R2 + 1, :], start=False, stop=True).then_inc(sem("e_hp"), 1)
                            if j == 2 and within(g - 1):
                                mixed(g - 1, 1 - k)
                            if j == 3 and within(g - 1):
                                combine(g - 1)
                    elif within(g - 1):
                        mixed(g - 1, 1 - k)
                        combine(g - 1)
                groups(pe, body, 1, NG)

        end_program()


_INS = ["L0_attn_x", "L0_attn_Wq", "L0_attn_Wk", "L0_attn_Wv", "L0_attn_Wb", "L0_attn_Wa", "L0_attn_A_log",
        "L0_attn_dt_bias", "L0_attn_Wg", "L0_attn_o_norm_w", "L0_attn_Wo", "L0_attn_W_fc", "L0_attn_W_proj",
        "L0_ffn_gate_w", "L0_ffn_expert_w", "L0_ffn_expert_b", "L0_ffn_combine_w"]


def kernel(**inputs):
    import numpy as _np
    import concourse.bacc as _bacc
    from concourse.bass_utils import run_bass_kernel_spmd as _run

    nc = _bacc.Bacc("TRN2", target_bir_lowering=False, num_devices=1)
    arrays, args = {}, []
    for name in _INS:
        a = _np.ascontiguousarray(inputs[name])
        arrays[f"in_{name}"] = a
        args.append(nc.dram_tensor(f"in_{name}", a.shape, mybir.dt.from_np(a.dtype), kind="ExternalInput").ap())
    shape = arrays["in_L0_attn_x"].shape
    args.append(nc.dram_tensor("out_0", shape, F32, kind="ExternalOutput").ap())
    tiles = shape[0] * shape[1] // P
    dram = {k: nc.dram_tensor(f"scratch_{k}", s, F32, kind="Internal").ap() for k, s in (
        ("hT", (tiles, P, P)), ("xp", (tiles, P, P)), ("x1", (tiles, P, P)),
        ("tT", (tiles, P, P)), ("al", (tiles * H, P)))}
    delta_moe(nc, *args, dram)
    r = _run(nc, [arrays], core_ids=[0])
    return r.results[0]["out_0"]
```
